# Optimizing a Trainium2 kernel written in Bass

```python
import numpy as np
import jax
import jax.numpy as jnp

def _softmax(x, axis=-1):
    return jax.nn.softmax(x, axis=axis)

def _gelu(x):
    return jax.nn.gelu(x, approximate=True)

def _silu(x):
    return jax.nn.silu(x)

def _sigmoid(x):
    return jax.nn.sigmoid(x)

def _layernorm(x, axis=-1, eps=1e-05):
    m = jnp.mean(x, axis=axis, keepdims=True)
    v = jnp.var(x, axis=axis, keepdims=True)
    return (x - m) / jnp.sqrt(v + eps)

def _scatter_add(tgt, idx, src, axis=0):
    return tgt.at[idx].add(src)

def _segment_sum(src, seg, n):
    return jax.ops.segment_sum(src, seg, n)
kernel_name = 'mk_decoder_preln_d2_seqx_r8_c20ed4'

def setup_inputs(seed: int=0):
    np.random.seed(seed)
    _w = jnp.asarray

    def _rec_inputs():
        import jax
        import jax.numpy as jnp
        _rk = jax.random.key(seed)
        x = -0.0002928 + 1 * jax.random.normal(jax.random.fold_in(_rk, 1), (8, 128, 128), jnp.float32)
        _lenS = 128 - jax.random.randint(jax.random.fold_in(_rk, 7), (8,), 0, max(1, 128 // 4) + 1, jnp.int32)
        _lenS2 = 128 - jax.random.randint(jax.random.fold_in(_rk, 8), (8,), 0, max(1, 128 // 4) + 1, jnp.int32)
        _ctx_1024P = jax.random.normal(jax.random.fold_in(_rk, 11), (8, 16, 128), jnp.float32)
        _ctx_1024c = jax.random.dirichlet(jax.random.fold_in(_rk, 511), 0.3 * jnp.ones((16,), jnp.float32), (8, 128))
        _ctx_1024t = jnp.einsum('bsk,bkd->bsd', _ctx_1024c, _ctx_1024P)
        _ctx_1024t = _ctx_1024t * jax.lax.rsqrt(jnp.mean(jnp.square(_ctx_1024t)) + 1e-12) * 0.953939
        ctx_1024 = -1.39393e-06 + 0.999914 * (_ctx_1024t + 0.3 * jax.random.normal(jax.random.fold_in(_rk, 611), (8, 128, 128), jnp.float32))
        _validS = jnp.arange(128)[None, :] < _lenS[:, None]
        _validS2 = jnp.arange(128)[None, :] < _lenS2[:, None]
        _causal = jnp.tril(jnp.ones((128, 128), dtype=bool))
        mask_Bx1xSxS2_ik1 = jnp.where(jnp.broadcast_to(_validS2[:, None, None, :], (8, 1, 128, 128)), 1, 0).astype(jnp.int32)
        return (x, ctx_1024, mask_Bx1xSxS2_ik1)
    x, ctx_1024, mask_Bx1xSxS2_ik1 = _rec_inputs()

    def _L0_attn_setup():
        import jax, jax.numpy as jnp
        import numpy as np
        B, N, D = (4, 512, 128)
        H, DH = (16, 64)
        DFF = 512
        M = 64
        EPS_KERN = 1e-06
        EPS_LN = 1e-06

        def _softmax_kernel_feats(data, proj, is_query):
            dn = 1.0 / jnp.sqrt(jnp.sqrt(jnp.float32(data.shape[-1])))
            ratio = 1.0 / jnp.sqrt(jnp.float32(proj.shape[0]))
            data_dash = jnp.einsum('bnhd,md->bnhm', data * dn, proj)
            diag = jnp.sum(jnp.square(data), axis=-1, keepdims=True) * (dn * dn) / 2.0
            if is_query:
                mx = jnp.max(data_dash, axis=-1, keepdims=True)
            else:
                mx = jnp.max(data_dash)
            return ratio * (jnp.exp(data_dash - diag - mx) + EPS_KERN)

        def _layernorm(x, g, b):
            mu = jnp.mean(x, axis=-1, keepdims=True)
            var = jnp.mean(jnp.square(x - mu), axis=-1, keepdims=True)
            return (x - mu) * jax.lax.rsqrt(var + EPS_LN) * g + b

        def _encoder_forward(x, Wq, Wk, Wv, Wo, proj, W1, b1, W2, b2, ln1_g, ln1_b, ln2_g, ln2_b):
            q = jnp.einsum('bnd,dhk->bnhk', x, Wq)
            k = jnp.einsum('bnd,dhk->bnhk', x, Wk)
            v = jnp.einsum('bnd,dhk->bnhk', x, Wv)
            qf = _softmax_kernel_feats(q, proj, True)
            kf = _softmax_kernel_feats(k, proj, False)
            kv = jnp.einsum('bnhm,bnhd->bhmd', kf, v)
            num = jnp.einsum('bnhm,bhmd->bnhd', qf, kv)
            den = jnp.einsum('bnhm,bhm->bnh', qf, jnp.sum(kf, axis=1))
            attn = num / den[..., None]
            attn_out = jnp.einsum('bnhd,hdo->bno', attn, Wo)
            out1 = _layernorm(x + attn_out, ln1_g, ln1_b)
            h = jax.nn.elu(out1 @ W1 + b1)
            ffn_out = h @ W2 + b2
            return _layernorm(out1 + ffn_out, ln2_g, ln2_b)
        key = jax.random.key(seed)
        ks = jax.random.split(key, 12)
        s = 0.02
        inp = {'x': jax.random.normal(ks[0], (B, N, D), jnp.float32), 'Wq': jax.random.normal(ks[1], (D, H, DH), jnp.float32) * s, 'Wk': jax.random.normal(ks[2], (D, H, DH), jnp.float32) * s, 'Wv': jax.random.normal(ks[3], (D, H, DH), jnp.float32) * s, 'Wo': jax.random.normal(ks[4], (H, DH, D), jnp.float32) * s, 'proj': jax.random.normal(ks[5], (M, DH), jnp.float32), 'W1': jax.random.normal(ks[6], (D, DFF), jnp.float32) * s, 'b1': jnp.zeros((DFF,), jnp.float32), 'W2': jax.random.normal(ks[7], (DFF, D), jnp.float32) * s, 'b2': jnp.zeros((D,), jnp.float32), 'ln1_g': jnp.ones((D,), jnp.float32), 'ln1_b': jnp.zeros((D,), jnp.float32), 'ln2_g': jnp.ones((D,), jnp.float32), 'ln2_b': jnp.zeros((D,), jnp.float32)}
        return inp
    _L0_attn_all = _L0_attn_setup()
    _L0_attn_in = {k: v for k, v in _L0_attn_all.items() if k in ('Wq', 'Wk', 'Wv', 'Wo', 'proj', 'W1', 'b1', 'W2', 'b2', 'ln1_g', 'ln1_b', 'ln2_g', 'ln2_b')}
    del _L0_attn_all

    def _L0_xattn_setup():
        import jax, jax.numpy as jnp
        import numpy as np
        DIM = 128
        NUM_HEADS = 16
        HEAD_DIM = DIM // NUM_HEADS
        key = jax.random.key(seed)
        ks = jax.random.split(key, 11)
        B, N, C = (2, 256, DIM)
        s = 1.0 / np.sqrt(C)
        inp = {'q': jax.random.normal(ks[0], (B, N, C), jnp.float32), 'k': jax.random.normal(ks[1], (B, N, C), jnp.float32), 'v': jax.random.normal(ks[2], (B, N, C), jnp.float32), 'Wq': jax.random.normal(ks[3], (C, C), jnp.float32) * s, 'bq': jnp.zeros((C,), jnp.float32), 'Wk': jax.random.normal(ks[4], (C, C), jnp.float32) * s, 'bk': jnp.zeros((C,), jnp.float32), 'Wv': jax.random.normal(ks[5], (C, C), jnp.float32) * s, 'bv': jnp.zeros((C,), jnp.float32), 'Wo': jax.random.normal(ks[6], (C, C), jnp.float32) * s, 'bo': jnp.zeros((C,), jnp.float32)}
        return inp
    _L0_xattn_all = _L0_xattn_setup()
    _L0_xattn_in = {k: v for k, v in _L0_xattn_all.items() if k in ('Wq', 'bq', 'Wk', 'bk', 'Wv', 'bv', 'Wo', 'bo')}
    del _L0_xattn_all

    def _L0_ffn_setup():
        import jax, jax.numpy as jnp
        import numpy as np
        TOP_K = 2
        key = jax.random.key(seed)
        k1, k2, k3, k4, k5 = jax.random.split(key, 5)
        B, S, D, F, E = (2, 128, 128, 256, 8)
        return {'x': jax.random.normal(k1, (B, S, D), dtype=jnp.float32), 'router_kernel_DE': jax.random.normal(k2, (D, E), dtype=jnp.float32) * 0.02, 'kernel_gating_EDF': jax.random.normal(k3, (E, D, F), dtype=jnp.float32) * 0.02, 'kernel_up_EDF': jax.random.normal(k4, (E, D, F), dtype=jnp.float32) * 0.02, 'kernel_down_EFD': jax.random.normal(k5, (E, F, D), dtype=jnp.float32) * 0.02}
    _L0_ffn_all = _L0_ffn_setup()
    _L0_ffn_in = {k: v for k, v in _L0_ffn_all.items() if k in ('router_kernel_DE', 'kernel_gating_EDF', 'kernel_up_EDF', 'kernel_down_EFD')}
    del _L0_ffn_all

    def _L1_attn_setup():
        import jax, jax.numpy as jnp
        import numpy as np
        L, E, H = (4, 128, 16)
        HD = E // H
        EPS_LN = 1e-05

        def _layernorm(x, w, b):
            m = jnp.mean(x, axis=-1, keepdims=True)
            v = jnp.mean((x - m) ** 2, axis=-1, keepdims=True)
            return (x - m) / jnp.sqrt(v + EPS_LN) * w + b

        def _to_quaternion(x):
            p1 = jnp.diff(x, axis=1, prepend=x[:, :1])
            p2 = jnp.roll(x, 1, axis=2)
            p3 = jnp.cos(x)
            return jnp.stack([x, p1, p2, p3], axis=-1)

        def _hamilton(a, b):
            a0, a1, a2, a3 = (a[..., 0], a[..., 1], a[..., 2], a[..., 3])
            b0, b1, b2, b3 = (b[..., 0], b[..., 1], b[..., 2], b[..., 3])
            return jnp.stack([a0 * b0 - a1 * b1 - a2 * b2 - a3 * b3, a0 * b1 + a1 * b0 + a2 * b3 - a3 * b2, a0 * b2 - a1 * b3 + a2 * b0 + a3 * b1, a0 * b3 + a1 * b2 - a2 * b1 + a3 * b0], axis=-1)

        def _spectral_filter(S):
            ks = jnp.fft.fftfreq(S).astype(jnp.float32)[:, None, None]
            kh = jnp.fft.fftfreq(H).astype(jnp.float32)[None, :, None]
            kd = jnp.fft.fftfreq(HD).astype(jnp.float32)[None, None, :]
            km = jnp.sqrt(ks ** 2 + kh ** 2 + kd ** 2 + 1e-10)
            f = jnp.exp(1j * jnp.arctan(jnp.log(km + 1e-10)))
            return f[None, :, :, :, None].astype(jnp.complex64)

        def _modulation(S):
            lam = jnp.arange(S, dtype=jnp.float32) / S
            t = jnp.arange(S, dtype=jnp.float32) * 0.1
            probe = jnp.sin(t + lam)
            phase = t - 2.0 * lam + 0.5 * lam ** 2
            return (probe * jnp.cos(phase))[None, :, None, None]

        def _attention(x, aw, ab, pw, pb):
            B, S, _ = x.shape
            qkv = (x @ aw + ab).reshape(B, S, H, 3 * HD)
            q, k, v = jnp.split(qkv, 3, axis=-1)
            qk = _hamilton(_to_quaternion(q), _to_quaternion(k))
            qkv_p = _hamilton(qk, _to_quaternion(v))
            f = jnp.fft.fftn(qkv_p.astype(jnp.complex64), axes=(-3, -2))
            out = jnp.fft.ifftn(f * _spectral_filter(S), axes=(-3, -2)).real
            a = out[..., 0] * (1.0 + 0.1 * _modulation(S))
            return a.reshape(B, S, E) @ pw + pb

        def _layer(x, p):
            ln1w, ln1b, aw, ab, pw, pb, ln2w, ln2b, fw, fb, mw, mb = p
            x = x + _attention(_layernorm(x, ln1w, ln1b), aw, ab, pw, pb)
            h = _layernorm(x, ln2w, ln2b)
            h = jax.nn.gelu(h @ fw + fb, approximate=False) @ mw + mb
            return x + h
        key = jax.random.key(seed)
        ks = jax.random.split(key, 6)
        s = 0.02
        return {'x': jax.random.normal(ks[0], (2, 256, E), jnp.float32), 'ln1_w': jnp.ones((L, E), jnp.float32), 'ln1_b': jnp.zeros((L, E), jnp.float32), 'attn_w': jax.random.normal(ks[1], (L, E, 3 * E), jnp.float32) * s, 'attn_b': jnp.zeros((L, 3 * E), jnp.float32), 'aproj_w': jax.random.normal(ks[2], (L, E, E), jnp.float32) * s, 'aproj_b': jnp.zeros((L, E), jnp.float32), 'ln2_w': jnp.ones((L, E), jnp.float32), 'ln2_b': jnp.zeros((L, E), jnp.float32), 'fc_w': jax.random.normal(ks[3], (L, E, 4 * E), jnp.float32) * s, 'fc_b': jnp.zeros((L, 4 * E), jnp.float32), 'mproj_w': jax.random.normal(ks[4], (L, 4 * E, E), jnp.float32) * s, 'mproj_b': jnp.zeros((L, E), jnp.float32)}
    _L1_attn_all = _L1_attn_setup()
    _L1_attn_in = {k: v for k, v in _L1_attn_all.items() if k in ('ln1_w', 'ln1_b', 'attn_w', 'attn_b', 'aproj_w', 'aproj_b', 'ln2_w', 'ln2_b', 'fc_w', 'fc_b', 'mproj_w', 'mproj_b')}
    del _L1_attn_all

    def _L1_xattn_setup():
        import jax, jax.numpy as jnp
        import numpy as np
        DIM = 128
        HEADS = 4
        PER_HEAD = DIM // HEADS

        def _split_head(x):
            B, T, _ = x.shape
            return x.reshape(B, T, HEADS, PER_HEAD).transpose(0, 2, 1, 3)
        key = jax.random.key(seed)
        ks = jax.random.split(key, 12)
        B, T = (4, 256)
        s = 1.0 / np.sqrt(DIM)
        return {'query': jax.random.normal(ks[0], (B, T, DIM), jnp.float32), 'keys': jax.random.normal(ks[1], (B, T, DIM), jnp.float32), 'values': jax.random.normal(ks[2], (B, T, DIM), jnp.float32), 'mask': jax.random.randint(ks[3], (B, 1, T, T), 0, 2, jnp.int32), 'Wq': jax.random.normal(ks[4], (DIM, DIM), jnp.float32) * s, 'bq': jnp.zeros((DIM,), jnp.float32), 'Wk': jax.random.normal(ks[5], (DIM, DIM), jnp.float32) * s, 'bk': jnp.zeros((DIM,), jnp.float32), 'Wv': jax.random.normal(ks[6], (DIM, DIM), jnp.float32) * s, 'bv': jnp.zeros((DIM,), jnp.float32), 'Wo': jax.random.normal(ks[7], (DIM, DIM), jnp.float32) * s, 'bo': jnp.zeros((DIM,), jnp.float32)}
    _L1_xattn_all = _L1_xattn_setup()
    _L1_xattn_in = {k: v for k, v in _L1_xattn_all.items() if k in ('Wq', 'bq', 'Wk', 'bk', 'Wv', 'bv', 'Wo', 'bo')}
    del _L1_xattn_all

    def _L1_ffn_setup():
        import jax, jax.numpy as jnp
        import numpy as np
        EXPERT_NUM = 8
        CAPACITY = 100
        key = jax.random.key(seed)
        k1, k2, k3 = jax.random.split(key, 3)
        B, S, H, E = (8, 256, 128, EXPERT_NUM)
        x = jax.random.normal(k1, (B, S, H), dtype=jnp.float32)
        w_gate = jax.random.normal(k2, (H, E), dtype=jnp.float32) * 0.02
        w_expert = jax.random.normal(k3, (H, H), dtype=jnp.float32) * 0.02
        b_expert = jnp.zeros((H,), dtype=jnp.float32)
        return {'x': x, 'w_gate': w_gate, 'w_expert': w_expert, 'b_expert': b_expert}
    _L1_ffn_all = _L1_ffn_setup()
    _L1_ffn_in = {k: v for k, v in _L1_ffn_all.items() if k in ('w_gate', 'w_expert', 'b_expert')}
    del _L1_ffn_all
    return {'x': x, 'ctx_1024': ctx_1024, 'mask_Bx1xSxS2_ik1': mask_Bx1xSxS2_ik1, 'L0_attn_Wq': _L0_attn_in['Wq'], 'L0_attn_Wk': _L0_attn_in['Wk'], 'L0_attn_Wv': _L0_attn_in['Wv'], 'L0_attn_Wo': _L0_attn_in['Wo'], 'L0_attn_proj': _L0_attn_in['proj'], 'L0_attn_W1': _L0_attn_in['W1'], 'L0_attn_b1': _L0_attn_in['b1'], 'L0_attn_W2': _L0_attn_in['W2'], 'L0_attn_b2': _L0_attn_in['b2'], 'L0_attn_ln1_g': _L0_attn_in['ln1_g'], 'L0_attn_ln1_b': _L0_attn_in['ln1_b'], 'L0_attn_ln2_g': _L0_attn_in['ln2_g'], 'L0_attn_ln2_b': _L0_attn_in['ln2_b'], 'L0_xattn_Wq': _L0_xattn_in['Wq'], 'L0_xattn_bq': _L0_xattn_in['bq'], 'L0_xattn_Wk': _L0_xattn_in['Wk'], 'L0_xattn_bk': _L0_xattn_in['bk'], 'L0_xattn_Wv': _L0_xattn_in['Wv'], 'L0_xattn_bv': _L0_xattn_in['bv'], 'L0_xattn_Wo': _L0_xattn_in['Wo'], 'L0_xattn_bo': _L0_xattn_in['bo'], 'L0_ffn_router_kernel_DE': _L0_ffn_in['router_kernel_DE'], 'L0_ffn_kernel_gating_EDF': _L0_ffn_in['kernel_gating_EDF'], 'L0_ffn_kernel_up_EDF': _L0_ffn_in['kernel_up_EDF'], 'L0_ffn_kernel_down_EFD': _L0_ffn_in['kernel_down_EFD'], 'L1_attn_ln1_w': _L1_attn_in['ln1_w'], 'L1_attn_ln1_b': _L1_attn_in['ln1_b'], 'L1_attn_attn_w': _L1_attn_in['attn_w'], 'L1_attn_attn_b': _L1_attn_in['attn_b'], 'L1_attn_aproj_w': _L1_attn_in['aproj_w'], 'L1_attn_aproj_b': _L1_attn_in['aproj_b'], 'L1_attn_ln2_w': _L1_attn_in['ln2_w'], 'L1_attn_ln2_b': _L1_attn_in['ln2_b'], 'L1_attn_fc_w': _L1_attn_in['fc_w'], 'L1_attn_fc_b': _L1_attn_in['fc_b'], 'L1_attn_mproj_w': _L1_attn_in['mproj_w'], 'L1_attn_mproj_b': _L1_attn_in['mproj_b'], 'L1_xattn_Wq': _L1_xattn_in['Wq'], 'L1_xattn_bq': _L1_xattn_in['bq'], 'L1_xattn_Wk': _L1_xattn_in['Wk'], 'L1_xattn_bk': _L1_xattn_in['bk'], 'L1_xattn_Wv': _L1_xattn_in['Wv'], 'L1_xattn_bv': _L1_xattn_in['bv'], 'L1_xattn_Wo': _L1_xattn_in['Wo'], 'L1_xattn_bo': _L1_xattn_in['bo'], 'L1_ffn_w_gate': _L1_ffn_in['w_gate'], 'L1_ffn_w_expert': _L1_ffn_in['w_expert'], 'L1_ffn_b_expert': _L1_ffn_in['b_expert']}

def reference(x, ctx_1024, mask_Bx1xSxS2_ik1, L0_attn_Wq, L0_attn_Wk, L0_attn_Wv, L0_attn_Wo, L0_attn_proj, L0_attn_W1, L0_attn_b1, L0_attn_W2, L0_attn_b2, L0_attn_ln1_g, L0_attn_ln1_b, L0_attn_ln2_g, L0_attn_ln2_b, L0_xattn_Wq, L0_xattn_bq, L0_xattn_Wk, L0_xattn_bk, L0_xattn_Wv, L0_xattn_bv, L0_xattn_Wo, L0_xattn_bo, L0_ffn_router_kernel_DE, L0_ffn_kernel_gating_EDF, L0_ffn_kernel_up_EDF, L0_ffn_kernel_down_EFD, L1_attn_ln1_w, L1_attn_ln1_b, L1_attn_attn_w, L1_attn_attn_b, L1_attn_aproj_w, L1_attn_aproj_b, L1_attn_ln2_w, L1_attn_ln2_b, L1_attn_fc_w, L1_attn_fc_b, L1_attn_mproj_w, L1_attn_mproj_b, L1_xattn_Wq, L1_xattn_bq, L1_xattn_Wk, L1_xattn_bk, L1_xattn_Wv, L1_xattn_bv, L1_xattn_Wo, L1_xattn_bo, L1_ffn_w_gate, L1_ffn_w_expert, L1_ffn_b_expert):
    import jax
    import jax.numpy as jnp

    def _L0_attn_ref(x, Wq, Wk, Wv, Wo, proj, W1, b1, W2, b2, ln1_g, ln1_b, ln2_g, ln2_b):
        import jax, jax.numpy as jnp
        import numpy as np
        B, N, D = (4, 512, 128)
        H, DH = (16, 64)
        DFF = 512
        M = 64
        EPS_KERN = 1e-06
        EPS_LN = 1e-06

        def _softmax_kernel_feats(data, proj, is_query):
            dn = 1.0 / jnp.sqrt(jnp.sqrt(jnp.float32(data.shape[-1])))
            ratio = 1.0 / jnp.sqrt(jnp.float32(proj.shape[0]))
            data_dash = jnp.einsum('bnhd,md->bnhm', data * dn, proj)
            diag = jnp.sum(jnp.square(data), axis=-1, keepdims=True) * (dn * dn) / 2.0
            if is_query:
                mx = jnp.max(data_dash, axis=-1, keepdims=True)
            else:
                mx = jnp.max(data_dash)
            return ratio * (jnp.exp(data_dash - diag - mx) + EPS_KERN)

        def _layernorm(x, g, b):
            mu = jnp.mean(x, axis=-1, keepdims=True)
            var = jnp.mean(jnp.square(x - mu), axis=-1, keepdims=True)
            return (x - mu) * jax.lax.rsqrt(var + EPS_LN) * g + b

        def _encoder_forward(x, Wq, Wk, Wv, Wo, proj, W1, b1, W2, b2, ln1_g, ln1_b, ln2_g, ln2_b):
            q = jnp.einsum('bnd,dhk->bnhk', x, Wq)
            k = jnp.einsum('bnd,dhk->bnhk', x, Wk)
            v = jnp.einsum('bnd,dhk->bnhk', x, Wv)
            qf = _softmax_kernel_feats(q, proj, True)
            kf = _softmax_kernel_feats(k, proj, False)
            kv = jnp.einsum('bnhm,bnhd->bhmd', kf, v)
            num = jnp.einsum('bnhm,bhmd->bnhd', qf, kv)
            den = jnp.einsum('bnhm,bhm->bnh', qf, jnp.sum(kf, axis=1))
            attn = num / den[..., None]
            attn_out = jnp.einsum('bnhd,hdo->bno', attn, Wo)
            out1 = _layernorm(x + attn_out, ln1_g, ln1_b)
            h = jax.nn.elu(out1 @ W1 + b1)
            ffn_out = h @ W2 + b2
            return _layernorm(out1 + ffn_out, ln2_g, ln2_b)
        return _encoder_forward(x, Wq, Wk, Wv, Wo, proj, W1, b1, W2, b2, ln1_g, ln1_b, ln2_g, ln2_b)

    def _L0_xattn_ref(q, k, v, Wq, bq, Wk, bk, Wv, bv, Wo, bo):
        import jax, jax.numpy as jnp
        import numpy as np
        DIM = 128
        NUM_HEADS = 16
        HEAD_DIM = DIM // NUM_HEADS
        B, Nq, C = q.shape
        Nkv = k.shape[1]
        H, D = (NUM_HEADS, HEAD_DIM)
        qh = (q @ Wq.T + bq).reshape(B, Nq, H, D).transpose(0, 2, 1, 3)
        kh = (k @ Wk.T + bk).reshape(B, Nkv, H, D).transpose(0, 2, 1, 3)
        vh = (v @ Wv.T + bv).reshape(B, Nkv, H, D).transpose(0, 2, 1, 3)
        scale = D ** (-0.5)
        attn = jax.nn.softmax(jnp.einsum('bhqd,bhkd->bhqk', qh, kh) * scale, axis=-1)
        out = jnp.einsum('bhqk,bhkd->bhqd', attn, vh)
        out = out.transpose(0, 2, 1, 3).reshape(B, Nq, C)
        return out @ Wo.T + bo

    def _L0_ffn_ref(x, router_kernel_DE, kernel_gating_EDF, kernel_up_EDF, kernel_down_EFD):
        import jax, jax.numpy as jnp
        import numpy as np
        TOP_K = 2
        E = router_kernel_DE.shape[-1]
        x = x.astype(jnp.float32)
        logits_BSE = jnp.einsum('BSD,DE->BSE', x, router_kernel_DE)
        probs_BSE = jax.nn.softmax(logits_BSE.astype(jnp.float32), axis=-1)
        weights_BSK, indices_BSK = jax.lax.top_k(probs_BSE, TOP_K)
        norm_weights_BSK = jax.nn.softmax(weights_BSK, axis=-1)
        one_hot_BSKE = jax.nn.one_hot(indices_BSK, num_classes=E, dtype=x.dtype)
        full_weights_BSE = jnp.sum(one_hot_BSKE * norm_weights_BSK[..., None], axis=2)
        gating_BSEF = jnp.einsum('BSD,EDF->BSEF', x, kernel_gating_EDF)
        act_BSEF = jax.nn.silu(gating_BSEF)
        up_BSEF = jnp.einsum('BSD,EDF->BSEF', x, kernel_up_EDF)
        fuse_BSEF = act_BSEF * up_BSEF
        down_BSED = jnp.einsum('BSEF,EFD->BSED', fuse_BSEF, kernel_down_EFD)
        out_BSD = jnp.einsum('BSED,BSE->BSD', down_BSED, full_weights_BSE)
        return out_BSD.astype(jnp.float32)

    def _L1_attn_ref(x, ln1_w, ln1_b, attn_w, attn_b, aproj_w, aproj_b, ln2_w, ln2_b, fc_w, fc_b, mproj_w, mproj_b):
        import jax, jax.numpy as jnp
        import numpy as np
        L, E, H = (4, 128, 16)
        HD = E // H
        EPS_LN = 1e-05

        def _layernorm(x, w, b):
            m = jnp.mean(x, axis=-1, keepdims=True)
            v = jnp.mean((x - m) ** 2, axis=-1, keepdims=True)
            return (x - m) / jnp.sqrt(v + EPS_LN) * w + b

        def _to_quaternion(x):
            p1 = jnp.diff(x, axis=1, prepend=x[:, :1])
            p2 = jnp.roll(x, 1, axis=2)
            p3 = jnp.cos(x)
            return jnp.stack([x, p1, p2, p3], axis=-1)

        def _hamilton(a, b):
            a0, a1, a2, a3 = (a[..., 0], a[..., 1], a[..., 2], a[..., 3])
            b0, b1, b2, b3 = (b[..., 0], b[..., 1], b[..., 2], b[..., 3])
            return jnp.stack([a0 * b0 - a1 * b1 - a2 * b2 - a3 * b3, a0 * b1 + a1 * b0 + a2 * b3 - a3 * b2, a0 * b2 - a1 * b3 + a2 * b0 + a3 * b1, a0 * b3 + a1 * b2 - a2 * b1 + a3 * b0], axis=-1)

        def _spectral_filter(S):
            ks = jnp.fft.fftfreq(S).astype(jnp.float32)[:, None, None]
            kh = jnp.fft.fftfreq(H).astype(jnp.float32)[None, :, None]
            kd = jnp.fft.fftfreq(HD).astype(jnp.float32)[None, None, :]
            km = jnp.sqrt(ks ** 2 + kh ** 2 + kd ** 2 + 1e-10)
            f = jnp.exp(1j * jnp.arctan(jnp.log(km + 1e-10)))
            return f[None, :, :, :, None].astype(jnp.complex64)

        def _modulation(S):
            lam = jnp.arange(S, dtype=jnp.float32) / S
            t = jnp.arange(S, dtype=jnp.float32) * 0.1
            probe = jnp.sin(t + lam)
            phase = t - 2.0 * lam + 0.5 * lam ** 2
            return (probe * jnp.cos(phase))[None, :, None, None]

        def _attention(x, aw, ab, pw, pb):
            B, S, _ = x.shape
            qkv = (x @ aw + ab).reshape(B, S, H, 3 * HD)
            q, k, v = jnp.split(qkv, 3, axis=-1)
            qk = _hamilton(_to_quaternion(q), _to_quaternion(k))
            qkv_p = _hamilton(qk, _to_quaternion(v))
            f = jnp.fft.fftn(qkv_p.astype(jnp.complex64), axes=(-3, -2))
            out = jnp.fft.ifftn(f * _spectral_filter(S), axes=(-3, -2)).real
            a = out[..., 0] * (1.0 + 0.1 * _modulation(S))
            return a.reshape(B, S, E) @ pw + pb

        def _layer(x, p):
            ln1w, ln1b, aw, ab, pw, pb, ln2w, ln2b, fw, fb, mw, mb = p
            x = x + _attention(_layernorm(x, ln1w, ln1b), aw, ab, pw, pb)
            h = _layernorm(x, ln2w, ln2b)
            h = jax.nn.gelu(h @ fw + fb, approximate=False) @ mw + mb
            return x + h
        for i in range(L):
            x = _layer(x, (ln1_w[i], ln1_b[i], attn_w[i], attn_b[i], aproj_w[i], aproj_b[i], ln2_w[i], ln2_b[i], fc_w[i], fc_b[i], mproj_w[i], mproj_b[i]))
        return x

    def _L1_xattn_ref(query, keys, values, mask, Wq, bq, Wk, bk, Wv, bv, Wo, bo):
        import jax, jax.numpy as jnp
        import numpy as np
        DIM = 128
        HEADS = 4
        PER_HEAD = DIM // HEADS

        def _split_head(x):
            B, T, _ = x.shape
            return x.reshape(B, T, HEADS, PER_HEAD).transpose(0, 2, 1, 3)
        q = _split_head(query @ Wq.T + bq)
        k = _split_head(keys @ Wk.T + bk)
        v = _split_head(values @ Wv.T + bv)
        scale = 1.0 / np.sqrt(PER_HEAD).astype(np.float32)
        weights = jnp.einsum('bhqd,bhkd->bhqk', q, k) * scale
        weights = jnp.where(mask == 0, jnp.float32(-1000000000.0), weights)
        weights = jax.nn.softmax(weights, axis=-2)
        wv = jnp.einsum('bhqk,bhkd->bhqd', weights, v)
        B = q.shape[0]
        wv = wv.transpose(0, 2, 1, 3).reshape(B, -1, DIM)
        return wv @ Wo.T + bo

    def _L1_ffn_ref(x, w_gate, w_expert, b_expert):
        import jax, jax.numpy as jnp
        import numpy as np
        EXPERT_NUM = 8
        CAPACITY = 100
        B, S, H = x.shape
        E, C = (EXPERT_NUM, CAPACITY)
        hs = x.reshape(-1, H)
        logits = hs @ w_gate
        probs = jax.nn.softmax(logits, axis=1)
        best = jnp.argmax(probs, axis=1)
        mask = jax.nn.one_hot(best, E, dtype=jnp.int32)
        gate = jnp.sum(probs * mask.astype(probs.dtype), axis=1)
        locations = jnp.cumsum(mask, axis=0) - 1
        mask = mask * (locations < C).astype(jnp.int32)
        loc_sum = jnp.sum(locations * mask, axis=1)
        new_gates = gate[:, None] * mask.astype(probs.dtype)
        loc_oh = jax.nn.one_hot(loc_sum, C, dtype=probs.dtype)
        combine = new_gates[:, :, None] * loc_oh[:, None, :]
        dispatch = (combine != 0).astype(hs.dtype)
        dispatched = jnp.einsum('tec,th->ech', dispatch, hs).reshape(E * C, H)
        expert_out = dispatched @ w_expert + b_expert
        combined = combine.reshape(-1, E * C) @ expert_out
        return combined.reshape(B, S, H)
    x = x + _L0_attn_ref(_layernorm(x, axis=-1), L0_attn_Wq, L0_attn_Wk, L0_attn_Wv, L0_attn_Wo, L0_attn_proj, L0_attn_W1, L0_attn_b1, L0_attn_W2, L0_attn_b2, L0_attn_ln1_g, L0_attn_ln1_b, L0_attn_ln2_g, L0_attn_ln2_b)
    x = x + _L0_xattn_ref(_layernorm(x, axis=-1), ctx_1024, ctx_1024, L0_xattn_Wq, L0_xattn_bq, L0_xattn_Wk, L0_xattn_bk, L0_xattn_Wv, L0_xattn_bv, L0_xattn_Wo, L0_xattn_bo)
    x = x + _L0_ffn_ref(_layernorm(x, axis=-1), L0_ffn_router_kernel_DE, L0_ffn_kernel_gating_EDF, L0_ffn_kernel_up_EDF, L0_ffn_kernel_down_EFD)
    x = x + _L1_attn_ref(_layernorm(x, axis=-1), L1_attn_ln1_w, L1_attn_ln1_b, L1_attn_attn_w, L1_attn_attn_b, L1_attn_aproj_w, L1_attn_aproj_b, L1_attn_ln2_w, L1_attn_ln2_b, L1_attn_fc_w, L1_attn_fc_b, L1_attn_mproj_w, L1_attn_mproj_b)
    x = x + _L1_xattn_ref(_layernorm(x, axis=-1), ctx_1024, ctx_1024, mask_Bx1xSxS2_ik1, L1_xattn_Wq, L1_xattn_bq, L1_xattn_Wk, L1_xattn_bk, L1_xattn_Wv, L1_xattn_bv, L1_xattn_Wo, L1_xattn_bo)
    x = x + _L1_ffn_ref(_layernorm(x, axis=-1), L1_ffn_w_gate, L1_ffn_w_expert, L1_ffn_b_expert)
    return x

_drawn_inputs = setup_inputs


def setup_inputs(seed=0):
    import zlib

    import numpy as np

    out = dict(_drawn_inputs(seed))
    spreads = {'L0_attn_b1': (0.0, 0.448),
     'L0_attn_b2': (0.0, 0.1),
     'L0_attn_ln1_g': (1.0, 0.2),
     'L0_attn_ln1_b': (0.0, 0.1),
     'L0_attn_ln2_g': (1.0, 0.2),
     'L0_attn_ln2_b': (0.0, 0.1),
     'L0_xattn_bq': (0.0, 0.718),
     'L0_xattn_bk': (0.0, 2.0),
     'L0_xattn_bv': (0.0, 0.1),
     'L0_xattn_bo': (0.0, 0.1),
     'L1_attn_ln1_w': (1.0, 0.6),
     'L1_attn_ln1_b': (0.0, 2.0),
     'L1_attn_attn_b': (0.0, 0.394),
     'L1_attn_aproj_b': (0.0, 0.1),
     'L1_attn_ln2_w': (1.0, 0.6),
     'L1_attn_ln2_b': (0.0, 2.0),
     'L1_attn_fc_b': (0.0, 0.491),
     'L1_attn_mproj_b': (0.0, 0.1),
     'L1_xattn_bq': (0.0, 2.0),
     'L1_xattn_bk': (0.0, 0.497),
     'L1_xattn_bv': (0.0, 0.268),
     'L1_xattn_bo': (0.0, 0.327),
     'L1_ffn_b_expert': (0.0, 0.8)}
    factors = {'L0_attn_Wq': 64.0,
     'L0_attn_Wk': 64.0,
     'L0_attn_Wv': 8.0,
     'L0_attn_Wo': 8.0,
     'L0_attn_proj': 64.0,
     'L0_ffn_router_kernel_DE': 8.0,
     'L0_ffn_kernel_gating_EDF': 8.0,
     'L0_ffn_kernel_up_EDF': 8.0,
     'L0_ffn_kernel_down_EFD': 8.0,
     'L1_ffn_w_gate': 8.0,
     'L1_ffn_w_expert': 5.22}
    for name, (base, spread) in spreads.items():
        noise = np.random.default_rng([zlib.crc32(name.encode()), seed]).standard_normal(out[name].shape)
        drawn = base * np.exp(spread * noise) if base else spread * noise
        out[name] = jnp.asarray(drawn.astype(out[name].dtype))
    for name, factor in factors.items():
        out[name] = (out[name] * factor).astype(out[name].dtype)
    return out
```

```python
from contextlib import ExitStack

import numpy as np

import concourse.bass as bass
from concourse import mybir

F32 = mybir.dt.float32
I32 = mybir.dt.int32
ACT = mybir.ActivationFunctionType
ALU = mybir.AluOpType
AX = mybir.AxisListType

P = 128
NB = 8
HB = NB // 2
D = 128
HALF = HB * P
EPS_OUTER = 1e-5

PH, PD, PM = 16, 64, 64
NPAIR = PH // 2
VA = PD + 1
PAIR = 2 * VA
DN = float(PD) ** -0.25
EPS_KERN = 1e-6
PF = 512
PFB = PF // P


def load(eng, dst, src, sem):
    eng.dma_start(dst, src).then_inc(sem, 16)


class Shared:
    pass



class Norm:

    def __init__(self, sem, name):
        self.stats, self.mv, self.eps, self.rstd, self.hat, self.turned, self.xT = (
            sem(f"{name}_{n}") for n in ("stats", "mv", "var_eps", "rstd", "xhat", "turned", "xT"))


def norm_vector(dve, S, N, src, dst, n0=0):
    for h in range(2):
        for i in range(HB):
            m = dve.bn_stats(S.stats[:, h, i], src[:, HB * h + i])
        m.then_inc(N.stats, 1)
        dve.wait_ge(N.stats, n0 + h + 1)
        for i in range(HB):
            m = dve.bn_aggr(S.mv[:, h, i], S.stats[:, h, i])
        m.then_inc(N.mv, 1)
    for h in range(2):
        dve.wait_ge(N.mv, n0 + h + 1)
        dve.wait_ge(N.rstd, n0 + h + 1)
        for i in range(HB):
            b = HB * h + i
            m = dve.tensor_scalar(dst[:, b], src[:, b], S.mv[:, h, i, 0:1], S.rstd[:, h, i:i + 1],
                                  ALU.subtract, ALU.mult)
        m.then_inc(N.hat, 1)


def norm_pool(pool, S, N, eps, n0=0):
    for h in range(2):
        pool.wait_ge(N.mv, n0 + h + 1)
        pool.tensor_scalar(S.rstd[:, h], S.mv[:, h, :, 1], eps, 1.0, ALU.add, ALU.mult).then_inc(N.eps, 1)
        pool.wait_ge(N.eps, n0 + h + 1)
        pool.tensor_tensor(S.rstd[:, h], S.rstd[:, h], S.nhalf[:, 0:HB], ALU.pow).then_inc(N.rstd, 1)


def norm_tensor(pe, S, N, bank):
    for h in range(2):
        pe.wait_ge(N.hat, h + 1)
        for i in range(HB):
            m = pe.transpose(S.psum[:, bank + h, i * P:(i + 1) * P], S.xhat[:, HB * h + i], S.ident[:])
        m.then_inc(N.turned, 1)


def norm_scalar(act, S, N, bank, dst):
    for h in range(2):
        act.wait_ge(N.turned, h + 1)
        act.activation(dst[:, h * HALF:(h + 1) * HALF], S.psum[:, bank + h], ACT.Copy).then_inc(N.xT, 1)


def stage_performer(nc, S, A):
    with ExitStack() as ctx:
        def sb(name, shape, dt=F32):
            return ctx.enter_context(nc.sbuf_tensor(name, shape, dt))

        sem = S.sem
        psum = S.psum
        xres, xhat, xT, ident, mv, stats = S.xres, S.xhat, S.xT, S.ident, S.mv, S.stats

        wq, wk, wv = (sb(f"p_w{n}", [P, PH * PD]) for n in "qkv")
        wo = sb("p_wo", [P, NPAIR, D])
        w1, w2 = sb("p_w1", [P, PF]), sb("p_w2", [P, PFB, D])
        b1 = sb("p_b1", [P, PFB])
        rows = sb("p_rows", [P, 5, D])
        proj2 = sb("p_proj2", [P, P])
        wdq, wdk = sb("p_wdq", [P, PH * PM]), sb("p_wdk", [P, PH * PM])
        xTp = sb("p_xTp", [P, 2, P])
        vaug = sb("p_vaug", [P, NB, PH, VA])
        ddk = sb("p_ddk", [P, NB, PH * PM])
        sq = sb("p_sq", [P, 2, PH * PD])
        diag = sb("p_diag", [P, 2, PH])
        kmax = sb("p_kmax", [P, NB])
        kmax1 = sb("p_kmax1", [P, 1])
        kmaxn = sb("p_kmaxn", [1, 1])
        nkmax = sb("p_nkmax", [P, 1])
        epsk = sb("p_epsk", [P, 1])
        ones = S.ones

        in_x, in_id, in_row = sem("in_x"), sem("in_ident"), sem("in_rows")
        in_wk, in_wdk, in_wv, in_wq, in_wo, in_ffn = (sem(n) for n in (
            "in_wk", "in_wdk", "in_wv", "in_wq", "in_wo", "in_ffn"))
        with ExitStack() as c2:
            wqT = c2.enter_context(nc.sbuf_tensor("p_wqT", [P, NPAIR, D], F32))
            wkT = c2.enter_context(nc.sbuf_tensor("p_wkT", [P, NPAIR, D], F32))
            cst, dstat, dmv, rstd, hat, tp, xTr = (sem(n) for n in (
                "a_const", "a_stats", "a_mv", "a_rstd", "a_hat", "a_tp", "a_xT"))
            wdp, wde, xtp, k_in, dk_in, v_in, sq_ok, v_ok, red_ok, dk_ok, pchain = (sem(n) for n in (
                "a_wd_psum", "a_wd", "a_xTp", "a_k_psum", "a_dk_psum", "a_v_psum", "a_sq", "a_v", "a_red",
                "a_dk_used", "a_pool"))
            m1, m2, m3, m4, m5 = (sem(n) for n in ("a_max1", "a_maxT", "a_max2", "a_maxbc", "a_max3"))
            block = c2.enter_context(nc.Block())

            @block.sync
            def _(sp):
                load(sp, xres[:], A["x"], in_x)
                load(sp, ident[:], A["ident"], in_id)
                load(sp, wkT[:], A["pwkT"], in_wdk)
                sp.wait_ge(cst, 1)
                load(sp, proj2[0:PD, 0:PM], A["projT"], in_wdk)
                load(sp, proj2[PD:P, PM:P], A["projT"], in_wdk)
                load(sp, wk[:], A["pwk"], in_wk)
                load(sp, wv[:], A["pwv"], in_wv)
                load(sp, wqT[:], A["pwqT"], in_wq)
                load(sp, wq[:], A["pwq"], in_wq)
                load(sp, wo[:], A["pwo"], in_wo)
                load(sp, w1[:], A["pw1"], in_ffn)
                load(sp, w2[:], A["pw2"], in_ffn)
                load(sp, b1[:], A["pb1"], in_ffn)
                load(sp, S.ctxT[:], A["ctxT"], S.in_x0)
                for i, n in enumerate("qkvo"):
                    load(sp, S.x0w[:, i], A["x0w" + n], S.in_x0)
                load(sp, S.headmask[:], A["headmask"], S.in_x0)
                load(sp, S.x0cols[:, 0:1], A["x0bq"], S.in_x0)
                load(sp, S.x0cols[:, 1:2], A["x0bk"], S.in_x0)
                load(sp, S.x0rows[:, 0], A["x0bv"].partition_broadcast(P), S.in_x0)
                load(sp, S.x0rows[:, 1], A["x0bo"].partition_broadcast(P), S.in_x0)
                for i, n in enumerate(("pln1g", "pln1b", "pln2g", "pln2b", "pb2")):
                    load(sp, rows[:, i, :], A[n].partition_broadcast(P), in_row)

            @block.gpsimd
            def _(pool):
                pool.memset(proj2[:], 0.0).then_inc(cst, 1)
                pool.memset(ones[:], 1.0).then_inc(pchain, 1)
                pool.memset(S.nhalf[:], -0.5).then_inc(pchain, 1)
                pool.memset(epsk[:], EPS_KERN).then_inc(pchain, 1)
                pool.memset(vaug[:, :, :, PD:VA], 1.0).then_inc(pchain, 1)
                pool.wait_ge(pchain, 4)
                for h in range(2):
                    pool.wait_ge(dmv, h + 1)
                    pool.tensor_scalar(S.rstd[:, h], mv[:, h, :, 1], EPS_OUTER, None, ALU.add).then_inc(pchain, 1)
                    pool.wait_ge(pchain, 5 + h)
                    pool.tensor_tensor(S.rstd[:, h], S.rstd[:, h], S.nhalf[:, 0:HB], ALU.pow).then_inc(rstd, 1)
                with pool.Fori(0, NB // 2) as i:
                    b = i * 2
                    for j in range(2):
                        pool.wait_ge(xTr, 2)
                        pool.wait_ge(v_in, b + j)
                        pool.tensor_copy(xTp[:, j], xT[:, bass.ds((b + j) * P, P)]).then_inc(xtp, 1)

            @block.vector
            def _(dve):
                dve.wait_ge(in_x, 16)
                for h in range(2):
                    for i in range(HB):
                        dve.bn_stats(stats[:, h, i], xres[:, HB * h + i]).then_inc(dstat, 1)
                    dve.wait_ge(dstat, HB * (h + 1))
                    for i in range(HB):
                        m = dve.bn_aggr(mv[:, h, i], stats[:, h, i])
                    m.then_inc(dmv, 1)
                for h in range(2):
                    dve.wait_ge(dmv, h + 1)
                    dve.wait_ge(rstd, h + 1)
                    for i in range(HB):
                        b = HB * h + i
                        m = dve.tensor_scalar(xhat[:, b], xres[:, b], mv[:, h, i, 0:1], S.rstd[:, h, i:i + 1],
                                              ALU.subtract, ALU.mult)
                    m.then_inc(hat, 1)
                dve.sem_inc(red_ok, 1)
                with dve.Fori(0, NB // 2) as i:
                    b = i * 2
                    for j in range(2):
                        dve.wait_ge(sq_ok, b + (j + 1))
                        dve.wait_ge(dk_ok, b + j)
                        dve.tensor_reduce(diag[:, j], sq[:, j].rearrange("p (h d) -> p h d", h=PH), AX.X, ALU.add
                                          ).then_inc(red_ok, 1)
                        dve.wait_ge(dk_in, b + (j + 1))
                        dve.tensor_reduce(kmax[:, bass.ds(b + j, 1)], psum[:, 2:4, :].rearrange("p a n -> p (a n)"), AX.X, ALU.max)
                        dve.wait_ge(red_ok, b + (j + 2))
                        dve.tensor_tensor(ddk[:, bass.ds(b + j, 1), :].rearrange("p o (h m) -> p (o h) m", h=PH),
                                          psum[:, 2:4, :].rearrange("p a (h m) -> p (a h) m", m=PM),
                                          diag[:, j, :, None].broadcast_to([P, PH, PM]),
                                          ALU.subtract).then_inc(dk_ok, 1)
                dve.wait_ge(dk_ok, NB)
                dve.tensor_reduce(kmax1[:], kmax[:], AX.X, ALU.max).then_inc(m1, 1)
                dve.wait_ge(m2, 1)
                dve.tensor_reduce(kmaxn[:], psum[0:1, 6, 0:P], AX.X, ALU.max).then_inc(m3, 1)
                dve.wait_ge(m4, 1)
                dve.tensor_scalar(nkmax[:], psum[:, 7, 0:1], -1.0, None, ALU.mult).then_inc(m5, 1)

            @block.tensor
            def _(pe):
                pe.wait_ge(in_id, 16)
                for h in range(2):
                    pe.wait_ge(hat, h + 1)
                    for i in range(HB):
                        m = pe.transpose(psum[:, 6 + h, i * P:(i + 1) * P], xhat[:, HB * h + i], ident[:])
                    m.then_inc(tp, 1)
                pe.wait_ge(in_wdk, 48)
                for n, w in enumerate((wkT, wqT)):
                    if n:
                        pe.wait_ge(in_wq, 32)
                        pe.wait_ge(wde, 1)
                    for q in range(NPAIR):
                        m = pe.matmul(psum[:, q // 4, (q % 4) * P:(q % 4 + 1) * P], w[:, q], proj2[:], start=True, stop=True)
                    m.then_inc(wdp, 1)
                pe.wait_ge(in_wk, 16)
                pe.wait_ge(in_wv, 16)
                pe.wait_ge(wde, 2)
                pe.sem_inc(v_in, 1)
                with pe.Fori(0, NB // 2) as i:
                    b = i * 2
                    for j in range(2):
                        pe.wait_ge(xtp, b + (j + 1))
                        for (w, bank, done, used) in ((wk, 0, k_in, sq_ok), (wdk, 2, dk_in, dk_ok), (wv, 4, v_in, v_ok)):
                            pe.wait_ge(used, b + j)
                            for n in range(2):
                                m = pe.matmul(psum[:, bank + n, :], xTp[:, j], w[:, n * 512:(n + 1) * 512], start=True, stop=True)
                            m.then_inc(done, 1)
                pe.wait_ge(m1, 1)
                pe.transpose(psum[0:1, 6, 0:P], kmax1[:], ident[:]).then_inc(m2, 1)
                pe.wait_ge(m3, 1)
                pe.matmul(psum[:, 7, 0:1], ones[0:1, :], kmaxn[:], start=True, stop=True).then_inc(m4, 1)

            @block.scalar
            def _(act):
                for h in range(2):
                    act.wait_ge(tp, h + 1)
                    act.activation(xT[:, h * HALF:(h + 1) * HALF], psum[:, 6 + h], ACT.Copy).then_inc(xTr, 1)
                for n, w in enumerate((wdk, wdq)):
                    act.wait_ge(wdp, n + 1)
                    act.activation(w[:], psum[:, 0:2].rearrange("p a n -> p (a n)"), ACT.Copy, scale=DN).then_inc(wde, 1)
                with act.Fori(0, NB // 2) as i:
                    b = i * 2
                    for j in range(2):
                        act.wait_ge(k_in, b + (j + 1))
                        act.wait_ge(red_ok, b + j)
                        act.activation(sq[:, j], psum[:, 0:2].rearrange("p a n -> p (a n)"), ACT.Square,
                                       scale=DN / 2 ** 0.5).then_inc(sq_ok, 1)
                        act.wait_ge(v_in, b + (j + 2))
                        act.activation(vaug[:, bass.ds(b + j, 1), :, 0:PD].rearrange("p o h d -> p (o h) d"),
                                       psum[:, 4:6].rearrange("p a (h d) -> p (a h) d", d=PD),
                                       ACT.Copy).then_inc(v_ok, 1)
        kept = dict(wq=wq, wdq=wdq, wo=wo, w1=w1, w2=w2, b1=b1, rows=rows, xTp=xTp, vaug=vaug, ddk=ddk, sq=sq, diag=diag,
                    nkmax=nkmax, epsk=epsk, in_wq=in_wq, in_wo=in_wo, in_ffn=in_ffn, in_row=in_row)
        performer_queries(nc, S, ctx, kept)


def performer_queries(nc, S, ctx, L):
    sem, psum, xres, xhat, xT, ident = S.sem, S.psum, S.xres, S.xhat, S.xT, S.ident
    wq, wdq, wo, w1, w2, b1, rows = (L[n] for n in ("wq", "wdq", "wo", "w1", "w2", "b1", "rows"))
    xTp, vaug, ddk, sq, diag, nkmax, epsk = (L[n] for n in ("xTp", "vaug", "ddk", "sq", "diag", "nkmax", "epsk"))
    c2 = ctx

    def sb(name, shape, dt=F32):
        return c2.enter_context(nc.sbuf_tensor(name, shape, dt))

    qe = sb("p_qe", [P, 2, PH * PM])
    qfT = sb("p_qfT", [P, 2, NPAIR, P])
    kf = sb("p_kf", [P, 2, PH * PM])
    kvb = sb("p_kvb", [P, 2, NPAIR, PAIR])
    qmax, qtot, rden = sb("p_qmax", [P, 2, PH]), sb("p_qtot", [P, 2, PH]), sb("p_rden", [P, 2, PH])
    att, attT = sb("p_att", [P, 2, PH * PD]), sb("p_attT", [P, 2, NPAIR, P])

    kvz, xtp, kfe, kfr, q_in, sqr, red, dq_in, qmx, qto, dqs, qex, qft, qfte, kv_in, kvr, num_in, rdn, nrm, att_in, atte, wo_in, xo = (
        sem(n) for n in (
            "b_zeros", "b_xTp", "b_kf_exp", "b_kf", "b_q_psum", "b_sq", "b_diag", "b_dq_psum", "b_qmax", "b_qtot",
            "b_qe", "b_qf", "b_qfT_psum", "b_qfT", "b_kv_psum", "b_kv", "b_num_psum", "b_rden", "b_att",
            "b_attT_psum", "b_attT", "b_wo_psum", "b_x"))

    with nc.Block() as block:
        @block.gpsimd
        def _(pool):
            pool.memset(kvb[:], 0.0).then_inc(kvz, 1)
            with pool.Fori(0, NB // 2) as i:
                b = i * 2
                pool.wait_ge(dq_in, b)
                for j in range(2):
                    pool.tensor_copy(xTp[:, j], xT[:, bass.ds((b + j) * P, P)]).then_inc(xtp, 1)
                for j in range(2):
                    pool.wait_ge(kfe, b + (j + 1))
                    pool.tensor_tensor(kf[:, j], kf[:, j], epsk[:].broadcast_to([P, PH * PM]), ALU.add).then_inc(kfr, 1)

        @block.scalar
        def _(act):
            def exp_k(b, j):
                act.activation(kf[:, j], ddk[:, bass.ds(b + j, 1), :].rearrange("p o n -> p (o n)"), ACT.Exp,
                               bias=nkmax[:]).then_inc(kfe, 1)

            def square_q(b, j):
                act.wait_ge(q_in, b + (j + 1))
                act.activation(sq[:, j], psum[:, 0:2].rearrange("p a n -> p (a n)"), ACT.Square,
                               scale=DN / 2 ** 0.5).then_inc(sqr, 1)

            def exp_q(b, j):
                act.wait_ge(dqs, b + (j + 1))
                act.activation(qe[:, j], qe[:, j], ACT.Exp).then_inc(qex, 1)

            def take_qfT(b, j):
                act.wait_ge(qft, b + (j + 1))
                act.activation(qfT[:, j].rearrange("p q n -> p (q n)"), psum[:, 0:2].rearrange("p a n -> p (a n)"),
                               ACT.Identity, bias=epsk[:]).then_inc(qfte, 1)

            def take_attT(b, j):
                act.wait_ge(att_in, b + (j + 1))
                bank = 2 - 2 * j
                act.activation(attT[:, j].rearrange("p q n -> p (q n)"),
                               psum[:, bank:bank + 2].rearrange("p a n -> p (a n)"), ACT.Copy).then_inc(atte, 1)

            with act.Fori(0, NB // 2) as i:
                b = i * 2
                exp_k(b, 0)
                square_q(b, 0)
                exp_k(b, 1)
                exp_q(b, 0)
                square_q(b, 1)
                take_qfT(b, 0)
                exp_q(b, 1)
                take_qfT(b, 1)
                take_attT(b, 0)
                take_attT(b, 1)

        @block.vector
        def _(dve):
            def shift_q(b, j):
                dd = psum[:, 2:4, :].rearrange("p a (h m) -> p (a h) m", m=PM)
                dve.wait_ge(sqr, b + (j + 1))
                dve.tensor_reduce(diag[:, j], sq[:, j].rearrange("p (h d) -> p h d", h=PH), AX.X, ALU.add).then_inc(red, 1)
                dve.wait_ge(dq_in, b + (j + 1))
                dve.tensor_reduce(qmax[:, j], dd, AX.X, ALU.max).then_inc(qmx, 1)
                dve.wait_ge(red, b + (j + 1))
                dve.wait_ge(qmx, b + (j + 1))
                dve.tensor_tensor(qtot[:, j], diag[:, j], qmax[:, j], ALU.add).then_inc(qto, 1)
                dve.wait_ge(qto, b + (j + 1))
                dve.tensor_tensor(qe[:, j].rearrange("p (h m) -> p h m", h=PH), dd,
                                  qtot[:, j, :, None].broadcast_to([P, PH, PM]), ALU.subtract).then_inc(dqs, 1)

            def take_kv(b, j):
                dve.wait_ge(kv_in, b + (j + 1))
                for lo, c in ((0, 0), (PD, VA)):
                    for q, n, banks in ((0, 3, 2), (6, 2, 1)):
                        m = dve.tensor_copy(
                            kvb[lo:lo + PD, j, q:q + n * banks, c:c + VA],
                            psum[lo:lo + PD, 4 + q // 3:4 + q // 3 + banks, 0:n * PAIR].rearrange(
                                "p a (q n) -> p (a q) n" if banks == 1 else "p a (q n) -> p a q n", n=PAIR)[..., c:c + VA])
                m.then_inc(kvr, 1)

            def divide(b, j):
                dve.wait_ge(num_in, b + (j + 1))
                two = psum[:, 4:6, 0:3 * PAIR].rearrange("p a (h n) -> p a h n", n=VA)
                one = psum[:, 6, 0:2 * PAIR].rearrange("p (h n) -> p h n", n=VA)
                dve.reciprocal(rden[:, j, 0:12].rearrange("p (a h) -> p a h", a=2), two[:, :, :, PD])
                dve.reciprocal(rden[:, j, 12:16], one[:, :, PD]).then_inc(rdn, 1)
                dve.wait_ge(rdn, b + (j + 1))
                dve.tensor_tensor(att[:, j, 0:12 * PD].rearrange("p (a h d) -> p a h d", a=2, h=6), two[:, :, :, 0:PD],
                                  rden[:, j, 0:12, None].rearrange("p (a h) o -> p a h o", a=2).broadcast_to([P, 2, 6, PD]),
                                  ALU.mult)
                dve.tensor_tensor(att[:, j, 12 * PD:].rearrange("p (h d) -> p h d", h=4), one[:, :, 0:PD],
                                  rden[:, j, 12:16, None].broadcast_to([P, 4, PD]), ALU.mult).then_inc(nrm, 1)

            dve.wait_ge(kvz, 1)
            with dve.Fori(0, NB // 2) as i:
                b = i * 2
                for j in range(2):
                    shift_q(b, j)
                    take_kv(b, j)
                for j in range(2):
                    divide(b, j)
                for j in range(2):
                    dve.wait_ge(wo_in, b + (j + 1))
                    xb = xhat[:, bass.ds(b + j, 1), :].rearrange("p o d -> p (o d)")
                    dve.tensor_tensor(xb, psum[:, 7, 0:D], xb, ALU.add).then_inc(xo, 1)

        @block.tensor
        def _(pe):
            def project(b, j):
                pe.wait_ge(xtp, b + (j + 1))
                for w, bank, done in ((wq, 0, q_in), (wdq, 2, dq_in)):
                    if j:
                        pe.wait_ge(sqr if bank == 0 else dqs, b + 1)
                    else:
                        pe.wait_ge(atte, b)
                    for n in range(2):
                        m = pe.matmul(psum[:, bank + n, :], xTp[:, j], w[:, n * 512:(n + 1) * 512], start=True, stop=True)
                    m.then_inc(done, 1)

            def keys_values(b, j):
                pe.wait_ge(kfr, b + (j + 1))
                pe.wait_ge(kvr, b + j)
                pe.wait_ge(nrm, b)
                for q in range(NPAIR):
                    m = pe.matmul(psum[:, 4 + q // 3, (q % 3) * PAIR:(q % 3 + 1) * PAIR], kf[:, j, q * P:(q + 1) * P],
                                  vaug[:, bass.ds(b + j, 1), 2 * q:2 * q + 2, :].rearrange("p o h d -> p (o h d)"),
                                  start=True, stop=True)
                m.then_inc(kv_in, 1)

            def turn_q(b, j):
                pe.wait_ge(qex, b + (j + 1))
                if j:
                    pe.wait_ge(qfte, b + 1)
                else:
                    pe.wait_ge(sqr, b + 2)
                for q in range(NPAIR):
                    m = pe.transpose(psum[:, q // 4, (q % 4) * P:(q % 4 + 1) * P], qe[:, j, q * P:(q + 1) * P], ident[:])
                m.then_inc(qft, 1)

            def numerators(b, j):
                pe.wait_ge(qfte, b + (j + 1))
                pe.wait_ge(kvr, b + 2)
                if j:
                    pe.wait_ge(nrm, b + 1)
                for q in range(NPAIR):
                    m = pe.matmul(psum[:, 4 + q // 3, (q % 3) * PAIR:(q % 3 + 1) * PAIR], qfT[:, j, q], kvb[:, j, q],
                                  start=True, stop=True)
                m.then_inc(num_in, 1)

            def turn_att(b, j):
                pe.wait_ge(nrm, b + (j + 1))
                if j:
                    pe.wait_ge(qfte, b + 2)
                else:
                    pe.wait_ge(dqs, b + 2)
                for q in range(NPAIR):
                    m = pe.transpose(psum[:, 2 - 2 * j + q // 4, (q % 4) * P:(q % 4 + 1) * P], att[:, j, q * P:(q + 1) * P], ident[:])
                m.then_inc(att_in, 1)

            def output(b, j):
                pe.wait_ge(atte, b + (j + 1))
                pe.wait_ge(xo, b + j)
                for q in range(NPAIR):
                    m = pe.matmul(psum[:, 7, 0:D], attT[:, j, q], wo[:, q], start=(q == 0), stop=(q == NPAIR - 1))
                m.then_inc(wo_in, 1)

            pe.wait_ge(L["in_wq"], 32)
            pe.wait_ge(L["in_wo"], 16)
            with pe.Fori(0, NB // 2) as i:
                b = i * 2
                project(b, 0)
                keys_values(b, 0)
                project(b, 1)
                turn_q(b, 0)
                keys_values(b, 1)
                numerators(b, 0)
                turn_q(b, 1)
                numerators(b, 1)
                turn_att(b, 0)
                turn_att(b, 1)
                output(b, 0)
                output(b, 1)
    performer_ffn(nc, S, L, w1, w2, b1, rows)


def performer_ffn(nc, S, L, w1, w2, b1, rows):
    sem, psum, xres, xhat, xT, ident = S.sem, S.psum, S.xres, S.xhat, S.xT, S.ident
    stats, mv, rstd = S.stats, S.mv, S.rstd
    EPS = 1e-6
    with ExitStack() as c:
        def sb(name, shape, dt=F32):
            return c.enter_context(nc.sbuf_tensor(name, shape, dt))

        o1b = sb("f_o1b", [P, NB, D])
        hb, he = (L["ddk"][:, n * HB:(n + 1) * HB, :].rearrange("p b (a n) -> p (b a n)", n=HALF).rearrange(
            "p (h f n) -> p h f n", h=2, n=HALF) for n in range(2))
        flat = L["vaug"][:].rearrange("p b h d -> p (b h d)")
        hm, hT = (flat[:, n * NB * HALF:(n + 1) * NB * HALF].rearrange("p (h f n) -> p h f n", h=2, n=HALF) for n in range(2))
        st, mvr, eps_, rs, half1, o1, o1br, tp, o1T, h_in, hbr, hmr, her, hpr, hTr, y_in, x2, half2, nrm, xr = (
            sem(n) for n in (
                "f_stats", "f_mv", "f_var_eps", "f_rstd", "f_ln_half", "f_out1", "f_out1_b2", "f_tp", "f_out1T",
                "f_h_psum", "f_hb", "f_hm", "f_he", "f_hp", "f_hT", "f_y_psum", "f_x2", "f_ln_half2", "f_ln2", "f_x"))
        with nc.Block() as block:
            @block.gpsimd
            def _(pool):
                def rsqrt(n, h):
                    pool.wait_ge(mvr, n + 1)
                    pool.tensor_scalar(rstd[:, h], mv[:, h, :, 1], EPS, 1.0, ALU.add, ALU.mult).then_inc(eps_, 1)
                    pool.wait_ge(eps_, n + 1)
                    pool.tensor_tensor(rstd[:, h], rstd[:, h], S.nhalf[:, 0:HB], ALU.pow).then_inc(rs, 1)

                rsqrt(0, 0)
                rsqrt(1, 1)
                pool.wait_ge(L["in_row"], 80)
                for h in range(2):
                    pool.wait_ge(o1, h + 1)
                    t = slice(HB * h, HB * h + HB)
                    pool.tensor_tensor(o1b[:, t], xhat[:, t], rows[:, 4, None, :].broadcast_to([P, HB, D]), ALU.add
                                       ).then_inc(o1br, 1)
                rsqrt(2, 0)
                rsqrt(3, 1)

            @block.vector
            def _(dve):
                def statistics(n, h, src):
                    for i in range(HB):
                        dve.bn_stats(stats[:, h, i], src[:, HB * h + i]).then_inc(st, 1)
                    dve.wait_ge(st, HB * (n + 1))
                    for i in range(HB):
                        m = dve.bn_aggr(mv[:, h, i], stats[:, h, i])
                    m.then_inc(mvr, 1)

                def normalise(n, h, x, g, half, done):
                    dve.wait_ge(rs, n + 1)
                    dve.wait_ge(mvr, n + 1)
                    for i in range(HB):
                        b = HB * h + i
                        m = dve.scalar_tensor_tensor(out=x[:, b], in0=x[:, b], scalar=mv[:, h, i, 0:1], in1=rows[:, g],
                                                     op0=ALU.subtract, op1=ALU.mult)
                    m.then_inc(half, 1)
                    dve.wait_ge(half, h + 1)
                    for i in range(HB):
                        b = HB * h + i
                        m = dve.scalar_tensor_tensor(out=x[:, b], in0=x[:, b], scalar=rstd[:, h, i:i + 1],
                                                     in1=rows[:, g + 1], op0=ALU.mult, op1=ALU.add)
                    m.then_inc(done, 1)

                statistics(0, 0, xhat)
                statistics(1, 1, xhat)
                dve.wait_ge(L["in_row"], 80)
                normalise(0, 0, xhat, 0, half1, o1)
                normalise(1, 1, xhat, 0, half1, o1)
                for h in range(2):
                    for f in range(PFB):
                        n = PFB * h + f
                        dve.wait_ge(hbr, n + 1)
                        dve.tensor_scalar(hm[:, h, f], hb[:, h, f], 0.0, None, ALU.min).then_inc(hmr, 1)
                        dve.tensor_scalar(hb[:, h, f], hb[:, h, f], 0.0, -1.0, ALU.max, ALU.add).then_inc(hpr, 1)
                    for f in range(PFB):
                        n = PFB * h + f
                        dve.wait_ge(her, n + 1)
                        dve.wait_ge(hpr, n + 1)
                        dve.tensor_tensor(hT[:, h, f], hb[:, h, f], he[:, h, f], ALU.add).then_inc(hTr, 1)
                for h in range(2):
                    t = slice(HB * h, HB * h + HB)
                    dve.wait_ge(y_in, h + 1)
                    dve.wait_ge(o1br, h + 1)
                    dve.tensor_tensor(o1b[:, t], psum[:, 6 + h].rearrange("p (b d) -> p b d", b=HB), o1b[:, t], ALU.add
                                      ).then_inc(x2, 1)
                    dve.wait_ge(x2, h + 1)
                    statistics(2 + h, h, o1b)
                for h in range(2):
                    t = slice(HB * h, HB * h + HB)
                    normalise(2 + h, h, o1b, 2, half2, nrm)
                    dve.wait_ge(nrm, h + 1)
                    dve.tensor_tensor(xres[:, t], xres[:, t], o1b[:, t], ALU.add).then_inc(xr, 1)

            @block.tensor
            def _(pe):
                pe.wait_ge(L["in_ffn"], 48)
                for h in range(2):
                    pe.wait_ge(o1, h + 1)
                    for i in range(HB):
                        m = pe.transpose(psum[:, h, i * P:(i + 1) * P], xhat[:, HB * h + i], ident[:])
                    m.then_inc(tp, 1)
                    pe.wait_ge(o1T, h + 1)
                    for f in range(PFB):
                        if h:
                            pe.wait_ge(hbr, f + 1)
                        pe.matmul(psum[:, 2 + f], w1[:, f * P:(f + 1) * P], xT[:, h * HALF:(h + 1) * HALF],
                                  start=True, stop=True).then_inc(h_in, 1)
                for h in range(2):
                    pe.wait_ge(hTr, PFB * (h + 1))
                    for i in range(HB):
                        for f in range(PFB):
                            m = pe.matmul(psum[:, 6 + h, i * P:(i + 1) * P], hT[:, h, f, i * P:(i + 1) * P], w2[:, f],
                                          start=(f == 0), stop=(f == PFB - 1))
                    m.then_inc(y_in, 1)

            @block.scalar
            def _(act):
                act.wait_ge(L["in_ffn"], 48)
                for h in range(2):
                    act.wait_ge(tp, h + 1)
                    act.activation(xT[:, h * HALF:(h + 1) * HALF], psum[:, h], ACT.Copy).then_inc(o1T, 1)
                    for f in range(PFB):
                        act.wait_ge(h_in, PFB * h + f + 1)
                        act.activation(hb[:, h, f], psum[:, 2 + f], ACT.Identity, bias=b1[:, f:f + 1]).then_inc(hbr, 1)
                    for f in range(PFB):
                        act.wait_ge(hmr, PFB * h + f + 1)
                        act.activation(he[:, h, f], hm[:, h, f], ACT.Exp).then_inc(her, 1)


XH, XD = 16, 8
XC = 4
XHC = XH // XC


def stage_cross0(nc, S, A):
    psum, ident, xres, xhat, xT = S.psum, S.ident, S.xres, S.xhat, S.xT
    with ExitStack() as c:
        sem = S.sem

        def sb(name, shape, dt=F32):
            return c.enter_context(nc.sbuf_tensor(name, shape, dt))

        qT, kT = sb("x_qT", [P, NB * P]), sb("x_kT", [P, NB * P])
        vall = sb("x_v", [P, NB, XH, XD + 1])
        km = sb("x_km", [P, 2, XH, P])
        qTp = sb("x_qTp", [P, 2, P])
        mx = sb("x_max", [P, 2, XH])
        e, eT = sb("x_e", [P, 2, XH, P]), sb("x_eT", [P, 2, XH, P])
        rden, att, attT = sb("x_rden", [P, 2, XH]), sb("x_att", [P, 2, D]), sb("x_attT", [P, 2, P])
        N = Norm(sem, "x")
        ones_v, kps, kTr, vps, vr, qps, qTr, xb = (sem(n) for n in (
            "x_ones", "x_k_psum", "x_kT", "x_v_psum", "x_v", "x_q_psum", "x_qT", "x_x_bo"))
        with nc.Block() as block:
            @block.gpsimd
            def _(pool):
                pool.memset(vall[:, :, :, XD:XD + 1], 1.0).then_inc(ones_v, 1)
                norm_pool(pool, S, N, EPS_OUTER)
                pool.wait_ge(S.in_x0, 16 * 10)
                pool.wait_ge(N.hat, 2)
                pool.tensor_tensor(xres[:], xres[:], S.x0rows[:, 1, None, :].broadcast_to([P, NB, D]), ALU.add).then_inc(xb, 1)

            @block.vector
            def _(dve):
                norm_vector(dve, S, N, xres, xhat)
                dve.wait_ge(S.in_x0, 16 * 10)
                for h in range(2):
                    dve.wait_ge(vps, h + 1)
                    dve.tensor_tensor(vall[:, HB * h:HB * h + HB, :, 0:XD],
                                      psum[:, 2 + h].rearrange("p (b h d) -> p b h d", b=HB, h=XH),
                                      S.x0rows[:, 0, :].rearrange("p (o h d) -> p o h d", o=1, h=XH).broadcast_to([P, HB, XH, XD]),
                                      ALU.add).then_inc(vr, 1)

            @block.tensor
            def _(pe):
                pe.wait_ge(S.in_x0, 16 * 10)
                for h in range(2):
                    pe.matmul(psum[:, h], S.x0w[:, 1], S.ctxT[:, h * HALF:(h + 1) * HALF], start=True, stop=True).then_inc(kps, 1)
                for h in range(2):
                    for i in range(HB):
                        b = HB * h + i
                        m = pe.matmul(psum[:, 2 + h, i * P:(i + 1) * P], S.ctxT[:, b * P:(b + 1) * P], S.x0w[:, 2],
                                      start=True, stop=True)
                    m.then_inc(vps, 1)
                norm_tensor(pe, S, N, 4)
                for h in range(2):
                    pe.wait_ge(N.xT, h + 1)
                    pe.matmul(psum[:, 6 + h], S.x0w[:, 0], xT[:, h * HALF:(h + 1) * HALF], start=True, stop=True).then_inc(qps, 1)

            @block.scalar
            def _(act):
                act.wait_ge(S.in_x0, 16 * 10)
                for h in range(2):
                    act.wait_ge(kps, h + 1)
                    act.activation(kT[:, h * HALF:(h + 1) * HALF], psum[:, h], ACT.Identity, bias=S.x0cols[:, 1:2]).then_inc(kTr, 1)
                norm_scalar(act, S, N, 4, xT)
                for h in range(2):
                    act.wait_ge(qps, h + 1)
                    act.activation(qT[:, h * HALF:(h + 1) * HALF], psum[:, 6 + h], ACT.Identity, bias=S.x0cols[:, 0:1]).then_inc(qTr, 1)

        kmr, qpr, s_in, mxr, sub, ex, t_in, t_out, o_in, rd, o_out, at_in, at_out, y_in, y_out = (sem(n) for n in (
            "xl_km", "xl_qT", "xl_s_psum", "xl_max", "xl_e_sub", "xl_e", "xl_eT_psum", "xl_eT", "xl_o_psum", "xl_rden",
            "xl_att", "xl_attT_psum", "xl_attT", "xl_y_psum", "xl_x"))
        with nc.Block() as block:
            @block.gpsimd
            def _(pool):
                with pool.Fori(0, NB // 2) as i:
                    b = i * 2
                    pool.wait_ge(s_in, b * XC)
                    for j in range(2):
                        pool.tensor_tensor(
                            km[:, j], kT[:, bass.ds((b + j) * P, P)].rearrange("p (o n) -> p o n", o=1).broadcast_to([P, XH, P]),
                            S.headmask[:, :, None].broadcast_to([P, XH, P]), ALU.mult).then_inc(kmr, 1)

            @block.scalar
            def _(act):
                with act.Fori(0, NB // 2) as i:
                    b = i * 2
                    act.wait_ge(s_in, b * XC)
                    for j in range(2):
                        act.activation(qTp[:, j], qT[:, bass.ds((b + j) * P, P)], ACT.Copy).then_inc(qpr, 1)

                    def exp(j, k):
                        act.wait_ge(sub, (b + j) * XC + (k + 1 + XC))
                        ap = e[:, j, k * XHC:(k + 1) * XHC]
                        act.activation(ap, ap, ACT.Exp, scale=float(XD) ** -0.5).then_inc(ex, 1)

                    def take(j, k):
                        act.wait_ge(t_in, (b + j) * XC + (k + 1))
                        act.activation(eT[:, j, k * XHC:(k + 1) * XHC].rearrange("p h n -> p (h n)"), psum[:, 4 + k % 2],
                                       ACT.Copy).then_inc(t_out, 1)

                    for k in range(XC):
                        exp(0, k)
                    for k in range(XC):
                        take(0, k)
                        exp(1, k)
                    for k in range(XC):
                        take(1, k)
                    for j in range(2):
                        act.wait_ge(at_in, b + (j + 1))
                        act.activation(attT[:, j], psum[:, 7, 0:P], ACT.Copy).then_inc(at_out, 1)

            @block.vector
            def _(dve):
                dve.sem_inc(sub, XC)
                with dve.Fori(0, NB // 2) as i:
                    b = i * 2
                    for j in range(2):
                        for k in range(XC):
                            s = psum[:, k].rearrange("p (h n) -> p h n", h=XHC)
                            dve.wait_ge(s_in, (b + j) * XC + (k + 1))
                            dve.tensor_reduce(mx[:, j, k * XHC:(k + 1) * XHC], s, AX.X, ALU.max).then_inc(mxr, 1)
                            dve.wait_ge(mxr, (b + j) * XC + (k + 1))
                            dve.tensor_tensor(e[:, j, k * XHC:(k + 1) * XHC], s,
                                              mx[:, j, k * XHC:(k + 1) * XHC, None].broadcast_to([P, XHC, P]),
                                              ALU.subtract).then_inc(sub, 1)
                    for j in range(2):
                        o = psum[:, 6, 0:XH * (XD + 1)].rearrange("p (h d) -> p h d", h=XH)
                        dve.wait_ge(o_in, b + (j + 1))
                        dve.reciprocal(rden[:, j], o[:, :, XD]).then_inc(rd, 1)
                        dve.wait_ge(rd, b + (j + 1))
                        dve.tensor_tensor(att[:, j].rearrange("p (h d) -> p h d", h=XH), o[:, :, 0:XD],
                                          rden[:, j, :, None].broadcast_to([P, XH, XD]), ALU.mult).then_inc(o_out, 1)
                    for j in range(2):
                        xb_ = xres[:, bass.ds(b + j, 1), :].rearrange("p o d -> p (o d)")
                        dve.wait_ge(y_in, b + (j + 1))
                        dve.tensor_tensor(xb_, psum[:, 7, P:2 * P], xb_, ALU.add).then_inc(y_out, 1)

            @block.tensor
            def _(pe):
                pe.sem_inc(t_out, 2)
                with pe.Fori(0, NB // 2) as i:
                    b = i * 2

                    def scores(j):
                        pe.wait_ge(kmr, b + (j + 1))
                        pe.wait_ge(qpr, b + (j + 1))
                        for k in range(XC):
                            pe.wait_ge(sub, (b + j) * XC + (k + 1))
                            pe.matmul(psum[:, k], qTp[:, j], km[:, j, k * XHC:(k + 1) * XHC].rearrange("p h n -> p (h n)"),
                                      start=True, stop=True).then_inc(s_in, 1)

                    def turn(j, k):
                        pe.wait_ge(ex, (b + j) * XC + (k + 1))
                        pe.wait_ge(t_out, (b + j) * XC + (k + 1))
                        for h in range(XHC):
                            m = pe.transpose(psum[:, 4 + k % 2, h * P:(h + 1) * P], e[:, j, k * XHC + h], ident[:])
                        m.then_inc(t_in, 1)

                    def values(j):
                        pe.wait_ge(t_out, (b + j) * XC + (XC + 2))
                        pe.wait_ge(o_out, b + j)
                        for h in range(XH):
                            m = pe.matmul(psum[:, 6, h * (XD + 1):(h + 1) * (XD + 1)], eT[:, j, h],
                                          vall[:, bass.ds(b + j, 1), h].rearrange("p o d -> p (o d)"), start=True, stop=True)
                        m.then_inc(o_in, 1)

                    def turn_att(j):
                        pe.wait_ge(o_out, b + (j + 1))
                        pe.wait_ge(y_out, b + j)
                        pe.transpose(psum[:, 7, 0:P], att[:, j], ident[:]).then_inc(at_in, 1)

                    def output(j):
                        pe.wait_ge(at_out, b + (j + 1))
                        pe.matmul(psum[:, 7, P:2 * P], attT[:, j], S.x0w[:, 3], start=True, stop=True).then_inc(y_in, 1)

                    scores(0)
                    scores(1)
                    for k in range(XC):
                        turn(0, k)
                    turn(1, 0)
                    turn(1, 1)
                    values(0)
                    turn(1, 2)
                    turn(1, 3)
                    turn_att(0)
                    values(1)
                    output(0)
                    turn_att(1)
                    output(1)


ME, MF = 8, 256
MFB = MF // P
MU = 2 * MFB


def stage_moe(nc, S, A):
    psum, ident, xres, xhat, xT = S.psum, S.ident, S.xres, S.xhat, S.xT
    with ExitStack() as c:
        sem = S.sem

        def sb(name, shape, dt=F32):
            return c.enter_context(nc.sbuf_tensor(name, shape, dt))

        router = sb("m_router", [P, ME])
        wg, wu = sb("m_wg", [P, 2, MF]), sb("m_wu", [P, 2, MF])
        wd = sb("m_wd", [P, ME * MFB, D])
        wT = sb("m_wT", [ME, NB * P])
        wTm = sb("m_wTm", [ME, ME, NB * P])
        zero = sb("m_zero", [P, P])
        rank = sb("m_rank", [P, ME])
        R = sb("m_r", [P, 8, NB, ME])
        r1 = sb("m_r1", [P, 8, NB])
        wbc = sb("m_wbc", [P, 2, HALF])
        sg, fT = sb("m_sg", [P, 2, HALF]), sb("m_fT", [P, 4, HALF])
        N = Norm(sem, "m")
        in_r, in_wd, lg, cs, v, ae, wps, wTr, wm, zr = (sem(n) for n in (
            "m_in_router", "m_in_wd", "m_logits", "m_const", "m_route", "m_exp", "m_wT_psum", "m_wT", "m_wTm", "m_zeroed"))
        in_w = [sem(f"m_in_w{j}") for j in range(2)]
        gu, sgr, sgw, fr, dn, wb_in, wb, xr = (sem(n) for n in (
            "m_gu_psum", "m_silu", "m_weighted", "m_fused", "m_down", "m_wbc_psum", "m_wbc", "m_x"))

        def flat(t):
            return t.rearrange("p b e -> p (b e)")

        with nc.Block() as block:
            @block.sync
            def _(sp):
                load(sp, router[:], A["router"], in_r)
                load(sp, rank[:], A["rank"].partition_broadcast(P), in_r)
                load(sp, wd[:], A["mwd"], in_wd)
                with sp.Fori(0, ME // 2) as i:
                    for j in range(2):
                        sp.wait_ge(gu, i * (2 * MU) + (j + 1) * MU)
                        for w, n in ((wg, "mwg"), (wu, "mwu")):
                            sp.dma_start(w[:, j], A[n][:, bass.ds(i * 2 + j, 1), :].rearrange("p o f -> p (o f)")).then_inc(in_w[j], 16)

            @block.gpsimd
            def _(pool):
                pool.memset(zero[:], 0.0).then_inc(cs, 1)
                norm_pool(pool, S, N, EPS_OUTER)
                with pool.Fori(0, ME // 2) as i:
                    for n in range(2 * MU):
                        u = i * (2 * MU)
                        pool.wait_ge(sgr, u + (n + 1))
                        pool.wait_ge(wb, i * 4 + (2 * (n // MU) + n % 2 + 1))
                        pool.tensor_tensor(sg[:, n % 2], sg[:, n % 2], wbc[:, n % 2], ALU.mult).then_inc(sgw, 1)

            @block.scalar
            def _(act):
                norm_scalar(act, S, N, 0, xT)
                act.wait_ge(v, 2)
                act.activation(flat(R[:, 0]), flat(R[:, 0]), ACT.Exp).then_inc(ae, 1)
                act.wait_ge(v, 17)
                act.activation(r1[:, 5], r1[:, 4], ACT.Exp).then_inc(ae, 1)
                for h in range(2):
                    act.wait_ge(wps, h + 1)
                    act.activation(wT[:, h * HALF:(h + 1) * HALF], psum[0:ME, 3 + h], ACT.Copy).then_inc(wTr, 1)
                with act.Fori(0, ME // 2) as i:
                    u = i * (2 * MU)
                    for n in range(2 * MU):
                        if n % MU < 2:
                            act.wait_ge(wb_in, i * 4 + (2 * (n // MU) + n % 2 + 1))
                            act.wait_ge(sgw, u + (n - n % MU))
                            act.activation(wbc[:, n % 2], psum[:, 4 + n % 2], ACT.Copy).then_inc(wb, 1)
                        act.wait_ge(gu, u + (n + 1 + 2 * MU))
                        act.wait_ge(fr, u + (n + 2))
                        act.activation(sg[:, n % 2], psum[:, n % 2], ACT.Silu).then_inc(sgr, 1)

            @block.vector
            def _(dve):
                norm_vector(dve, S, N, xres, xhat)
                count = [0]

                def step(m):
                    count[0] += 1
                    m.then_inc(v, 1)
                    dve.wait_ge(v, count[0])

                def bc(a):
                    return a[:, :, None].broadcast_to([P, NB, ME])

                dve.wait_ge(lg, 1)
                dve.wait_ge(in_r, 32)
                lgt = psum[:, 2, 0:NB * ME].rearrange("p (b e) -> p b e", b=NB)
                rk = rank[:, None, :].broadcast_to([P, NB, ME])
                step(dve.tensor_reduce(r1[:, 0], lgt, AX.X, ALU.max))
                step(dve.tensor_tensor(R[:, 0], lgt, bc(r1[:, 0]), ALU.subtract))
                dve.wait_ge(ae, 1)
                step(dve.tensor_reduce(r1[:, 1], R[:, 0], AX.X, ALU.add))
                step(dve.reciprocal(r1[:, 2], r1[:, 1]))
                step(dve.tensor_tensor(R[:, 1], R[:, 0], bc(r1[:, 2]), ALU.mult))
                for k in range(2):
                    pr, first = R[:, 1 + 3 * k], R[:, 3 + 3 * k]
                    step(dve.tensor_reduce(r1[:, 3 + 3 * k], pr, AX.X, ALU.max))
                    step(dve.tensor_tensor(R[:, 2 + 3 * k], pr, bc(r1[:, 3 + 3 * k]), ALU.is_equal))
                    step(dve.tensor_tensor(R[:, 2 + 3 * k], R[:, 2 + 3 * k], rk, ALU.mult))
                    step(dve.tensor_reduce(r1[:, 7], R[:, 2 + 3 * k], AX.X, ALU.max))
                    step(dve.tensor_tensor(first, R[:, 2 + 3 * k], bc(r1[:, 7]), ALU.is_equal))
                    if k == 0:
                        step(dve.scalar_tensor_tensor(out=flat(R[:, 4]), in0=flat(first), scalar=-2.0, in1=flat(pr),
                                                      op0=ALU.mult, op1=ALU.add))
                step(dve.tensor_tensor(r1[:, 4], r1[:, 6], r1[:, 3], ALU.subtract))
                assert count[0] == 17
                dve.wait_ge(ae, 2)
                step(dve.tensor_scalar(r1[:, 0], r1[:, 5], 1.0, None, ALU.add))
                step(dve.reciprocal(r1[:, 1], r1[:, 0]))
                step(dve.tensor_tensor(r1[:, 2], r1[:, 5], r1[:, 1], ALU.mult))
                step(dve.tensor_tensor(R[:, 3], R[:, 3], bc(r1[:, 1]), ALU.mult))
                step(dve.tensor_tensor(R[:, 6], R[:, 6], bc(r1[:, 2]), ALU.mult))
                step(dve.tensor_tensor(R[:, 7], R[:, 3], R[:, 6], ALU.add))
                dve.wait_ge(wTr, 2)
                for x in range(ME):
                    m = dve.tensor_scalar(wTm[:, x], wT[:], ident[0:ME, x:x + 1], None, ALU.mult)
                m.then_inc(wm, 1)
                dve.sem_inc(fr, 3)
                with dve.Fori(0, ME // 2) as i:
                    u = i * (2 * MU)
                    for n in range(2 * MU):
                        dve.wait_ge(sgw, u + (n + 1))
                        dve.wait_ge(dn, u + (n + 1))
                        dve.tensor_tensor(fT[:, n % 4], sg[:, n % 2], psum[:, 2 + n % 2],
                                          ALU.mult).then_inc(fr, 1)
                dve.wait_ge(dn, ME * MU + 4)
                for h in range(2):
                    t = slice(HB * h, HB * h + HB)
                    dve.tensor_tensor(xres[:, t], psum[:, 6 + h].rearrange("p (b d) -> p b d", b=HB), xres[:, t], ALU.add).then_inc(xr, 1)

            @block.tensor
            def _(pe):
                norm_tensor(pe, S, N, 0)
                pe.wait_ge(in_r, 32)
                pe.wait_ge(N.xT, 2)
                for b in range(NB):
                    m = pe.matmul(psum[:, 2, b * ME:(b + 1) * ME], xT[:, b * P:(b + 1) * P], router[:], start=True, stop=True)
                m.then_inc(lg, 1)
                pe.wait_ge(cs, 1)
                for h in range(2):
                    m = pe.matmul(psum[:, 6 + h], zero[:], xT[:, h * HALF:(h + 1) * HALF], start=True, stop=False,
                                  skip_group_check=True)
                m.then_inc(zr, 1)
                pe.wait_ge(v, 23)
                for h in range(2):
                    for i in range(HB):
                        m = pe.transpose(psum[0:ME, 3 + h, i * P:(i + 1) * P], R[:, 7, HB * h + i], ident[:])
                    m.then_inc(wps, 1)
                pe.wait_ge(wm, 1)
                pe.wait_ge(in_wd, 16)
                pe.sem_inc(gu, 2 * MU)
                pe.sem_inc(dn, 4)
                with pe.Fori(0, ME // 2) as i:
                    u = i * (2 * MU)

                    def up(n):
                        j, fb, h = n // MU, n % MU // 2, n % 2
                        if n % MU == 0:
                            pe.wait_ge(in_w[j], i * 32 + 32)
                        if n % MU < 2:
                            pe.wait_ge(wb, i * 4 + 2 * j)
                            pe.matmul(psum[:, 4 + h], S.ones[0:ME, :], wTm[:, bass.ds(i * 2 + j, 1), h * HALF:(h + 1) * HALF]
                                      .rearrange("p o n -> p (o n)"), start=True, stop=True).then_inc(wb_in, 1)
                        pe.wait_ge(fr, u + (n + 2))
                        pe.matmul(psum[:, h], wg[:, j, fb * P:(fb + 1) * P], xT[:, h * HALF:(h + 1) * HALF], start=True, stop=True)
                        pe.matmul(psum[:, 2 + h], wu[:, j, fb * P:(fb + 1) * P], xT[:, h * HALF:(h + 1) * HALF],
                                  start=True, stop=True).then_inc(gu, 1)

                    def down(n):
                        j, fb, h = n // MU, n % MU // 2, n % 2
                        pe.wait_ge(fr, u + (n + 4))
                        for q in range(HB):
                            m = pe.matmul(psum[:, 6 + h, q * P:(q + 1) * P], fT[:, n % 4, q * P:(q + 1) * P],
                                          wd[:, bass.ds((i * 2 + j) * MFB + fb, 1), :].rearrange("p o d -> p (o d)"),
                                          start=False, stop=False, skip_group_check=True)
                        m.then_inc(dn, 1)

                    for n in range(2 * MU):
                        up(n)
                        if n >= 2:
                            down(n - 2)
                    down(2 * MU - 2)
                    down(2 * MU - 1)



LL = 4
QH, QD = 16, 8
LF = 512
LFB = LF // P
NQ = 6
EPS_L1 = 1e-5
ROUND = 1.5 * 2.0 ** 23
LW1, LB1, LW2, LB2, LQB, LFC = 0, 1, 2, 3, 4, 4 + NQ
LCOLS = LFC + LFB
POOL_COLS = P


def stage_layers(nc, S, A):
    psum, ident, xres, xhat = S.psum, S.ident, S.xres, S.xhat
    with ExitStack() as c:
        sem = S.sem

        def sb(name, shape, dt=F32):
            return c.enter_context(nc.sbuf_tensor(name, shape, dt))

        wqkv, wp, wc = sb("l_wqkv", [P, NQ, P]), sb("l_wp", [P, D]), sb("l_wc", [P, D])
        wf, wm = sb("l_wf", [P, LF]), sb("l_wm", [P, LFB, D])
        cols, rows = sb("l_cols", [P, LL, LCOLS]), sb("l_rows", [P, LL, 2, D])
        hart, hneg, filt = sb("l_hart", [P, P]), sb("l_hneg", [P, P]), sb("l_filt", [P, P])
        halfpi, rnd = sb("l_halfpi", [P, 1]), sb("l_round", [P, 2])
        xl = sb("l_x", [P, NB, D])
        xnT = sb("l_xnT", [P, 2, HALF])
        Q = sb("l_q", [P, 2, 4, 3, HALF])
        R, T = sb("l_r", [P, 2, 4, HALF]), sb("l_t", [P, 3, 4, HALF])
        z = sb("l_z", [P, 2, HALF])
        gT = sb("l_g", [P, 2, LFB, HALF])
        N0 = Norm(sem, "l0")
        N = Norm(sem, "l")
        in_c, in_q, in_p, in_f, in_m, cst, neg = (sem(n) for n in (
            "l_in_const", "l_in_wqkv", "l_in_wp", "l_in_wf", "l_in_wm", "l_const", "l_hneg_made"))
        q_in, q_out, rr, kk, red_, absd, cosd, dif, hv, hp = (sem(n) for n in (
            "l_q_psum", "l_q_taken", "l_turns_t", "l_turns", "l_reduced", "l_abs", "l_cos", "l_diff",
            "l_ham_vector", "l_ham_pool"))
        wc_in, wc_out, f_in, f_out, p_in, x1, xb, t2, h_in, g_out, y_in, x2, xb2 = (sem(n) for n in (
            "l_wc_psum", "l_wc_made", "l_hart_psum", "l_z_made", "l_proj_psum", "l_x1", "l_x_bias", "l_turned2",
            "l_h_psum", "l_gelu", "l_y_psum", "l_x2", "l_x_bias2"))
        last = sem("l_x_out")
        colr = sem("l_columns")
        lcol = sb("l_lcol", [P, LCOLS])

        with nc.Block() as block:
            @block.sync
            def _(sp):
                load(sp, cols[:], A["lcols"], in_c)
                load(sp, hart[:], A["hartley"], in_c)
                load(sp, filt[:], A["filter"], in_c)
                load(sp, rows[:].rearrange("p l k d -> p (l k d)"), A["lrows"].partition_broadcast(P), in_c)
                with sp.Fori(0, LL) as l:
                    for w, n, used, per, got in ((wqkv, "lwqkv", q_in, 2 * NQ, in_q), (wp, "lwp", wc_in, 1, in_p),
                                                 (wf, "lwf", h_in, 2 * LFB, in_f), (wm, "lwm", y_in, 2, in_m)):
                        sp.wait_ge(used, l * per)
                        dst = w[:].rearrange("p a b -> p (a b)") if len(w.shape) == 3 else w[:]
                        sp.dma_start(dst, A[n][:, bass.ds(l, 1), :].rearrange("p o f -> p (o f)")).then_inc(got, 16)

            def parts(h, k, lo, hi):
                return Q[:, h, :, k, lo:hi]

            def hamilton(eng, h, lo, hi, count, base, sem_):
                n = hi - lo
                a, b, v = parts(h, 0, lo, hi), parts(h, 1, lo, hi), parts(h, 2, lo, hi)
                r = R[:, h, :, lo:hi]

                def t(i):
                    return T[:, i, :, lo:hi]

                def sq(x):
                    return x.rearrange("p (s c) n -> p s c n", s=2)

                def bc(i, shape):
                    x = a[:, i]
                    return (x[:, None, :] if len(shape) == 3 else x[:, None, None, :]).broadcast_to(shape)

                def go(out, x, y, op, after=0):
                    if after:
                        eng.wait_ge(sem_, base + after)
                    eng.tensor_tensor(out, x, y, op).then_inc(sem_, 1)

                def first():
                    go(r, bc(0, [P, 4, n]), b, ALU.mult)
                    go(sq(t(0)), bc(1, [P, 2, 2, n]), sq(b)[:, :, ::-1], ALU.mult)
                    go(sq(t(1)), bc(2, [P, 2, 2, n]), sq(b)[:, ::-1], ALU.mult)
                    go(r[:, 0:4:2], r[:, 0:4:2], t(0)[:, 0:4:2], ALU.subtract, 2)
                    go(r[:, 1:4:2], r[:, 1:4:2], t(0)[:, 1:4:2], ALU.add, 2)

                def second():
                    go(t(2), bc(3, [P, 4, n]), b[:, ::-1], ALU.mult)
                    go(r[:, 0:4:3], r[:, 0:4:3], t(1)[:, 0:4:3], ALU.subtract, 5)
                    go(r[:, 1:3], r[:, 1:3], t(1)[:, 1:3], ALU.add, 5)

                def third():
                    go(r[:, 0:2], r[:, 0:2], t(2)[:, 0:2], ALU.subtract, 8)
                    go(r[:, 2:4], r[:, 2:4], t(2)[:, 2:4], ALU.add, 8)
                    go(r, r, v, ALU.mult, 10)

                return first, second, third

            STEPS = 11

            @block.gpsimd
            def _(pool):
                norm_pool(pool, S, N0, EPS_OUTER)
                pool.memset(halfpi[:], float(np.pi / 2)).then_inc(cst, 1)
                pool.memset(rnd[:, 0:1], ROUND).then_inc(cst, 1)
                pool.memset(rnd[:, 1:2], -ROUND).then_inc(cst, 1)
                pool.memset(S.eps[:], EPS_L1).then_inc(cst, 1)
                for h in range(2):
                    for k in range(3):
                        pool.memset(Q[:, h, 1, k].rearrange("p (b n) -> p b n", n=P)[:, :, 0:1], 0.0).then_inc(cst, 1)
                pool.wait_ge(cst, 10)

                with pool.Fori(0, LL) as l:
                    def rsqrt(i, h):
                        pool.wait_ge(N.mv, l * 4 + (i + 1))
                        pool.tensor_tensor(S.rstd[:, h], S.mv[:, h, :, 1], S.eps[:, 0:HB], ALU.add).then_inc(N.eps, 1)
                        pool.wait_ge(N.eps, l * 4 + (i + 1))
                        pool.tensor_tensor(S.rstd[:, h], S.rstd[:, h], S.nhalf[:, 0:HB], ALU.pow).then_inc(N.rstd, 1)

                    def add_bias(k, h, after, n, done):
                        pool.wait_ge(in_c, 64)
                        pool.wait_ge(after, n)
                        x = xl[:, HB * h:HB * h + HB]
                        row = rows[:, bass.ds(l, 1), k, :].broadcast_to([P, HB, D])
                        pool.tensor_tensor(x, x, row, ALU.add).then_inc(done, 1)

                    rsqrt(0, 0)
                    rsqrt(1, 1)
                    pool.wait_ge(in_c, 64)
                    ham = []
                    for h in range(2):
                        ham.append(hamilton(pool, h, HALF - POOL_COLS, HALF, None, l * (2 * STEPS) + h * STEPS, hp))
                    add_bias(0, 0, N.hat, l * 4 + 1, xb)
                    add_bias(0, 1, N.hat, l * 4 + 2, xb)
                    pool.wait_ge(cosd, l * 2 + 1)
                    pool.wait_ge(dif, l * 2 + 1)
                    for part in ham[0]:
                        part()
                    pool.wait_ge(cosd, l * 2 + 2)
                    pool.wait_ge(dif, l * 2 + 2)
                    ham[1][0]()
                    ham[1][1]()
                    rsqrt(2, 0)
                    ham[1][2]()
                    add_bias(1, 0, N.hat, l * 4 + 3, xb2)
                    rsqrt(3, 1)
                    add_bias(1, 1, N.hat, l * 4 + 4, xb2)

            @block.vector
            def _(dve):
                norm_vector(dve, S, N0, xres, xl)
                dve.wait_ge(in_c, 64)
                dve.tensor_scalar(hneg[:], hart[:], -1.0, None, ALU.mult).then_inc(neg, 1)
                dve.wait_ge(cst, 10)
                dve.wait_ge(N0.hat, 2)
                dve.sem_inc(x2, 2)
                with dve.Fori(0, LL) as l:
                    def statistics(i, h):
                        for k in range(HB):
                            m = dve.bn_stats(S.stats[:, h, k], xl[:, HB * h + k])
                        dve.drain()
                        for k in range(HB):
                            m = dve.bn_aggr(S.mv[:, h, k], S.stats[:, h, k])
                        m.then_inc(N.mv, 1)

                    def normalise(i, h):
                        dve.wait_ge(N.mv, l * 4 + (i + 1))
                        dve.wait_ge(N.rstd, l * 4 + (i + 1))
                        for k in range(HB):
                            b = HB * h + k
                            m = dve.tensor_scalar(xhat[:, b], xl[:, b], S.mv[:, h, k, 0:1], S.rstd[:, h, k:k + 1],
                                                  ALU.subtract, ALU.mult)
                        m.then_inc(N.hat, 1)

                    def before(h):
                        dve.wait_ge(kk, l * 2 + (h + 1))
                        x = Q[:, h, 0].rearrange("p k n -> p (k n)")
                        y = Q[:, h, 3].rearrange("p k n -> p (k n)")
                        dve.scalar_tensor_tensor(out=y, in0=y, scalar=-2.0 * float(np.pi), in1=x,
                                                 op0=ALU.mult, op1=ALU.add).then_inc(red_, 1)
                        x = Q[:, h, 0].rearrange("p k (b n) -> p (k b) n", n=P)
                        y = Q[:, h, 1].rearrange("p k (b n) -> p (k b) n", n=P)
                        dve.tensor_tensor(y[:, :, 1:P], x[:, :, 1:P], x[:, :, 0:P - 1], ALU.subtract).then_inc(dif, 1)

                    def filtered(h):
                        dve.wait_ge(f_in, l * 2 + (h + 1))
                        dve.tensor_tensor(z[:, h].rearrange("p (b n) -> p b n", n=P),
                                          psum[:, 7].rearrange("p (b n) -> p b n", n=P),
                                          filt[:, None, :].broadcast_to([P, HB, P]), ALU.mult).then_inc(f_out, 1)

                    def residual(h, bank, got, biased, done, credit):
                        x = xl[:, HB * h:HB * h + HB]
                        dve.wait_ge(got, l * 2 + (h + 1))
                        dve.wait_ge(biased, l * 2 + (h + 1))
                        dve.tensor_tensor(x, psum[:, bank].rearrange("p (b d) -> p b d", b=HB), x, ALU.add).then_inc(done, 1)
                        dve.wait_ge(done, l * 2 + (h + 1 + credit))

                    for h in range(2):
                        statistics(h, h)
                    for h in range(2):
                        normalise(h, h)
                    ham = [hamilton(dve, h, 0, HALF - POOL_COLS, None, l * (2 * STEPS) + h * STEPS, hv) for h in range(2)]
                    before(0)
                    dve.wait_ge(cosd, l * 2 + 1)
                    dve.wait_ge(dif, l * 2 + 1)
                    for part in ham[0]:
                        part()
                    before(1)
                    dve.wait_ge(cosd, l * 2 + 2)
                    dve.wait_ge(dif, l * 2 + 2)
                    ham[1][0]()
                    filtered(0)
                    ham[1][1]()
                    residual(0, 7, p_in, xb, x1, 0)
                    statistics(2, 0)
                    ham[1][2]()
                    normalise(2, 0)
                    filtered(1)
                    residual(1, 7, p_in, xb, x1, 0)
                    statistics(3, 1)
                    normalise(3, 1)
                    for h in range(2):
                        residual(h, 5 + h, y_in, xb2, x2, 2)
                for h in range(2):
                    t = slice(HB * h, HB * h + HB)
                    m = dve.tensor_tensor(xres[:, t], xres[:, t], xl[:, t], ALU.add)
                m.then_inc(last, 1)

            @block.scalar
            def _(act):
                act.wait_ge(cst, 10)
                act.wait_ge(in_c, 64)

                def col(l, k):
                    return lcol[:, k:k + 1]

                with act.Fori(0, LL) as l:
                    act.drain()
                    act.activation(lcol[:], cols[:, bass.ds(l, 1), :].rearrange("p o k -> p (o k)"), ACT.Copy).then_inc(colr, 1)
                    act.wait_ge(colr, l + 1)
                    def take_norm(i, h, w, b):
                        act.wait_ge(N.turned, l * 4 + (i + 1))
                        act.activation(xnT[:, h], psum[:, 0], ACT.Identity, scale=col(l, w), bias=col(l, b)).then_inc(N.xT, 1)

                    def take_q(h, k):
                        act.wait_ge(q_in, l * (2 * NQ) + (NQ * h + k + 1))
                        act.activation(Q[:, h, 2 * (k // 3), k % 3], psum[:, 1 + k], ACT.Identity,
                                       bias=col(l, LQB + k)).then_inc(q_out, 1)

                    def turns(h):
                        x = Q[:, h, 0].rearrange("p k n -> p (k n)")
                        y = Q[:, h, 3].rearrange("p k n -> p (k n)")
                        act.wait_ge(q_out, l * (2 * NQ) + (NQ * h + 3))
                        act.activation(y, x, ACT.Identity, scale=float(0.5 / np.pi), bias=rnd[:, 0:1]).then_inc(rr, 1)
                        act.wait_ge(rr, l * 2 + (h + 1))
                        act.activation(y, y, ACT.Identity, bias=rnd[:, 1:2]).then_inc(kk, 1)

                    def cosine(h):
                        y = Q[:, h, 3].rearrange("p k n -> p (k n)")
                        act.wait_ge(red_, l * 2 + (h + 1))
                        act.activation(y, y, ACT.Abs).then_inc(absd, 1)
                        act.wait_ge(absd, l * 2 + (h + 1))
                        act.activation(y, y, ACT.Sin, scale=-1.0, bias=halfpi[:]).then_inc(cosd, 1)

                    for h in range(2):
                        take_norm(h, h, LW1, LB1)
                        if h == 0:
                            act.wait_ge(wc_in, l + 1)
                            act.activation(wc[:], psum[:, 7, 0:D], ACT.Copy).then_inc(wc_out, 1)
                        for k in range(3):
                            take_q(h, k)
                        turns(h)
                        for k in range(3, NQ):
                            take_q(h, k)
                        cosine(h)
                    for h in range(2):
                        take_norm(2 + h, h, LW2, LB2)
                        for f in range(LFB):
                            act.wait_ge(h_in, l * (2 * LFB) + (LFB * h + f + 1))
                            act.activation(gT[:, h, f], psum[:, 1 + f], ACT.Gelu, bias=col(l, LFC + f)).then_inc(g_out, 1)

            @block.tensor
            def _(pe):
                pe.wait_ge(in_c, 64)
                pe.wait_ge(neg, 1)
                with pe.Fori(0, LL) as l:
                    def turn(i, h):
                        pe.wait_ge(N.hat, l * 4 + (i + 1))
                        if i:
                            pe.wait_ge(N.xT, l * 4 + i)
                        else:
                            pe.wait_ge(N.xT, l * 4)
                        for k in range(HB):
                            m = pe.transpose(psum[:, 0, k * P:(k + 1) * P], xhat[:, HB * h + k], ident[:])
                        m.then_inc(N.turned, 1)

                    def project(h):
                        pe.wait_ge(N.xT, l * 4 + (h + 1))
                        if h == 0:
                            pe.wait_ge(in_q, l * 16 + 16)
                            pe.wait_ge(g_out, l * (2 * LFB))
                            pe.wait_ge(x2, l * 2 + 2)
                        for k in range(NQ):
                            if h:
                                pe.wait_ge(q_out, l * (2 * NQ) + (k + 1))
                            pe.matmul(psum[:, 1 + k], wqkv[:, k], xnT[:, h], start=True, stop=True).then_inc(q_in, 1)

                    def hartley(h):
                        pe.wait_ge(hv, l * (2 * STEPS) + STEPS * (h + 1))
                        pe.wait_ge(hp, l * (2 * STEPS) + STEPS * (h + 1))
                        if h:
                            pe.wait_ge(x1, l * 2 + 1)
                        else:
                            pe.wait_ge(wc_out, l + 1)
                        for k in range(4):
                            m = pe.matmul(psum[:, 7], (hneg if k else hart)[:], R[:, h, k], start=(k == 0), stop=(k == 3))
                        m.then_inc(f_in, 1)

                    def out(h):
                        pe.wait_ge(f_out, l * 2 + (h + 1))
                        for k in range(HB):
                            m = pe.matmul(psum[:, 7, k * P:(k + 1) * P], z[:, h, k * P:(k + 1) * P], wc[:], start=True, stop=True)
                        m.then_inc(p_in, 1)

                    def fc(h):
                        pe.wait_ge(N.xT, l * 4 + (h + 3))
                        pe.wait_ge(in_f, l * 16 + 16)
                        for f in range(LFB):
                            if h:
                                pe.wait_ge(g_out, l * (2 * LFB) + (f + 1))
                            else:
                                pe.wait_ge(q_out, l * (2 * NQ) + 2 * NQ)
                            pe.matmul(psum[:, 1 + f], wf[:, f * P:(f + 1) * P], xnT[:, h], start=True, stop=True).then_inc(h_in, 1)

                    def mproj(h):
                        pe.wait_ge(g_out, l * (2 * LFB) + LFB * (h + 1))
                        pe.wait_ge(in_m, l * 16 + 16)
                        for k in range(HB):
                            for f in range(LFB):
                                m = pe.matmul(psum[:, 5 + h, k * P:(k + 1) * P], gT[:, h, f, k * P:(k + 1) * P], wm[:, f],
                                              start=(f == 0), stop=(f == LFB - 1))
                        m.then_inc(y_in, 1)

                    pe.wait_ge(in_p, l * 16 + 16)
                    pe.wait_ge(x1, l * 2)
                    pe.matmul(psum[:, 7, 0:D], hart[:], wp[:], start=True, stop=True).then_inc(wc_in, 1)
                    turn(0, 0)
                    project(0)
                    turn(1, 1)
                    project(1)
                    hartley(0)
                    out(0)
                    hartley(1)
                    turn(2, 0)
                    fc(0)
                    out(1)
                    mproj(0)
                    turn(3, 1)
                    fc(1)
                    mproj(1)


YH, YD = 4, 32


def stage_cross1(nc, S, A):
    psum, ident, xres, xhat, xT = S.psum, S.ident, S.xres, S.xhat, S.xT
    with ExitStack() as c:
        sem = S.sem

        def sb(name, shape, dt=F32):
            return c.enter_context(nc.sbuf_tensor(name, shape, dt))

        w, cols, rows = sb("y_w", [P, 4, D]), sb("y_cols", [P, 2]), sb("y_rows", [P, 2, D])
        maski, keep, fill = sb("y_mask", [P, NB, P], I32), sb("y_keep", [P, NB, P]), sb("y_fill", [P, NB, P])
        qT, kT, vall = sb("y_qT", [P, NB * P]), sb("y_kT", [P, NB * P]), sb("y_v", [P, NB, D])
        qTp, kTp = sb("y_qTp", [P, 2, P]), sb("y_kTp", [P, 2, P])
        wt, e = sb("y_wt", [P, 2, YH, P]), sb("y_e", [P, 2, YH, P])
        mx, nmx, ssum, rs = (sb(f"y_{n}", [P, 2, YH]) for n in ("max", "nmax", "sum", "rsum"))
        vn, oT = sb("y_vn", [P, 2, D]), sb("y_oT", [P, 2, P])
        N = Norm(sem, "y")
        in_y, kps, kTr, vps, vr, qps, qTr, xb, kpr, fl = (sem(n) for n in (
            "y_in", "y_k_psum", "y_kT_made", "y_v_psum", "y_v_made", "y_q_psum", "y_qT_made", "y_x_bo", "y_keep_made",
            "y_fill_made"))
        with nc.Block() as block:
            @block.sync
            def _(sp):
                for k, n in enumerate("kvqo"):
                    load(sp, w[:, "qkvo".index(n)], A["y" + "w" + n], in_y)
                load(sp, cols[:, 0:1], A["ybq"], in_y)
                load(sp, cols[:, 1:2], A["ybk"], in_y)
                load(sp, rows[:, 0], A["ybv"].partition_broadcast(P), in_y)
                load(sp, rows[:, 1], A["ybo"].partition_broadcast(P), in_y)
                load(sp, maski[:], A["maskT"], in_y)

            @block.gpsimd
            def _(pool):
                norm_pool(pool, S, N, EPS_OUTER)
                pool.wait_ge(in_y, 16 * 9)
                pool.wait_ge(N.hat, 2)
                pool.tensor_tensor(xres[:], xres[:], rows[:, 1, None, :].broadcast_to([P, NB, D]), ALU.add).then_inc(xb, 1)

            @block.vector
            def _(dve):
                norm_vector(dve, S, N, xres, xhat)
                dve.wait_ge(in_y, 16 * 9)
                for h in range(2):
                    dve.wait_ge(vps, h + 1)
                    dve.tensor_tensor(vall[:, HB * h:HB * h + HB], psum[:, 2 + h].rearrange("p (b d) -> p b d", b=HB),
                                      rows[:, 0, None, :].broadcast_to([P, HB, D]), ALU.add).then_inc(vr, 1)
                dve.tensor_scalar(keep[:], maski[:], 0.0, None, ALU.not_equal).then_inc(kpr, 1)
                dve.wait_ge(kpr, 1)
                dve.tensor_scalar(fill[:], keep[:], -1.0, 1e9, ALU.add, ALU.mult).then_inc(fl, 1)

            @block.tensor
            def _(pe):
                pe.wait_ge(in_y, 16 * 9)
                for h in range(2):
                    pe.matmul(psum[:, h], w[:, 1], S.ctxT[:, h * HALF:(h + 1) * HALF], start=True, stop=True).then_inc(kps, 1)
                for h in range(2):
                    for i in range(HB):
                        b = HB * h + i
                        m = pe.matmul(psum[:, 2 + h, i * P:(i + 1) * P], S.ctxT[:, b * P:(b + 1) * P], w[:, 2], start=True, stop=True)
                    m.then_inc(vps, 1)
                norm_tensor(pe, S, N, 4)
                for h in range(2):
                    pe.wait_ge(N.xT, h + 1)
                    pe.matmul(psum[:, 6 + h], w[:, 0], xT[:, h * HALF:(h + 1) * HALF], start=True, stop=True).then_inc(qps, 1)

            @block.scalar
            def _(act):
                act.wait_ge(in_y, 16 * 9)
                for h in range(2):
                    act.wait_ge(kps, h + 1)
                    act.activation(kT[:, h * HALF:(h + 1) * HALF], psum[:, h], ACT.Identity, bias=cols[:, 1:2]).then_inc(kTr, 1)
                norm_scalar(act, S, N, 4, xT)
                for h in range(2):
                    act.wait_ge(qps, h + 1)
                    act.activation(qT[:, h * HALF:(h + 1) * HALF], psum[:, 6 + h], ACT.Identity, bias=cols[:, 0:1]).then_inc(qTr, 1)

        kpc, qpc, s_in, s_out, flr, mxr, nmr, ex, rsr, vnr, a_in, a_out, y_in, y_out = (sem(n) for n in (
            "yl_kT", "yl_qT", "yl_s_psum", "yl_kept", "yl_filled", "yl_max", "yl_nmax", "yl_e", "yl_rsum", "yl_vn",
            "yl_a_psum", "yl_oT", "yl_y_psum", "yl_x"))
        with nc.Block() as block:
            @block.gpsimd
            def _(pool):
                with pool.Fori(0, NB // 2) as i:
                    b = i * 2
                    pool.wait_ge(s_in, b)
                    for j in range(2):
                        pool.tensor_copy(kTp[:, j], kT[:, bass.ds((b + j) * P, P)]).then_inc(kpc, 1)
                        pool.tensor_copy(qTp[:, j], qT[:, bass.ds((b + j) * P, P)]).then_inc(qpc, 1)

            @block.scalar
            def _(act):
                with act.Fori(0, NB // 2) as i:
                    b = i * 2
                    for j in range(2):
                        act.wait_ge(nmr, b + (j + 1))
                        for h in range(YH):
                            m = act.activation(e[:, j, h], wt[:, j, h], ACT.Exp, bias=nmx[:, j, h:h + 1], accum_out=ssum[:, j, h:h + 1])
                        m.then_inc(ex, 1)
                    for j in range(2):
                        act.wait_ge(a_in, b + (j + 1))
                        act.activation(oT[:, j], psum[:, 4 + 2 * j, 0:P], ACT.Copy).then_inc(a_out, 1)

            @block.vector
            def _(dve):
                with dve.Fori(0, NB // 2) as i:
                    b = i * 2
                    for j in range(2):
                        dve.wait_ge(s_in, b + (j + 1))
                        mask = [t[:, bass.ds(b + j, 1), :].broadcast_to([P, YH, P]) for t in (keep, fill)]
                        dve.scalar_tensor_tensor(out=wt[:, j], in0=psum[:, 0:YH, 0:P], scalar=float(np.float32(YD) ** np.float32(-0.5)),
                                                 in1=mask[0], op0=ALU.mult, op1=ALU.mult).then_inc(s_out, 1)
                        dve.wait_ge(s_out, b + (j + 1))
                        dve.tensor_tensor(wt[:, j], wt[:, j], mask[1], ALU.add).then_inc(flr, 1)
                        dve.wait_ge(flr, b + (j + 1))
                        dve.tensor_reduce(mx[:, j], wt[:, j], AX.X, ALU.max).then_inc(mxr, 1)
                        dve.wait_ge(mxr, b + (j + 1))
                        dve.tensor_scalar(nmx[:, j], mx[:, j], -1.0, None, ALU.mult).then_inc(nmr, 1)
                    for j in range(2):
                        dve.wait_ge(ex, b + (j + 1))
                        dve.reciprocal(rs[:, j], ssum[:, j]).then_inc(rsr, 1)
                        dve.wait_ge(rsr, b + (j + 1))
                        dve.tensor_tensor(vn[:, j].rearrange("p (h d) -> p h d", h=YH),
                                          vall[:, bass.ds(b + j, 1), :].rearrange("p o (h d) -> p (o h) d", h=YH),
                                          rs[:, j, :, None].broadcast_to([P, YH, YD]), ALU.mult).then_inc(vnr, 1)
                    for j in range(2):
                        xb_ = xres[:, bass.ds(b + j, 1), :].rearrange("p o d -> p (o d)")
                        dve.wait_ge(y_in, b + (j + 1))
                        dve.tensor_tensor(xb_, psum[:, 5 + 2 * j, 0:D], xb_, ALU.add).then_inc(y_out, 1)

            @block.tensor
            def _(pe):
                with pe.Fori(0, NB // 2) as i:
                    b = i * 2
                    for j in range(2):
                        pe.wait_ge(kpc, b + (j + 1))
                        pe.wait_ge(qpc, b + (j + 1))
                        pe.wait_ge(s_out, b + j)
                        for h in range(YH):
                            rows_ = slice(YD * h, YD * h + YD)
                            m = pe.matmul(psum[:, h, 0:P], kTp[rows_, j], qTp[rows_, j], start=True, stop=True)
                        m.then_inc(s_in, 1)
                    for j in range(2):
                        pe.wait_ge(vnr, b + (j + 1))
                        pe.wait_ge(a_out, b)
                        for h in range(YH):
                            m = pe.matmul(psum[YD * h:YD * h + YD, 4 + 2 * j, 0:P], vn[:, j, YD * h:YD * h + YD], e[:, j, h],
                                          start=True, stop=True)
                        m.then_inc(a_in, 1)
                    for j in range(2):
                        pe.wait_ge(a_out, b + (j + 1))
                        pe.wait_ge(y_out, b)
                        pe.matmul(psum[:, 5 + 2 * j, 0:D], oT[:, j], w[:, 3], start=True, stop=True).then_inc(y_in, 1)


RE, CAP = 8, 100


def stage_router(nc, S, A):
    psum, ident, xres, xhat, xT = S.psum, S.ident, S.xres, S.xhat, S.xT
    with ExitStack() as c:
        sem = S.sem

        def sb(name, shape, dt=F32):
            return c.enter_context(nc.sbuf_tensor(name, shape, dt))

        wg, we, be = sb("r_wg", [P, RE]), sb("r_we", [P, D]), sb("r_be", [P, D])
        tri, rank = sb("r_tri", [P, P]), sb("r_rank", [P, RE])
        R = sb("r_r", [P, 6, NB, RE])
        r1 = sb("r_1", [P, 6, NB])
        y = sb("r_y", [P, NB, D])
        N = Norm(sem, "r")
        in_r, lg, v, ae, cm, e_in, yr, xr, done = (sem(n) for n in (
            "r_in", "r_logits", "r_chain", "r_exp", "r_count_psum", "r_e_psum", "r_expert", "r_x", "r_stored"))
        with nc.Block() as block:
            @block.sync
            def _(sp):
                load(sp, wg[:], A["rwg"], in_r)
                load(sp, we[:], A["rwe"], in_r)
                load(sp, be[:], A["rbe"].partition_broadcast(P), in_r)
                load(sp, tri[:], A["upto"], in_r)
                load(sp, rank[:], A["rank"].partition_broadcast(P), in_r)
                for h in range(2):
                    t = slice(HB * h, HB * h + HB)
                    sp.wait_ge(xr, h + 1)
                    sp.dma_start(A["out"][:, t], xres[:, t]).then_inc(done, 16)
                sp.wait_ge(done, 32)

            @block.gpsimd
            def _(pool):
                norm_pool(pool, S, N, EPS_OUTER)

            @block.vector
            def _(dve):
                norm_vector(dve, S, N, xres, xhat)
                count = [0]

                def step(m):
                    count[0] += 1
                    m.then_inc(v, 1)
                    dve.wait_ge(v, count[0])

                def bc(a):
                    return a[:, :, None].broadcast_to([P, NB, RE])

                dve.wait_ge(in_r, 80)
                dve.wait_ge(lg, 1)
                lgt = psum[:, 2, 0:NB * RE].rearrange("p (b e) -> p b e", b=NB)
                step(dve.tensor_reduce(r1[:, 0], lgt, AX.X, ALU.max))
                step(dve.tensor_tensor(R[:, 0], lgt, bc(r1[:, 0]), ALU.subtract))
                dve.wait_ge(ae, 1)
                step(dve.tensor_reduce(r1[:, 1], R[:, 0], AX.X, ALU.add))
                step(dve.reciprocal(r1[:, 2], r1[:, 1]))
                step(dve.tensor_tensor(R[:, 1], R[:, 0], bc(r1[:, 2]), ALU.mult))
                step(dve.tensor_reduce(r1[:, 3], R[:, 1], AX.X, ALU.max))
                step(dve.tensor_tensor(R[:, 2], R[:, 1], bc(r1[:, 3]), ALU.is_equal))
                step(dve.tensor_tensor(R[:, 2], R[:, 2], rank[:, None, :].broadcast_to([P, NB, RE]), ALU.mult))
                step(dve.tensor_reduce(r1[:, 4], R[:, 2], AX.X, ALU.max))
                step(dve.tensor_tensor(R[:, 3], R[:, 2], bc(r1[:, 4]), ALU.is_equal))
                dve.wait_ge(cm, 1)
                cnt = psum[:, 3, 0:NB * RE].rearrange("p (b e) -> p b e", b=NB)
                step(dve.tensor_scalar(R[:, 4], cnt, CAP + 0.5, None, ALU.is_lt))
                step(dve.tensor_tensor(R[:, 5], R[:, 4], R[:, 3], ALU.mult))
                step(dve.tensor_reduce(r1[:, 5], R[:, 5], AX.X, ALU.add))
                step(dve.tensor_tensor(r1[:, 4], r1[:, 5], r1[:, 3], ALU.mult))
                for h in range(2):
                    t = slice(HB * h, HB * h + HB)
                    dve.wait_ge(e_in, h + 1)
                    dve.tensor_tensor(y[:, t], psum[:, 4 + h].rearrange("p (b d) -> p b d", b=HB),
                                      be[:, None, :].broadcast_to([P, HB, D]), ALU.add).then_inc(yr, 1)
                    dve.wait_ge(yr, h + 1)
                    for i in range(HB):
                        b = HB * h + i
                        m = dve.scalar_tensor_tensor(out=xres[:, b], in0=y[:, b], scalar=r1[:, 4, b:b + 1], in1=xres[:, b],
                                                     op0=ALU.mult, op1=ALU.add)
                    m.then_inc(xr, 1)

            @block.scalar
            def _(act):
                norm_scalar(act, S, N, 0, xT)
                act.wait_ge(v, 2)
                act.activation(R[:, 0], R[:, 0], ACT.Exp).then_inc(ae, 1)

            @block.tensor
            def _(pe):
                norm_tensor(pe, S, N, 0)
                pe.wait_ge(in_r, 80)
                pe.wait_ge(N.xT, 2)
                for b in range(NB):
                    m = pe.matmul(psum[:, 2, b * RE:(b + 1) * RE], xT[:, b * P:(b + 1) * P], wg[:], start=True, stop=True)
                m.then_inc(lg, 1)
                for h in range(2):
                    for i in range(HB):
                        b = HB * h + i
                        m = pe.matmul(psum[:, 4 + h, i * P:(i + 1) * P], xT[:, b * P:(b + 1) * P], we[:], start=True, stop=True)
                    m.then_inc(e_in, 1)
                pe.wait_ge(v, 10)
                hot = R[:, 3].rearrange("p b e -> p (b e)")
                pe.matmul(psum[:, 3, 0:NB * RE], tri[:], hot, start=True, stop=False, skip_group_check=True)
                for k in range(1, NB):
                    m = pe.matmul(psum[:, 3, k * RE:NB * RE], S.ones[:], hot[:, 0:(NB - k) * RE], start=False,
                                  stop=(k == NB - 1), skip_group_check=True)
                m.then_inc(cm, 1)


def spectral_tables():
    h, d = np.divmod(np.arange(P), QD)
    turns = np.outer(h, h) / QH + np.outer(d, d) / QD
    hartley = np.cos(2 * np.pi * turns) + np.sin(2 * np.pi * turns)
    fs, fh, fd = np.fft.fftfreq(P), np.fft.fftfreq(QH)[h], np.fft.fftfreq(QD)[d]
    km = np.sqrt(fs[None, :] ** 2 + fh[:, None] ** 2 + fd[:, None] ** 2 + 1e-10)
    real = np.cos(np.arctan(np.log(km + 1e-10)))
    s = np.arange(P)
    lam, t = s / P, s * 0.1
    modulation = np.sin(t + lam) * np.cos(t - 2.0 * lam + 0.5 * lam ** 2)
    return hartley.astype(np.float32), (real * (1.0 + 0.1 * modulation) / P).astype(np.float32)


def program(nc, A):
    S = Shared()
    with ExitStack() as ctx:

        def sem(name):
            return ctx.enter_context(nc.semaphore(name))

        def sb(name, shape, dt=F32):
            return ctx.enter_context(nc.sbuf_tensor(name, shape, dt))

        S.sem = lambda name: nc.alloc_semaphore(name=name)
        S.psum = ctx.enter_context(nc.psum_tensor("psum", [P, 8, 512], F32))
        S.xres = sb("xres", [P, NB, D])
        S.xhat = sb("xhat", [P, NB, D])
        S.xT = sb("xT", [P, NB * P])
        S.ident = sb("ident", [P, P])
        S.ones = sb("ones", [P, P])
        S.nhalf = sb("nhalf", [P, NB])
        S.eps = sb("eps", [P, NB])
        S.stats = sb("stats", [P, 2, HB, 6])
        S.mv = sb("mv", [P, 2, HB, 2])
        S.rstd = sb("rstd", [P, 2, HB])
        S.ctxT = sb("ctxT", [P, NB * P])
        S.x0w, S.x0cols, S.x0rows = sb("x0w", [P, 4, D]), sb("x0cols", [P, 2]), sb("x0rows", [P, 2, D])
        S.headmask = sb("headmask", [P, XH])
        S.in_x0 = sem("in_x0")
        for stage in (stage_performer, stage_cross0, stage_moe, stage_layers, stage_cross1, stage_router):
            with nc.cleanup_on_exit():
                stage(nc, S, A)


def lay_out(i):
    c = np.ascontiguousarray
    wq, wk = i["L0_attn_Wq"], i["L0_attn_Wk"]
    r = {
        "x": c(i["x"].transpose(1, 0, 2)),
        "ident": np.eye(P, dtype=np.float32),
        "pwq": c(wq.reshape(D, -1)), "pwk": c(wk.reshape(D, -1)), "pwv": c(i["L0_attn_Wv"].reshape(D, -1)),
        "pwqT": c(wq.reshape(D, NPAIR, P).transpose(2, 1, 0)), "pwkT": c(wk.reshape(D, NPAIR, P).transpose(2, 1, 0)),
        "projT": c(i["L0_attn_proj"].T),
        "pwo": c(i["L0_attn_Wo"].reshape(NPAIR, P, D).transpose(1, 0, 2)),
        "pw1": i["L0_attn_W1"], "pw2": c(i["L0_attn_W2"].reshape(PFB, P, D).transpose(1, 0, 2)),
        "pb1": c(i["L0_attn_b1"].reshape(PFB, P).T), "pb2": i["L0_attn_b2"],
        "pln1g": i["L0_attn_ln1_g"], "pln1b": i["L0_attn_ln1_b"],
        "pln2g": i["L0_attn_ln2_g"], "pln2b": i["L0_attn_ln2_b"],
        "ctxT": c(i["ctx_1024"].transpose(2, 0, 1).reshape(D, -1)),
        "headmask": c(np.repeat(np.eye(XH, dtype=np.float32), XD, 0)),
        "router": i["L0_ffn_router_kernel_DE"],
        "rank": np.arange(ME, 0, -1, dtype=np.float32),
        "mwg": c(i["L0_ffn_kernel_gating_EDF"].transpose(1, 0, 2)), "mwu": c(i["L0_ffn_kernel_up_EDF"].transpose(1, 0, 2)),
        "mwd": c(i["L0_ffn_kernel_down_EFD"].reshape(ME * MFB, P, D).transpose(1, 0, 2)),
    }
    aw = i["L1_attn_attn_w"].reshape(LL, D, QH, 3, QD).transpose(1, 0, 3, 2, 4)
    ab = i["L1_attn_attn_b"].reshape(LL, QH, 3, QD).transpose(0, 2, 1, 3)
    r["lwqkv"] = c(np.concatenate([aw, np.roll(aw, 1, axis=3)], 2).reshape(D, LL, -1))
    ab6 = np.concatenate([ab, np.roll(ab, 1, axis=2)], 1).reshape(LL, NQ, D)
    r["lwp"] = c(i["L1_attn_aproj_w"].transpose(1, 0, 2))
    r["lwf"] = c(i["L1_attn_fc_w"].transpose(1, 0, 2))
    r["lwm"] = c(i["L1_attn_mproj_w"].reshape(LL, LFB, P, D).transpose(2, 0, 1, 3).reshape(P, LL, -1))
    ln = np.stack([i["L1_attn_" + n] for n in ("ln1_w", "ln1_b", "ln2_w", "ln2_b")], 1)
    r["lcols"] = c(np.concatenate([ln, ab6, i["L1_attn_fc_b"].reshape(LL, LFB, P)], 1).transpose(2, 0, 1))
    r["lrows"] = c(np.stack([i["L1_attn_aproj_b"], i["L1_attn_mproj_b"]], 1).reshape(-1))
    r["hartley"], r["filter"] = spectral_tables()
    r["maskT"] = c(i["mask_Bx1xSxS2_ik1"][:, 0].transpose(2, 0, 1))
    for n in "qkvo":
        r["yw" + n] = c(i["L1_xattn_W" + n].T)
        b = i["L1_xattn_b" + n]
        r["yb" + n] = b.reshape(D, 1) if n in "qk" else b
    r["rwg"], r["rwe"], r["rbe"] = i["L1_ffn_w_gate"], i["L1_ffn_w_expert"], i["L1_ffn_b_expert"]
    r["upto"] = np.triu(np.ones((P, P), np.float32))
    for n in "qkvo":
        r["x0w" + n] = c(i["L0_xattn_W" + n].T)
    for n in "qk":
        r["x0b" + n] = i["L0_xattn_b" + n].reshape(D, 1)
    for n in "vo":
        r["x0b" + n] = i["L0_xattn_b" + n]
    return r


def kernel(**inputs):
    import concourse.bacc as bacc
    from concourse.bass_utils import run_bass_kernel_spmd

    nc = bacc.Bacc("TRN2", target_bir_lowering=False, num_devices=1)
    arrays, A = {}, {}
    for name, a in lay_out({k: np.asarray(v) for k, v in inputs.items()}).items():
        a = np.ascontiguousarray(a)
        arrays[f"in_{name}_dram"] = a
        A[name] = nc.dram_tensor(f"in_{name}_dram", a.shape, mybir.dt.from_np(a.dtype), kind="ExternalInput").ap()
    A["out"] = nc.dram_tensor("out_0_dram", (P, NB, D), F32, kind="ExternalOutput").ap()
    program(nc, A)
    r = run_bass_kernel_spmd(nc, [arrays], core_ids=[0])
    return np.ascontiguousarray(r.results[0]["out_0_dram"].transpose(1, 0, 2))
```

```python
from contextlib import ExitStack

import numpy as np

import concourse.bass as bass
from concourse import mybir

F32 = mybir.dt.float32
I32 = mybir.dt.int32
ACT = mybir.ActivationFunctionType
ALU = mybir.AluOpType
AX = mybir.AxisListType

P = 128
NB = 8
HB = NB // 2
D = 128
HALF = HB * P
EPS_OUTER = 1e-5

PH, PD, PM = 16, 64, 64
NPAIR = PH // 2
VA = PD + 1
PAIR = 2 * VA
DN = float(PD) ** -0.25
EPS_KERN = 1e-6
PF = 512
PFB = PF // P


def load(eng, dst, src, sem):
    eng.dma_start(dst, src).then_inc(sem, 16)


def one(n):
    return slice(n, n + 1) if isinstance(n, int) else bass.ds(n, 1)


def batches(eng, slot):
    slot(0, 0)
    with eng.Fori(0, NB // 2 - 1) as i:
        slot(i * 2 + 1, 1)
        slot(i * 2 + 2, 0)
    slot(NB - 1, 1)
    slot(NB, 0)


def parts(n):
    return (n < NB - 1, n < NB, n > 0) if isinstance(n, int) else (True, True, True)


class Shared:
    pass



class Norm:

    def __init__(self, sem, name):
        self.stats, self.mv, self.eps, self.rstd, self.hat, self.turned, self.xT = (
            sem(f"{name}_{n}") for n in ("stats", "mv", "var_eps", "rstd", "xhat", "turned", "xT"))


def norm_vector(dve, S, N, src, dst, n0=0):
    for h in range(2):
        for i in range(HB):
            m = dve.bn_stats(S.stats[:, h, i], src[:, HB * h + i])
        m.then_inc(N.stats, 1)
        dve.wait_ge(N.stats, n0 + h + 1)
        for i in range(HB):
            m = dve.bn_aggr(S.mv[:, h, i], S.stats[:, h, i])
        m.then_inc(N.mv, 1)
    for h in range(2):
        dve.wait_ge(N.mv, n0 + h + 1)
        dve.wait_ge(N.rstd, n0 + h + 1)
        for i in range(HB):
            b = HB * h + i
            m = dve.tensor_scalar(dst[:, b], src[:, b], S.mv[:, h, i, 0:1], S.rstd[:, h, i:i + 1],
                                  ALU.subtract, ALU.mult)
        m.then_inc(N.hat, 1)


def norm_pool(pool, S, N, eps, n0=0):
    for h in range(2):
        pool.wait_ge(N.mv, n0 + h + 1)
        pool.tensor_scalar(S.rstd[:, h], S.mv[:, h, :, 1], eps, 1.0, ALU.add, ALU.mult).then_inc(N.eps, 1)
        pool.wait_ge(N.eps, n0 + h + 1)
        pool.tensor_tensor(S.rstd[:, h], S.rstd[:, h], S.nhalf[:, 0:HB], ALU.pow).then_inc(N.rstd, 1)


def norm_tensor(pe, S, N, bank):
    for h in range(2):
        pe.wait_ge(N.hat, h + 1)
        for i in range(HB):
            m = pe.transpose(S.psum[:, bank + h, i * P:(i + 1) * P], S.xhat[:, HB * h + i], S.ident[:])
        m.then_inc(N.turned, 1)


def norm_scalar(act, S, N, bank, dst):
    for h in range(2):
        act.wait_ge(N.turned, h + 1)
        act.activation(dst[:, h * HALF:(h + 1) * HALF], S.psum[:, bank + h], ACT.Copy).then_inc(N.xT, 1)


def stage_performer(nc, S, A):
    with ExitStack() as ctx:
        def sb(name, shape, dt=F32):
            return ctx.enter_context(nc.sbuf_tensor(name, shape, dt))

        sem = S.sem
        psum = S.psum
        xres, xhat, xT, ident, mv, stats = S.xres, S.xhat, S.xT, S.ident, S.mv, S.stats

        wq, wk, wv = (sb(f"p_w{n}", [P, PH * PD]) for n in "qkv")
        wo = sb("p_wo", [P, NPAIR, D])
        w1, w2 = sb("p_w1", [P, PF]), sb("p_w2", [P, PFB, D])
        b1 = sb("p_b1", [P, PFB])
        rows = sb("p_rows", [P, 5, D])
        proj2 = sb("p_proj2", [P, P])
        wdq, wdk = sb("p_wdq", [P, PH * PM]), sb("p_wdk", [P, PH * PM])
        xTp = sb("p_xTp", [P, 2, P])
        vaug = sb("p_vaug", [P, NB, PH, VA])
        ddk = sb("p_ddk", [P, NB, PH * PM])
        sq = sb("p_sq", [P, 2, PH * PD])
        diag = sb("p_diag", [P, 2, PH])
        kmax = sb("p_kmax", [P, NB])
        kmax1 = sb("p_kmax1", [P, 1])
        kmaxn = sb("p_kmaxn", [1, 1])
        nkmax = sb("p_nkmax", [P, 1])
        epsk = sb("p_epsk", [P, 1])
        ones = S.ones

        in_x, in_id, in_row = sem("in_x"), sem("in_ident"), sem("in_rows")
        in_wk, in_wdk, in_wv, in_wq, in_wo, in_ffn = (sem(n) for n in (
            "in_wk", "in_wdk", "in_wv", "in_wq", "in_wo", "in_ffn"))
        with ExitStack() as c2:
            wqT = c2.enter_context(nc.sbuf_tensor("p_wqT", [P, NPAIR, D], F32))
            wkT = c2.enter_context(nc.sbuf_tensor("p_wkT", [P, NPAIR, D], F32))
            cst, dstat, dmv, rstd, hat, tp, xTr = (sem(n) for n in (
                "a_const", "a_stats", "a_mv", "a_rstd", "a_hat", "a_tp", "a_xT"))
            wdp, wde, xtp, k_in, dk_in, v_in, sq_ok, v_ok, red_ok, dk_ok, pchain = (sem(n) for n in (
                "a_wd_psum", "a_wd", "a_xTp", "a_k_psum", "a_dk_psum", "a_v_psum", "a_sq", "a_v", "a_red",
                "a_dk_used", "a_pool"))
            m1, m2, m3, m4, m5 = (sem(n) for n in ("a_max1", "a_maxT", "a_max2", "a_maxbc", "a_max3"))
            block = c2.enter_context(nc.Block())

            @block.sync
            def _(sp):
                load(sp, xres[:], A["x"], in_x)
                load(sp, ident[:], A["ident"], in_id)
                load(sp, wkT[:], A["pwkT"], in_wdk)
                sp.wait_ge(cst, 1)
                load(sp, proj2[0:PD, 0:PM], A["projT"], in_wdk)
                load(sp, proj2[PD:P, PM:P], A["projT"], in_wdk)
                load(sp, wk[:], A["pwk"], in_wk)
                load(sp, wv[:], A["pwv"], in_wv)
                load(sp, wqT[:], A["pwqT"], in_wq)
                load(sp, wq[:], A["pwq"], in_wq)
                load(sp, wo[:], A["pwo"], in_wo)
                load(sp, w1[:], A["pw1"], in_ffn)
                load(sp, w2[:], A["pw2"], in_ffn)
                load(sp, b1[:], A["pb1"], in_ffn)
                load(sp, S.ctxT[:], A["ctxT"], S.in_x0)
                for i, n in enumerate("qkvo"):
                    load(sp, S.x0w[:, i], A["x0w" + n], S.in_x0)
                load(sp, S.headmask[:], A["headmask"], S.in_x0)
                load(sp, S.x0cols[:, 0:1], A["x0bq"], S.in_x0)
                load(sp, S.x0cols[:, 1:2], A["x0bk"], S.in_x0)
                load(sp, S.x0rows[:, 0], A["x0bv"].partition_broadcast(P), S.in_x0)
                load(sp, S.x0rows[:, 1], A["x0bo"].partition_broadcast(P), S.in_x0)
                for i, n in enumerate(("pln1g", "pln1b", "pln2g", "pln2b", "pb2")):
                    load(sp, rows[:, i, :], A[n].partition_broadcast(P), in_row)

            @block.gpsimd
            def _(pool):
                pool.memset(proj2[:], 0.0).then_inc(cst, 1)
                pool.memset(ones[:], 1.0).then_inc(pchain, 1)
                pool.memset(S.nhalf[:], -0.5).then_inc(pchain, 1)
                pool.memset(epsk[:], EPS_KERN).then_inc(pchain, 1)
                pool.memset(vaug[:, :, :, PD:VA], 1.0).then_inc(pchain, 1)
                pool.wait_ge(pchain, 4)
                for h in range(2):
                    pool.wait_ge(dmv, h + 1)
                    pool.tensor_scalar(S.rstd[:, h], mv[:, h, :, 1], EPS_OUTER, None, ALU.add).then_inc(pchain, 1)
                    pool.wait_ge(pchain, 5 + h)
                    pool.tensor_tensor(S.rstd[:, h], S.rstd[:, h], S.nhalf[:, 0:HB], ALU.pow).then_inc(rstd, 1)
                with pool.Fori(0, NB // 2) as i:
                    b = i * 2
                    for j in range(2):
                        pool.wait_ge(xTr, 2)
                        pool.wait_ge(v_in, b + (j + 1))
                        pool.tensor_copy(xTp[:, j], xT[:, bass.ds((b + j) * P, P)]).then_inc(xtp, 1)

            @block.vector
            def _(dve):
                dve.wait_ge(in_x, 16)
                for h in range(2):
                    for i in range(HB):
                        dve.bn_stats(stats[:, h, i], xres[:, HB * h + i]).then_inc(dstat, 1)
                    dve.wait_ge(dstat, HB * (h + 1))
                    for i in range(HB):
                        m = dve.bn_aggr(mv[:, h, i], stats[:, h, i])
                    m.then_inc(dmv, 1)
                for h in range(2):
                    dve.wait_ge(dmv, h + 1)
                    dve.wait_ge(rstd, h + 1)
                    for i in range(HB):
                        b = HB * h + i
                        m = dve.tensor_scalar(xhat[:, b], xres[:, b], mv[:, h, i, 0:1], S.rstd[:, h, i:i + 1],
                                              ALU.subtract, ALU.mult)
                    m.then_inc(hat, 1)
                dve.sem_inc(red_ok, 2)
                dve.sem_inc(dk_ok, 1)
                with dve.Fori(0, NB // 2) as i:
                    b = i * 2
                    for j in range(2):
                        dve.wait_ge(sq_ok, b + (j + 2))
                        dve.wait_ge(dk_ok, b + (j + 1))
                        dve.tensor_reduce(diag[:, j], sq[:, j].rearrange("p (h d) -> p h d", h=PH), AX.X, ALU.add
                                          ).then_inc(red_ok, 1)
                        dve.wait_ge(dk_in, b + (j + 1))
                        dve.tensor_reduce(kmax[:, bass.ds(b + j, 1)], psum[:, 2:4, :].rearrange("p a n -> p (a n)"), AX.X, ALU.max)
                        dve.wait_ge(red_ok, b + (j + 3))
                        dve.tensor_tensor(ddk[:, bass.ds(b + j, 1), :].rearrange("p o (h m) -> p (o h) m", h=PH),
                                          psum[:, 2:4, :].rearrange("p a (h m) -> p (a h) m", m=PM),
                                          diag[:, j, :, None].broadcast_to([P, PH, PM]),
                                          ALU.subtract).then_inc(dk_ok, 1)
                dve.wait_ge(dk_ok, NB + 1)
                dve.tensor_reduce(kmax1[:], kmax[:], AX.X, ALU.max).then_inc(m1, 1)
                dve.wait_ge(m2, 1)
                dve.tensor_reduce(kmaxn[:], psum[0:1, 6, 0:P], AX.X, ALU.max).then_inc(m3, 1)
                dve.wait_ge(m4, 1)
                dve.tensor_scalar(nkmax[:], psum[:, 7, 0:1], -1.0, None, ALU.mult).then_inc(m5, 1)

            @block.tensor
            def _(pe):
                pe.wait_ge(in_id, 16)
                for h in range(2):
                    pe.wait_ge(hat, h + 1)
                    for i in range(HB):
                        m = pe.transpose(psum[:, 6 + h, i * P:(i + 1) * P], xhat[:, HB * h + i], ident[:])
                    m.then_inc(tp, 1)
                pe.wait_ge(in_wdk, 48)
                for n, w in enumerate((wkT, wqT)):
                    if n:
                        pe.wait_ge(in_wq, 32)
                        pe.wait_ge(wde, 1)
                    for q in range(NPAIR):
                        m = pe.matmul(psum[:, q // 4, (q % 4) * P:(q % 4 + 1) * P], w[:, q], proj2[:], start=True, stop=True)
                    m.then_inc(wdp, 1)
                pe.wait_ge(in_wk, 16)
                pe.wait_ge(in_wv, 16)
                pe.wait_ge(wde, 2)
                pe.sem_inc(v_in, 2)
                pe.sem_inc(sq_ok, 1)
                pe.sem_inc(v_ok, 1)
                with pe.Fori(0, NB // 2) as i:
                    b = i * 2
                    for j in range(2):
                        pe.wait_ge(xtp, b + (j + 1))
                        for (w, bank, done, used) in ((wk, 0, k_in, sq_ok), (wdk, 2, dk_in, dk_ok), (wv, 4, v_in, v_ok)):
                            pe.wait_ge(used, b + (j + 1))
                            for n in range(2):
                                m = pe.matmul(psum[:, bank + n, :], xTp[:, j], w[:, n * 512:(n + 1) * 512], start=True, stop=True)
                            m.then_inc(done, 1)
                pe.wait_ge(m1, 1)
                pe.transpose(psum[0:1, 6, 0:P], kmax1[:], ident[:]).then_inc(m2, 1)
                pe.wait_ge(m3, 1)
                pe.matmul(psum[:, 7, 0:1], ones[0:1, :], kmaxn[:], start=True, stop=True).then_inc(m4, 1)

            @block.scalar
            def _(act):
                for h in range(2):
                    act.wait_ge(tp, h + 1)
                    act.activation(xT[:, h * HALF:(h + 1) * HALF], psum[:, 6 + h], ACT.Copy).then_inc(xTr, 1)
                for n, w in enumerate((wdk, wdq)):
                    act.wait_ge(wdp, n + 1)
                    act.activation(w[:], psum[:, 0:2].rearrange("p a n -> p (a n)"), ACT.Copy, scale=DN).then_inc(wde, 1)
                with act.Fori(0, NB // 2) as i:
                    b = i * 2
                    for j in range(2):
                        act.wait_ge(k_in, b + (j + 1))
                        act.wait_ge(red_ok, b + (j + 1))
                        act.activation(sq[:, j], psum[:, 0:2].rearrange("p a n -> p (a n)"), ACT.Square,
                                       scale=DN / 2 ** 0.5).then_inc(sq_ok, 1)
                        act.wait_ge(v_in, b + (j + 3))
                        act.activation(vaug[:, bass.ds(b + j, 1), :, 0:PD].rearrange("p o h d -> p (o h) d"),
                                       psum[:, 4:6].rearrange("p a (h d) -> p (a h) d", d=PD),
                                       ACT.Copy).then_inc(v_ok, 1)
        kept = dict(wq=wq, wdq=wdq, wo=wo, w1=w1, w2=w2, b1=b1, rows=rows, xTp=xTp, vaug=vaug, ddk=ddk, sq=sq, diag=diag,
                    nkmax=nkmax, epsk=epsk, in_wq=in_wq, in_wo=in_wo, in_ffn=in_ffn, in_row=in_row)
        performer_queries(nc, S, ctx, kept)


def performer_queries(nc, S, ctx, L):
    sem, psum, xres, xhat, xT, ident = S.sem, S.psum, S.xres, S.xhat, S.xT, S.ident
    wq, wdq, wo, w1, w2, b1, rows = (L[n] for n in ("wq", "wdq", "wo", "w1", "w2", "b1", "rows"))
    xTp, vaug, ddk, sq, diag, nkmax, epsk = (L[n] for n in ("xTp", "vaug", "ddk", "sq", "diag", "nkmax", "epsk"))
    c2 = ctx

    def sb(name, shape, dt=F32):
        return c2.enter_context(nc.sbuf_tensor(name, shape, dt))

    qe = sb("p_qe", [P, 2, PH * PM])
    qfT = sb("p_qfT", [P, 2, NPAIR, P])
    kf = sb("p_kf", [P, 2, PH * PM])
    kvb = sb("p_kvb", [P, 2, NPAIR, PAIR])
    qmax, qtot, rden = sb("p_qmax", [P, 2, PH]), sb("p_qtot", [P, 2, PH]), sb("p_rden", [P, 2, PH])
    att, attT = sb("p_att", [P, 2, PH * PD]), sb("p_attT", [P, 2, NPAIR, P])

    kvz, xtp, kfe, kfr, q_in, sqr, red, dq_in, qmx, qto, dqs, qex, qft, qfte, kv_in, kvr, num_in, rdn, nrm, att_in, atte, wo_in, xo = (
        sem(n) for n in (
            "b_zeros", "b_xTp", "b_kf_exp", "b_kf", "b_q_psum", "b_sq", "b_diag", "b_dq_psum", "b_qmax", "b_qtot",
            "b_qe", "b_qf", "b_qfT_psum", "b_qfT", "b_kv_psum", "b_kv", "b_num_psum", "b_rden", "b_att",
            "b_attT_psum", "b_attT", "b_wo_psum", "b_x"))

    DQ0, QF0, AT0, NR0, XO0 = 2, 2, 3, 2, 1
    with nc.Block() as block:
        @block.gpsimd
        def _(pool):
            pool.memset(kvb[:], 0.0).then_inc(kvz, 1)
            pool.sem_inc(dq_in, DQ0)
            with pool.Fori(0, NB // 2) as i:
                for j in range(2):
                    n = i * 2 + j
                    pool.wait_ge(dq_in, n - 1 + DQ0)
                    pool.tensor_copy(xTp[:, j], xT[:, bass.ds(n * P, P)]).then_inc(xtp, 1)
                    pool.wait_ge(kfe, n + 1)
                    pool.tensor_tensor(kf[:, j], kf[:, j], epsk[:].broadcast_to([P, PH * PM]), ALU.add).then_inc(kfr, 1)

        @block.scalar
        def _(act):
            def exp_k(n, j):
                act.activation(kf[:, j], ddk[:, one(n), :].rearrange("p o n -> p (o n)"), ACT.Exp,
                               bias=nkmax[:]).then_inc(kfe, 1)

            def square_q(n, j):
                act.wait_ge(q_in, n + 1)
                act.activation(sq[:, j], psum[:, 0:2].rearrange("p a n -> p (a n)"), ACT.Square,
                               scale=DN / 2 ** 0.5).then_inc(sqr, 1)

            def exp_q(n, j):
                act.wait_ge(dqs, n + 1)
                act.activation(qe[:, j], qe[:, j], ACT.Exp).then_inc(qex, 1)

            def take_qfT(n, j):
                act.wait_ge(qft, n + 1)
                act.activation(qfT[:, j].rearrange("p q n -> p (q n)"), psum[:, 0:2].rearrange("p a n -> p (a n)"),
                               ACT.Identity, bias=epsk[:]).then_inc(qfte, 1)

            def take_attT(n, j):
                act.wait_ge(att_in, n + 1)
                act.activation(attT[:, j].rearrange("p q n -> p (q n)"),
                               psum[:, 2:4].rearrange("p a n -> p (a n)"), ACT.Copy).then_inc(atte, 1)

            def slot(n, j):
                first, second, last = parts(n)
                if first:
                    exp_k(n + 1, 1 - j)
                    square_q(n + 1, 1 - j)
                if second:
                    take_qfT(n, j)
                if last:
                    take_attT(n - 1, 1 - j)
                if first:
                    exp_q(n + 1, 1 - j)

            exp_k(0, 0)
            square_q(0, 0)
            exp_q(0, 0)
            batches(act, slot)

        @block.vector
        def _(dve):
            def shift_q(n, j):
                dd = psum[:, 2:4, :].rearrange("p a (h m) -> p (a h) m", m=PM)
                dve.wait_ge(sqr, n + 1)
                dve.tensor_reduce(diag[:, j], sq[:, j].rearrange("p (h d) -> p h d", h=PH), AX.X, ALU.add).then_inc(red, 1)
                dve.wait_ge(dq_in, n + 1 + DQ0)
                dve.tensor_reduce(qmax[:, j], dd, AX.X, ALU.max).then_inc(qmx, 1)
                dve.wait_ge(red, n + 1)
                dve.wait_ge(qmx, n + 1)
                dve.tensor_tensor(qtot[:, j], diag[:, j], qmax[:, j], ALU.add).then_inc(qto, 1)
                dve.wait_ge(qto, n + 1)
                dve.tensor_tensor(qe[:, j].rearrange("p (h m) -> p h m", h=PH), dd,
                                  qtot[:, j, :, None].broadcast_to([P, PH, PM]), ALU.subtract).then_inc(dqs, 1)

            def take_kv(n, j):
                dve.wait_ge(kv_in, n + 1)
                for lo, c in ((0, 0), (PD, VA)):
                    for q, m_, banks in ((0, 3, 2), (6, 2, 1)):
                        m = dve.tensor_copy(
                            kvb[lo:lo + PD, j, q:q + m_ * banks, c:c + VA],
                            psum[lo:lo + PD, 4 + q // 3:4 + q // 3 + banks, 0:m_ * PAIR].rearrange(
                                "p a (q n) -> p (a q) n" if banks == 1 else "p a (q n) -> p a q n", n=PAIR)[..., c:c + VA])
                m.then_inc(kvr, 1)

            def divide(n, j):
                dve.wait_ge(num_in, n + 1)
                two = psum[:, 4:6, 0:3 * PAIR].rearrange("p a (h n) -> p a h n", n=VA)
                single = psum[:, 6, 0:2 * PAIR].rearrange("p (h n) -> p h n", n=VA)
                dve.reciprocal(rden[:, j, 0:12].rearrange("p (a h) -> p a h", a=2), two[:, :, :, PD])
                dve.reciprocal(rden[:, j, 12:16], single[:, :, PD]).then_inc(rdn, 1)
                dve.wait_ge(rdn, n + 1)
                dve.tensor_tensor(att[:, j, 0:12 * PD].rearrange("p (a h d) -> p a h d", a=2, h=6), two[:, :, :, 0:PD],
                                  rden[:, j, 0:12, None].rearrange("p (a h) o -> p a h o", a=2).broadcast_to([P, 2, 6, PD]),
                                  ALU.mult)
                dve.tensor_tensor(att[:, j, 12 * PD:].rearrange("p (h d) -> p h d", h=4), single[:, :, 0:PD],
                                  rden[:, j, 12:16, None].broadcast_to([P, 4, PD]), ALU.mult).then_inc(nrm, 1)

            def add(n):
                x = xhat[:, one(n), :].rearrange("p o d -> p (o d)")
                dve.wait_ge(wo_in, n + 1)
                dve.tensor_tensor(x, psum[:, 7, 0:D], x, ALU.add).then_inc(xo, 1)

            def slot(n, j):
                first, second, last = parts(n)
                if first:
                    shift_q(n + 1, 1 - j)
                    take_kv(n + 1, 1 - j)
                if second:
                    divide(n, j)
                if last:
                    add(n - 1)

            dve.wait_ge(kvz, 1)
            shift_q(0, 0)
            take_kv(0, 0)
            batches(dve, slot)

        @block.tensor
        def _(pe):
            def project(n, j):
                pe.wait_ge(xtp, n + 1)
                for w, bank, done, used, count in ((wq, 0, q_in, qfte, n - 1 + QF0), (wdq, 2, dq_in, atte, n - 2 + AT0)):
                    pe.wait_ge(used, count)
                    for c in range(2):
                        m = pe.matmul(psum[:, bank + c, :], xTp[:, j], w[:, c * 512:(c + 1) * 512], start=True, stop=True)
                    m.then_inc(done, 1)

            def keys_values(n, j):
                pe.wait_ge(kfr, n + 1)
                pe.wait_ge(nrm, n - 1 + NR0)
                for q in range(NPAIR):
                    m = pe.matmul(psum[:, 4 + q // 3, (q % 3) * PAIR:(q % 3 + 1) * PAIR], kf[:, j, q * P:(q + 1) * P],
                                  vaug[:, one(n), 2 * q:2 * q + 2, :].rearrange("p o h d -> p (o h d)"),
                                  start=True, stop=True)
                m.then_inc(kv_in, 1)

            def turn_q(n, j, squared):
                pe.wait_ge(qex, n + 1)
                pe.wait_ge(sqr, squared)
                for q in range(NPAIR):
                    m = pe.transpose(psum[:, q // 4, (q % 4) * P:(q % 4 + 1) * P], qe[:, j, q * P:(q + 1) * P], ident[:])
                m.then_inc(qft, 1)

            def numerators(n, j, taken):
                pe.wait_ge(kvr, taken)
                pe.wait_ge(qfte, n + 1 + QF0)
                for q in range(NPAIR):
                    m = pe.matmul(psum[:, 4 + q // 3, (q % 3) * PAIR:(q % 3 + 1) * PAIR], qfT[:, j, q], kvb[:, j, q],
                                  start=True, stop=True)
                m.then_inc(num_in, 1)

            def turn_att(n, j, shifted):
                pe.wait_ge(nrm, n + 1 + NR0)
                pe.wait_ge(dqs, shifted)
                for q in range(NPAIR):
                    m = pe.transpose(psum[:, 2 + q // 4, (q % 4) * P:(q % 4 + 1) * P], att[:, j, q * P:(q + 1) * P], ident[:])
                m.then_inc(att_in, 1)

            def output(n, j):
                pe.wait_ge(atte, n + 1 + AT0)
                pe.wait_ge(xo, n + XO0)
                for q in range(NPAIR):
                    m = pe.matmul(psum[:, 7, 0:D], attT[:, j, q], wo[:, q], start=(q == 0), stop=(q == NPAIR - 1))
                m.then_inc(wo_in, 1)

            def slot(n, j):
                first, second, last = parts(n)
                begun = n + 2 if first else NB
                if first:
                    project(n + 1, 1 - j)
                    keys_values(n + 1, 1 - j)
                if second:
                    turn_q(n, j, begun)
                if last:
                    turn_att(n - 1, 1 - j, begun)
                if second:
                    numerators(n, j, begun)
                if last:
                    output(n - 1, 1 - j)

            pe.wait_ge(L["in_wq"], 32)
            pe.wait_ge(L["in_wo"], 16)
            pe.sem_inc(qfte, QF0)
            pe.sem_inc(atte, AT0)
            pe.sem_inc(nrm, NR0)
            pe.sem_inc(xo, XO0)
            project(0, 0)
            keys_values(0, 0)
            pe.wait_ge(sqr, 1)
            pe.wait_ge(dqs, 1)
            pe.wait_ge(kvr, 1)
            batches(pe, slot)
    performer_ffn(nc, S, L, w1, w2, b1, rows)


def performer_ffn(nc, S, L, w1, w2, b1, rows):
    sem, psum, xres, xhat, xT, ident = S.sem, S.psum, S.xres, S.xhat, S.xT, S.ident
    stats, mv, rstd = S.stats, S.mv, S.rstd
    EPS = 1e-6
    with ExitStack() as c:
        def sb(name, shape, dt=F32):
            return c.enter_context(nc.sbuf_tensor(name, shape, dt))

        o1b = sb("f_o1b", [P, NB, D])
        hb, he = (L["ddk"][:, n * HB:(n + 1) * HB, :].rearrange("p b (a n) -> p (b a n)", n=HALF).rearrange(
            "p (h f n) -> p h f n", h=2, n=HALF) for n in range(2))
        flat = L["vaug"][:].rearrange("p b h d -> p (b h d)")
        hm, hT = (flat[:, n * NB * HALF:(n + 1) * NB * HALF].rearrange("p (h f n) -> p h f n", h=2, n=HALF) for n in range(2))
        st, mvr, eps_, rs, half1, o1, o1br, tp, o1T, h_in, hbr, hmr, her, hpr, hTr, y_in, x2, half2, nrm, xr = (
            sem(n) for n in (
                "f_stats", "f_mv", "f_var_eps", "f_rstd", "f_ln_half", "f_out1", "f_out1_b2", "f_tp", "f_out1T",
                "f_h_psum", "f_hb", "f_hm", "f_he", "f_hp", "f_hT", "f_y_psum", "f_x2", "f_ln_half2", "f_ln2", "f_x"))
        with nc.Block() as block:
            @block.gpsimd
            def _(pool):
                def rsqrt(n, h):
                    pool.wait_ge(mvr, n + 1)
                    pool.tensor_scalar(rstd[:, h], mv[:, h, :, 1], EPS, 1.0, ALU.add, ALU.mult).then_inc(eps_, 1)
                    pool.wait_ge(eps_, n + 1)
                    pool.tensor_tensor(rstd[:, h], rstd[:, h], S.nhalf[:, 0:HB], ALU.pow).then_inc(rs, 1)

                rsqrt(0, 0)
                rsqrt(1, 1)
                pool.wait_ge(L["in_row"], 80)
                for h in range(2):
                    pool.wait_ge(o1, h + 1)
                    t = slice(HB * h, HB * h + HB)
                    pool.tensor_tensor(o1b[:, t], xhat[:, t], rows[:, 4, None, :].broadcast_to([P, HB, D]), ALU.add
                                       ).then_inc(o1br, 1)
                rsqrt(2, 0)
                rsqrt(3, 1)

            @block.vector
            def _(dve):
                def statistics(n, h, src):
                    for i in range(HB):
                        dve.bn_stats(stats[:, h, i], src[:, HB * h + i]).then_inc(st, 1)
                    dve.wait_ge(st, HB * (n + 1))
                    for i in range(HB):
                        m = dve.bn_aggr(mv[:, h, i], stats[:, h, i])
                    m.then_inc(mvr, 1)

                def normalise(n, h, x, g, half, done):
                    dve.wait_ge(rs, n + 1)
                    dve.wait_ge(mvr, n + 1)
                    for i in range(HB):
                        b = HB * h + i
                        m = dve.scalar_tensor_tensor(out=x[:, b], in0=x[:, b], scalar=mv[:, h, i, 0:1], in1=rows[:, g],
                                                     op0=ALU.subtract, op1=ALU.mult)
                    m.then_inc(half, 1)
                    dve.wait_ge(half, h + 1)
                    for i in range(HB):
                        b = HB * h + i
                        m = dve.scalar_tensor_tensor(out=x[:, b], in0=x[:, b], scalar=rstd[:, h, i:i + 1],
                                                     in1=rows[:, g + 1], op0=ALU.mult, op1=ALU.add)
                    m.then_inc(done, 1)

                statistics(0, 0, xhat)
                statistics(1, 1, xhat)
                dve.wait_ge(L["in_row"], 80)
                normalise(0, 0, xhat, 0, half1, o1)
                normalise(1, 1, xhat, 0, half1, o1)
                for h in range(2):
                    for f in range(PFB):
                        n = PFB * h + f
                        dve.wait_ge(hbr, n + 1)
                        dve.tensor_scalar(hm[:, h, f], hb[:, h, f], 0.0, None, ALU.min).then_inc(hmr, 1)
                        dve.tensor_scalar(hb[:, h, f], hb[:, h, f], 0.0, -1.0, ALU.max, ALU.add).then_inc(hpr, 1)
                    for f in range(PFB):
                        n = PFB * h + f
                        dve.wait_ge(her, n + 1)
                        dve.wait_ge(hpr, n + 1)
                        dve.tensor_tensor(hT[:, h, f], hb[:, h, f], he[:, h, f], ALU.add).then_inc(hTr, 1)
                for h in range(2):
                    t = slice(HB * h, HB * h + HB)
                    dve.wait_ge(y_in, h + 1)
                    dve.wait_ge(o1br, h + 1)
                    dve.tensor_tensor(o1b[:, t], psum[:, 6 + h].rearrange("p (b d) -> p b d", b=HB), o1b[:, t], ALU.add
                                      ).then_inc(x2, 1)
                    dve.wait_ge(x2, h + 1)
                    statistics(2 + h, h, o1b)
                for h in range(2):
                    t = slice(HB * h, HB * h + HB)
                    normalise(2 + h, h, o1b, 2, half2, nrm)
                    dve.wait_ge(nrm, h + 1)
                    dve.tensor_tensor(xres[:, t], xres[:, t], o1b[:, t], ALU.add).then_inc(xr, 1)

            @block.tensor
            def _(pe):
                pe.wait_ge(L["in_ffn"], 48)
                for h in range(2):
                    pe.wait_ge(o1, h + 1)
                    for i in range(HB):
                        m = pe.transpose(psum[:, h, i * P:(i + 1) * P], xhat[:, HB * h + i], ident[:])
                    m.then_inc(tp, 1)
                    pe.wait_ge(o1T, h + 1)
                    for f in range(PFB):
                        if h:
                            pe.wait_ge(hbr, f + 1)
                        pe.matmul(psum[:, 2 + f], w1[:, f * P:(f + 1) * P], xT[:, h * HALF:(h + 1) * HALF],
                                  start=True, stop=True).then_inc(h_in, 1)
                for h in range(2):
                    pe.wait_ge(hTr, PFB * (h + 1))
                    for i in range(HB):
                        for f in range(PFB):
                            m = pe.matmul(psum[:, 6 + h, i * P:(i + 1) * P], hT[:, h, f, i * P:(i + 1) * P], w2[:, f],
                                          start=(f == 0), stop=(f == PFB - 1))
                    m.then_inc(y_in, 1)

            @block.scalar
            def _(act):
                act.wait_ge(L["in_ffn"], 48)
                for h in range(2):
                    act.wait_ge(tp, h + 1)
                    act.activation(xT[:, h * HALF:(h + 1) * HALF], psum[:, h], ACT.Copy).then_inc(o1T, 1)
                    for f in range(PFB):
                        act.wait_ge(h_in, PFB * h + f + 1)
                        act.activation(hb[:, h, f], psum[:, 2 + f], ACT.Identity, bias=b1[:, f:f + 1]).then_inc(hbr, 1)
                    for f in range(PFB):
                        act.wait_ge(hmr, PFB * h + f + 1)
                        act.activation(he[:, h, f], hm[:, h, f], ACT.Exp).then_inc(her, 1)


XH, XD = 16, 8
XC = 4
XHC = XH // XC
DIVIDE, TURN_ATT, TAKE_ATT, OUTPUT, RESIDUAL = 1, 3, 2, 4, 3


def stage_cross0(nc, S, A):
    psum, ident, xres, xhat, xT = S.psum, S.ident, S.xres, S.xhat, S.xT
    with ExitStack() as c:
        sem = S.sem

        def sb(name, shape, dt=F32):
            return c.enter_context(nc.sbuf_tensor(name, shape, dt))

        qT, kT = sb("x_qT", [P, NB * P]), sb("x_kT", [P, NB * P])
        vall = sb("x_v", [P, NB, XH, XD + 1])
        km = sb("x_km", [P, 2, XH, P])
        qTp = sb("x_qTp", [P, 2, P])
        mx = sb("x_max", [P, 2, XH])
        e, eT = sb("x_e", [P, 2, XH, P]), sb("x_eT", [P, 2, XH, P])
        rden, att, attT = sb("x_rden", [P, 2, XH]), sb("x_att", [P, 2, D]), sb("x_attT", [P, 2, P])
        N = Norm(sem, "x")
        ones_v, kps, kTr, vps, vr, qps, qTr, xb = (sem(n) for n in (
            "x_ones", "x_k_psum", "x_kT", "x_v_psum", "x_v", "x_q_psum", "x_qT", "x_x_bo"))
        with nc.Block() as block:
            @block.gpsimd
            def _(pool):
                pool.memset(vall[:, :, :, XD:XD + 1], 1.0).then_inc(ones_v, 1)
                norm_pool(pool, S, N, EPS_OUTER)
                pool.wait_ge(S.in_x0, 16 * 10)
                pool.wait_ge(N.hat, 2)
                pool.tensor_tensor(xres[:], xres[:], S.x0rows[:, 1, None, :].broadcast_to([P, NB, D]), ALU.add).then_inc(xb, 1)

            @block.vector
            def _(dve):
                norm_vector(dve, S, N, xres, xhat)
                dve.wait_ge(S.in_x0, 16 * 10)
                for h in range(2):
                    dve.wait_ge(vps, h + 1)
                    dve.tensor_tensor(vall[:, HB * h:HB * h + HB, :, 0:XD],
                                      psum[:, 2 + h].rearrange("p (b h d) -> p b h d", b=HB, h=XH),
                                      S.x0rows[:, 0, :].rearrange("p (o h d) -> p o h d", o=1, h=XH).broadcast_to([P, HB, XH, XD]),
                                      ALU.add).then_inc(vr, 1)

            @block.tensor
            def _(pe):
                pe.wait_ge(S.in_x0, 16 * 10)
                for h in range(2):
                    pe.matmul(psum[:, h], S.x0w[:, 1], S.ctxT[:, h * HALF:(h + 1) * HALF], start=True, stop=True).then_inc(kps, 1)
                for h in range(2):
                    for i in range(HB):
                        b = HB * h + i
                        m = pe.matmul(psum[:, 2 + h, i * P:(i + 1) * P], S.ctxT[:, b * P:(b + 1) * P], S.x0w[:, 2],
                                      start=True, stop=True)
                    m.then_inc(vps, 1)
                norm_tensor(pe, S, N, 4)
                for h in range(2):
                    pe.wait_ge(N.xT, h + 1)
                    pe.matmul(psum[:, 6 + h], S.x0w[:, 0], xT[:, h * HALF:(h + 1) * HALF], start=True, stop=True).then_inc(qps, 1)

            @block.scalar
            def _(act):
                act.wait_ge(S.in_x0, 16 * 10)
                for h in range(2):
                    act.wait_ge(kps, h + 1)
                    act.activation(kT[:, h * HALF:(h + 1) * HALF], psum[:, h], ACT.Identity, bias=S.x0cols[:, 1:2]).then_inc(kTr, 1)
                norm_scalar(act, S, N, 4, xT)
                for h in range(2):
                    act.wait_ge(qps, h + 1)
                    act.activation(qT[:, h * HALF:(h + 1) * HALF], psum[:, 6 + h], ACT.Identity, bias=S.x0cols[:, 0:1]).then_inc(qTr, 1)

        kmr, qpr, s_in, mxr, sub, ex, t_in, t_out, o_in, rd, o_out, at_in, at_out, y_in, y_out = (sem(n) for n in (
            "xl_km", "xl_qT", "xl_s_psum", "xl_max", "xl_e_sub", "xl_e", "xl_eT_psum", "xl_eT", "xl_o_psum", "xl_rden",
            "xl_att", "xl_attT_psum", "xl_attT", "xl_y_psum", "xl_x"))
        S0, E0, T0 = 2 * XC, XC, 2

        with nc.Block() as block:
            @block.gpsimd
            def _(pool):
                pool.sem_inc(s_in, S0)
                with pool.Fori(0, NB // 2) as i:
                    for j in range(2):
                        n = i * 2 + j
                        pool.wait_ge(s_in, n * XC + XC)
                        pool.tensor_copy(qTp[:, j], qT[:, bass.ds(n * P, P)]).then_inc(qpr, 1)
                        pool.tensor_tensor(
                            km[:, j], kT[:, bass.ds(n * P, P)].rearrange("p (o n) -> p o n", o=1).broadcast_to([P, XH, P]),
                            S.headmask[:, :, None].broadcast_to([P, XH, P]), ALU.mult).then_inc(kmr, 1)

            @block.scalar
            def _(act):
                def exp(n, j, k):
                    act.wait_ge(sub, n * XC + (k + 1 + E0))
                    ap = e[:, j, k * XHC:(k + 1) * XHC]
                    act.activation(ap, ap, ACT.Exp, scale=float(XD) ** -0.5).then_inc(ex, 1)

                def take(n, j, k):
                    act.wait_ge(t_in, n * XC + (k + 1))
                    act.activation(eT[:, j, k * XHC:(k + 1) * XHC].rearrange("p h n -> p (h n)"), psum[:, 4 + k % 2],
                                   ACT.Copy).then_inc(t_out, 1)

                def take_att(n, j):
                    act.wait_ge(at_in, n + 1)
                    act.activation(attT[:, j], psum[:, 7, 0:P], ACT.Copy).then_inc(at_out, 1)

                def slot(n, j):
                    first, second, last = parts(n)
                    for k in range(XC):
                        if second:
                            take(n, j, k)
                        if first:
                            exp(n + 1, 1 - j, k)
                        if k == TAKE_ATT and last:
                            take_att(n - 1, 1 - j)

                for k in range(XC):
                    exp(0, 0, k)
                batches(act, slot)

            @block.vector
            def _(dve):
                def shift(n, j, k):
                    s = psum[:, k].rearrange("p (h n) -> p h n", h=XHC)
                    dve.wait_ge(s_in, n * XC + (k + 1 + S0))
                    dve.tensor_reduce(mx[:, j, k * XHC:(k + 1) * XHC], s, AX.X, ALU.max).then_inc(mxr, 1)
                    dve.wait_ge(mxr, n * XC + (k + 1))
                    dve.tensor_tensor(e[:, j, k * XHC:(k + 1) * XHC], s,
                                      mx[:, j, k * XHC:(k + 1) * XHC, None].broadcast_to([P, XHC, P]),
                                      ALU.subtract).then_inc(sub, 1)

                def divide(n, j):
                    o = psum[:, 6, 0:XH * (XD + 1)].rearrange("p (h d) -> p h d", h=XH)
                    dve.wait_ge(o_in, n + 1)
                    dve.reciprocal(rden[:, j], o[:, :, XD]).then_inc(rd, 1)
                    dve.wait_ge(rd, n + 1)
                    dve.tensor_tensor(att[:, j].rearrange("p (h d) -> p h d", h=XH), o[:, :, 0:XD],
                                      rden[:, j, :, None].broadcast_to([P, XH, XD]), ALU.mult).then_inc(o_out, 1)

                def residual(n):
                    x = xres[:, one(n), :].rearrange("p o d -> p (o d)")
                    dve.wait_ge(y_in, n + 1)
                    dve.tensor_tensor(x, psum[:, 7, P:2 * P], x, ALU.add).then_inc(y_out, 1)

                def slot(n, j):
                    first, second, last = parts(n)
                    for k in range(XC):
                        if first:
                            shift(n + 1, 1 - j, k)
                        if last:
                            if k == DIVIDE:
                                divide(n - 1, 1 - j)
                            if k == RESIDUAL:
                                residual(n - 1)

                dve.sem_inc(sub, E0)
                for k in range(XC):
                    shift(0, 0, k)
                batches(dve, slot)

            @block.tensor
            def _(pe):
                pe.sem_inc(t_out, T0)
                pe.sem_inc(o_out, 1)
                pe.sem_inc(y_out, 1)

                def scores(n, j, k):
                    if k == 0:
                        pe.wait_ge(kmr, n + 1)
                        pe.wait_ge(qpr, n + 1)
                    pe.wait_ge(sub, n * XC + (k + 1))
                    pe.matmul(psum[:, k], qTp[:, j], km[:, j, k * XHC:(k + 1) * XHC].rearrange("p h n -> p (h n)"),
                              start=True, stop=True).then_inc(s_in, 1)

                def turn(n, j, k):
                    pe.wait_ge(ex, n * XC + (k + 1))
                    pe.wait_ge(t_out, n * XC + (k - 1 + T0))
                    for h in range(XHC):
                        m = pe.transpose(psum[:, 4 + k % 2, h * P:(h + 1) * P], e[:, j, k * XHC + h], ident[:])
                    m.then_inc(t_in, 1)

                def values(n, j, first, end):
                    if first == 0:
                        pe.wait_ge(t_out, n * XC + (XC + T0))
                        pe.wait_ge(o_out, n + 1)
                    for h in range(first, end):
                        m = pe.matmul(psum[:, 6, h * (XD + 1):(h + 1) * (XD + 1)], eT[:, j, h],
                                      vall[:, one(n), h].rearrange("p o d -> p (o d)"), start=True, stop=True)
                    if end == XH:
                        m.then_inc(o_in, 1)

                def turn_att(n, j):
                    pe.wait_ge(o_out, n + 2)
                    pe.wait_ge(y_out, n + 1)
                    pe.transpose(psum[:, 7, 0:P], att[:, j], ident[:]).then_inc(at_in, 1)

                def output(n, j):
                    pe.wait_ge(at_out, n + 1)
                    pe.matmul(psum[:, 7, P:2 * P], attT[:, j], S.x0w[:, 3], start=True, stop=True).then_inc(y_in, 1)

                def slot(n, j):
                    first, second, last = parts(n)
                    for k in range(XC):
                        if last:
                            if k == TURN_ATT:
                                turn_att(n - 1, 1 - j)
                            if k == OUTPUT:
                                output(n - 1, 1 - j)
                        if second:
                            turn(n, j, k)
                        if first:
                            scores(n + 1, 1 - j, k)
                        if k < 2 and last:
                            values(n - 1, 1 - j, k * XH // 2, (k + 1) * XH // 2)
                    if OUTPUT == XC and last:
                        output(n - 1, 1 - j)

                for k in range(XC):
                    scores(0, 0, k)
                batches(pe, slot)


ME, MF = 8, 256
MFB = MF // P
MU = 2 * MFB


def stage_moe(nc, S, A):
    psum, ident, xres, xhat, xT = S.psum, S.ident, S.xres, S.xhat, S.xT
    with ExitStack() as c:
        sem = S.sem

        def sb(name, shape, dt=F32):
            return c.enter_context(nc.sbuf_tensor(name, shape, dt))

        router = sb("m_router", [P, ME])
        wg, wu = sb("m_wg", [P, 2, MF]), sb("m_wu", [P, 2, MF])
        wd = sb("m_wd", [P, ME * MFB, D])
        rank = sb("m_rank", [P, ME])
        R = sb("m_r", [P, 8, NB, ME])
        r1 = sb("m_r1", [P, 8, NB])
        sg, fT = sb("m_sg", [P, 2, HALF]), sb("m_fT", [P, 2, MU, HALF])
        N = Norm(sem, "m")
        in_r, in_wd, lg, v, ae = (sem(n) for n in ("m_in_router", "m_in_wd", "m_logits", "m_route", "m_exp"))
        in_w = [sem(f"m_in_w{j}") for j in range(2)]
        gu, sgr, fr, dn, added = (sem(n) for n in ("m_gu_psum", "m_silu", "m_fused", "m_down_psum", "m_added"))
        F0, ADD0 = 2, 4

        def flat(t):
            return t.rearrange("p b e -> p (b e)")

        with nc.Block() as block:
            @block.sync
            def _(sp):
                def expert(e, j):
                    for w, n in ((wg, "mwg"), (wu, "mwu")):
                        sp.dma_start(w[:, j], A[n][:, one(e), :].rearrange("p o f -> p (o f)")).then_inc(in_w[j], 16)

                load(sp, router[:], A["router"], in_r)
                load(sp, rank[:], A["rank"].partition_broadcast(P), in_r)
                for j in range(2):
                    expert(j, j)
                load(sp, wd[:], A["mwd"], in_wd)
                with sp.Fori(1, ME // 2) as i:
                    for j in range(2):
                        sp.wait_ge(gu, (i * 2 + j - 1) * MU)
                        expert(i * 2 + j, j)

            @block.gpsimd
            def _(pool):
                norm_pool(pool, S, N, EPS_OUTER)

            @block.scalar
            def _(act):
                def silu(e, n):
                    act.wait_ge(gu, e * MU + (n + 1))
                    act.wait_ge(fr, e * MU + (n - 1 + F0))
                    act.activation(sg[:, n % 2], psum[:, n % 2], ACT.Silu).then_inc(sgr, 1)

                norm_scalar(act, S, N, 0, xT)
                act.wait_ge(v, 2)
                act.activation(flat(R[:, 0]), flat(R[:, 0]), ACT.Exp).then_inc(ae, 1)
                for n in range(2):
                    silu(0, n)
                act.wait_ge(v, 17)
                act.activation(r1[:, 5], r1[:, 4], ACT.Exp).then_inc(ae, 1)
                for n in range(2, MU):
                    silu(0, n)

                def slot(e, j):
                    if parts(e)[0]:
                        for n in range(MU):
                            silu(e + 1, n)

                batches(act, slot)

            @block.vector
            def _(dve):
                norm_vector(dve, S, N, xres, xhat)
                count = [0]

                def step(m):
                    count[0] += 1
                    m.then_inc(v, 1)
                    dve.wait_ge(v, count[0])

                def bc(a):
                    return a[:, :, None].broadcast_to([P, NB, ME])

                def fuse(e, j, n):
                    dve.wait_ge(sgr, e * MU + (n + 1))
                    dve.tensor_tensor(fT[:, j, n], sg[:, n % 2], psum[:, 2 + n % 2], ALU.mult).then_inc(fr, 1)

                def add(e, j, h):
                    dve.wait_ge(dn, e * 2 + (h + 1))
                    dve.wait_ge(added, e * 2 + (h - 1 + ADD0))
                    for q in range(HB):
                        b = HB * h + q
                        m = dve.scalar_tensor_tensor(out=xres[:, b], in0=psum[:, 4 + 2 * j + h, q * P:(q + 1) * P],
                                                     scalar=R[:, 7, b, one(e)], in1=xres[:, b], op0=ALU.mult, op1=ALU.add)
                    m.then_inc(added, 1)

                dve.sem_inc(added, ADD0)
                dve.wait_ge(lg, 1)
                dve.wait_ge(in_r, 32)
                lgt = psum[:, 7, 0:NB * ME].rearrange("p (b e) -> p b e", b=NB)
                rk = rank[:, None, :].broadcast_to([P, NB, ME])
                step(dve.tensor_reduce(r1[:, 0], lgt, AX.X, ALU.max))
                step(dve.tensor_tensor(R[:, 0], lgt, bc(r1[:, 0]), ALU.subtract))
                dve.wait_ge(ae, 1)
                step(dve.tensor_reduce(r1[:, 1], R[:, 0], AX.X, ALU.add))
                step(dve.reciprocal(r1[:, 2], r1[:, 1]))
                step(dve.tensor_tensor(R[:, 1], R[:, 0], bc(r1[:, 2]), ALU.mult))
                for k in range(2):
                    pr, first = R[:, 1 + 3 * k], R[:, 3 + 3 * k]
                    step(dve.tensor_reduce(r1[:, 3 + 3 * k], pr, AX.X, ALU.max))
                    step(dve.tensor_tensor(R[:, 2 + 3 * k], pr, bc(r1[:, 3 + 3 * k]), ALU.is_equal))
                    step(dve.tensor_tensor(R[:, 2 + 3 * k], R[:, 2 + 3 * k], rk, ALU.mult))
                    step(dve.tensor_reduce(r1[:, 7], R[:, 2 + 3 * k], AX.X, ALU.max))
                    step(dve.tensor_tensor(first, R[:, 2 + 3 * k], bc(r1[:, 7]), ALU.is_equal))
                    if k == 0:
                        step(dve.scalar_tensor_tensor(out=flat(R[:, 4]), in0=flat(first), scalar=-2.0, in1=flat(pr),
                                                      op0=ALU.mult, op1=ALU.add))
                    fuse(0, 0, k)
                step(dve.tensor_tensor(r1[:, 4], r1[:, 6], r1[:, 3], ALU.subtract))
                assert count[0] == 17
                dve.wait_ge(ae, 2)
                step(dve.tensor_scalar(r1[:, 0], r1[:, 5], 1.0, None, ALU.add))
                step(dve.reciprocal(r1[:, 1], r1[:, 0]))
                step(dve.tensor_tensor(r1[:, 2], r1[:, 5], r1[:, 1], ALU.mult))
                for n in range(2, MU):
                    fuse(0, 0, n)
                step(dve.tensor_tensor(R[:, 3], R[:, 3], bc(r1[:, 1]), ALU.mult))
                step(dve.tensor_tensor(R[:, 6], R[:, 6], bc(r1[:, 2]), ALU.mult))
                step(dve.tensor_tensor(R[:, 7], R[:, 3], R[:, 6], ALU.add))

                def slot(e, j):
                    first, second, last = parts(e)
                    for n in range(MU):
                        if first:
                            fuse(e + 1, 1 - j, n)
                        if second and n % 2:
                            add(e, j, n // 2)

                batches(dve, slot)

            @block.tensor
            def _(pe):
                def up(e, j, n):
                    fb, h = n // 2, n % 2
                    if n == 0:
                        pe.wait_ge(in_w[j], (e - j) * 16 + 32)
                    pe.wait_ge(fr, e * MU + (n - 1 + F0))
                    pe.matmul(psum[:, h], wg[:, j, fb * P:(fb + 1) * P], xT[:, h * HALF:(h + 1) * HALF], start=True, stop=True)
                    pe.matmul(psum[:, 2 + h], wu[:, j, fb * P:(fb + 1) * P], xT[:, h * HALF:(h + 1) * HALF],
                              start=True, stop=True).then_inc(gu, 1)

                def down(e, j, h):
                    pe.wait_ge(fr, e * MU + (MU - 1 + h + F0))
                    pe.wait_ge(added, e * 2 + (h - 3 + ADD0))
                    for q in range(HB):
                        for fb in range(MFB):
                            m = pe.matmul(psum[:, 4 + 2 * j + h, q * P:(q + 1) * P], fT[:, j, 2 * fb + h, q * P:(q + 1) * P],
                                          wd[:, one(e * MFB + fb), :].rearrange("p o d -> p (o d)"),
                                          start=(fb == 0), stop=(fb == MFB - 1))
                    m.then_inc(dn, 1)

                norm_tensor(pe, S, N, 0)
                pe.sem_inc(fr, F0)
                pe.wait_ge(in_r, 32)
                pe.wait_ge(N.xT, 2)
                for b in range(NB):
                    m = pe.matmul(psum[:, 7, b * ME:(b + 1) * ME], xT[:, b * P:(b + 1) * P], router[:], start=True, stop=True)
                m.then_inc(lg, 1)
                for n in range(MU):
                    up(0, 0, n)
                pe.wait_ge(in_wd, 16)
                pe.wait_ge(v, 2)

                def slot(e, j):
                    first, second, last = parts(e)
                    for n in range(MU):
                        if first:
                            up(e + 1, 1 - j, n)
                        if second and n % 2:
                            down(e, j, n // 2)

                batches(pe, slot)


LL = 4
QH, QD = 16, 8
LF = 512
LFB = LF // P
NQ = 6
KQV = (1, 0, 2)
EPS_L1 = 1e-5
ROUND = 1.5 * 2.0 ** 23
LW1, LB1, LW2, LB2, LQB, LFC = 0, 1, 2, 3, 4, 4 + NQ
LCOLS = LFC + LFB
STEPS = 11
WARM0, WARM = 2, 5
CUT = 8
POOL_COLS = 144


def stage_layers(nc, S, A):
    psum, ident, xres, xhat = S.psum, S.ident, S.xres, S.xhat
    with ExitStack() as c:
        sem = S.sem

        def sb(name, shape, dt=F32):
            return c.enter_context(nc.sbuf_tensor(name, shape, dt))

        def pair(name):
            return [sem(f"l_{name}{h}") for h in range(2)]

        wqkv, wf = sb("l_wqkv", [P, NQ, P]), sb("l_wf", [P, LF])
        wp, wc, wm = sb("l_wp", [P, LL, D]), sb("l_wc", [P, LL, D]), sb("l_wm", [P, LL * LFB, D])
        cols, rows = sb("l_cols", [P, LL, LCOLS]), sb("l_rows", [P, LL, 2, D])
        colA, colF = sb("l_col_a", [P, LCOLS]), sb("l_col_f", [P, LCOLS])
        hart, hneg, filt = sb("l_hart", [P, P]), sb("l_hneg", [P, P]), sb("l_filt", [P, P])
        halfpi, rnd = sb("l_halfpi", [P, 1]), sb("l_round", [P, 2])
        xl = sb("l_x", [P, NB, D])
        xnT = sb("l_xnT", [P, 2, HALF])
        Q = sb("l_q", [P, 2, 4, 3, HALF])
        R, T = sb("l_r", [P, 2, 4, HALF]), sb("l_t", [P, 3, 4, HALF])
        z = sb("l_z", [P, 2, HALF])
        gT = sb("l_g", [P, 2, LFB, HALF])
        N0 = Norm(sem, "l0")
        N = [Norm(sem, f"l{h}") for h in (1, 2)]
        in_c, in_q, in_p, in_f, in_m, cst, neg, wc_in, wc_out, hv, hp, col_a, col_f, last = (sem(f"l_{n}") for n in (
            "in_const", "in_wqkv", "in_wp", "in_wf", "in_wm", "const", "hneg_made", "wc_psum", "wc_made",
            "ham_vector", "ham_pool", "columns_a", "columns_f", "x_out"))
        q_in, q_out, rr, kk, red, absd, cosd, dif = (pair(n) for n in (
            "q_psum", "q_taken", "turns_t", "turns", "reduced", "abs", "cos", "diff"))
        f_in, f_out, p_in, x1, xb, h_in, g_out, y_in, x2, xb2 = (pair(n) for n in (
            "hart_psum", "z_made", "proj_psum", "x1", "x_bias", "h_psum", "gelu", "y_psum", "x2", "x_bias2"))

        def layers(eng, half_step):
            half_step(0, 0, None, None)
            half_step(1, 0, 0, 0)
            with eng.Fori(1, LL) as l:
                half_step(0, l, 1, l - 1)
                half_step(1, l, 0, l)
            half_step(None, None, 1, LL - 1)

        with nc.Block() as block:
            @block.sync
            def _(sp):
                load(sp, cols[:], A["lcols"], in_c)
                load(sp, hart[:], A["hartley"], in_c)
                load(sp, filt[:], A["filter"], in_c)
                load(sp, rows[:].rearrange("p l k d -> p (l k d)"), A["lrows"].partition_broadcast(P), in_c)
                load(sp, wqkv[:].rearrange("p a b -> p (a b)"), A["lwqkv"][:, 0], in_q)
                load(sp, wp[:], A["lwp"], in_p)
                load(sp, wf[:], A["lwf"][:, 0], in_f)
                load(sp, wm[:].rearrange("p a b -> p (a b)"), A["lwm"].rearrange("p l n -> p (l n)"), in_m)
                with sp.Fori(1, LL) as l:
                    sp.wait_ge(q_in[1], l * NQ)
                    sp.dma_start(wqkv[:].rearrange("p a b -> p (a b)"),
                                 A["lwqkv"][:, bass.ds(l, 1), :].rearrange("p o f -> p (o f)")).then_inc(in_q, 16)
                    sp.wait_ge(h_in[1], l * LFB)
                    sp.dma_start(wf[:], A["lwf"][:, bass.ds(l, 1), :].rearrange("p o f -> p (o f)")).then_inc(in_f, 16)

            def hamilton(eng, h, lo, hi, base, done):
                n = hi - lo
                a, b, v = (Q[:, h, :, k, lo:hi] for k in range(3))
                r = R[:, h, :, lo:hi]
                t = [T[:, i, :, lo:hi] for i in range(3)]

                def sq(x):
                    return x.rearrange("p (s c) n -> p s c n", s=2)

                def bc(i, shape):
                    x = a[:, i]
                    return (x[:, None, :] if len(shape) == 3 else x[:, None, None, :]).broadcast_to(shape)

                four, two = [P, 4, n], [P, 2, 2, n]
                steps = (
                    (r, bc(0, four), b, ALU.mult, 0),
                    (sq(t[0]), bc(1, two), sq(b)[:, :, ::-1], ALU.mult, 0),
                    (sq(t[1]), bc(2, two), sq(b)[:, ::-1], ALU.mult, 0),
                    (r[:, 0:4:2], r[:, 0:4:2], t[0][:, 0:4:2], ALU.subtract, 2),
                    (r[:, 1:4:2], r[:, 1:4:2], t[0][:, 1:4:2], ALU.add, 2),
                    (t[2], bc(3, four), b[:, ::-1], ALU.mult, 0),
                    (r[:, 0:4:3], r[:, 0:4:3], t[1][:, 0:4:3], ALU.subtract, 5),
                    (r[:, 1:3], r[:, 1:3], t[1][:, 1:3], ALU.add, 5),
                    (r[:, 0:2], r[:, 0:2], t[2][:, 0:2], ALU.subtract, 8),
                    (r[:, 2:4], r[:, 2:4], t[2][:, 2:4], ALU.add, 8),
                    (r, r, v, ALU.mult, 10))

                def run(first, end):
                    for out, x, y, op, after in steps[first:end]:
                        if after:
                            eng.wait_ge(done, base + after)
                        eng.tensor_tensor(out, x, y, op).then_inc(done, 1)

                return run

            @block.gpsimd
            def _(pool):
                norm_pool(pool, S, N0, EPS_OUTER)
                pool.memset(halfpi[:], float(np.pi / 2)).then_inc(cst, 1)
                pool.memset(rnd[:, 0:1], ROUND).then_inc(cst, 1)
                pool.memset(rnd[:, 1:2], -ROUND).then_inc(cst, 1)
                pool.memset(S.eps[:], EPS_L1).then_inc(cst, 1)
                for h in range(2):
                    for k in range(3):
                        pool.memset(Q[:, h, 1, k].rearrange("p (b n) -> p b n", n=P)[:, :, 0:1], 0.0).then_inc(cst, 1)
                pool.wait_ge(cst, 10)

                def rsqrt(h, l, i):
                    pool.wait_ge(N[h].mv, l * 2 + (i + 1))
                    pool.tensor_tensor(S.rstd[:, h], S.mv[:, h, :, 1], S.eps[:, 0:HB], ALU.add).then_inc(N[h].eps, 1)
                    pool.wait_ge(N[h].eps, l * 2 + (i + 1))
                    pool.tensor_tensor(S.rstd[:, h], S.rstd[:, h], S.nhalf[:, 0:HB], ALU.pow).then_inc(N[h].rstd, 1)

                def add_bias(h, l, i, done):
                    pool.wait_ge(in_c, 64)
                    pool.wait_ge(N[h].hat, l * 2 + (i + 1))
                    x = xl[:, HB * h:HB * h + HB]
                    row = rows[:, l, i, None, :] if isinstance(l, int) else rows[:, bass.ds(l, 1), i, :]
                    pool.tensor_tensor(x, x, row.broadcast_to([P, HB, D]), ALU.add).then_inc(done[h], 1)

                def quaternions(h, l):
                    pool.wait_ge(cosd[h], l * 3 + 1)
                    pool.wait_ge(dif[h], l * 3 + 2)
                    pool.wait_ge(q_out[h], l * NQ + 4)

                def half_step(h, l, o, m):
                    if h is not None:
                        add_bias(h, l, 0, xb)
                    if o is not None:
                        rsqrt(o, m, 1)
                        add_bias(o, m, 1, xb2)
                    if h is None:
                        return
                    ham = hamilton(pool, h, HALF - POOL_COLS, HALF, l * (2 * STEPS) + h * STEPS, hp)
                    quaternions(h, l)
                    ham(0, 5)
                    pool.wait_ge(cosd[h], l * 3 + 2)
                    ham(5, 10)
                    pool.wait_ge(dif[h], l * 3 + 3)
                    pool.wait_ge(cosd[h], l * 3 + 3)
                    ham(10, STEPS)
                    if o is not None:
                        rsqrt(o, m + 1, 0)

                rsqrt(0, 0, 0)
                rsqrt(1, 0, 0)
                layers(pool, half_step)

            @block.vector
            def _(dve):
                norm_vector(dve, S, N0, xres, xl)
                dve.wait_ge(in_c, 64)
                dve.tensor_scalar(hneg[:], hart[:], -1.0, None, ALU.mult).then_inc(neg, 1)
                dve.wait_ge(cst, 10)
                dve.wait_ge(N0.hat, 2)

                def statistics(h):
                    for k in range(HB):
                        m = dve.bn_stats(S.stats[:, h, k], xl[:, HB * h + k])
                    dve.drain()
                    for k in range(HB):
                        m = dve.bn_aggr(S.mv[:, h, k], S.stats[:, h, k])
                    m.then_inc(N[h].mv, 1)

                def normalise(h, l, i):
                    dve.wait_ge(N[h].mv, l * 2 + (i + 1))
                    dve.wait_ge(N[h].rstd, l * 2 + (i + 1))
                    for k in range(HB):
                        b = HB * h + k
                        m = dve.tensor_scalar(xhat[:, b], xl[:, b], S.mv[:, h, k, 0:1], S.rstd[:, h, k:k + 1],
                                              ALU.subtract, ALU.mult)
                    m.then_inc(N[h].hat, 1)

                def reduce(h, l, n):
                    k = KQV[n]
                    dve.wait_ge(kk[h], l * 3 + (n + 1))
                    dve.scalar_tensor_tensor(out=Q[:, h, 3, k], in0=Q[:, h, 3, k], scalar=-2.0 * float(np.pi),
                                             in1=Q[:, h, 0, k], op0=ALU.mult, op1=ALU.add).then_inc(red[h], 1)

                def differ(h, l, n):
                    x, y = (Q[:, h, c_, KQV[n]].rearrange("p (b n) -> p b n", n=P) for c_ in range(2))
                    dve.wait_ge(q_out[h], l * NQ + (2 * n + 1))
                    dve.tensor_tensor(y[:, :, 1:P], x[:, :, 1:P], x[:, :, 0:P - 1], ALU.subtract).then_inc(dif[h], 1)

                def quaternions(h, l):
                    dve.wait_ge(cosd[h], l * 3 + 1)
                    dve.wait_ge(dif[h], l * 3 + 2)
                    dve.wait_ge(q_out[h], l * NQ + 4)

                def filtered(h, l):
                    dve.wait_ge(f_in[h], l + 1)
                    dve.tensor_tensor(z[:, h].rearrange("p (b n) -> p b n", n=P),
                                      psum[:, 7].rearrange("p (b n) -> p b n", n=P),
                                      filt[:, None, :].broadcast_to([P, HB, P]), ALU.mult).then_inc(f_out[h], 1)

                def residual(h, l, bank, got, biased, done):
                    x = xl[:, HB * h:HB * h + HB]
                    dve.wait_ge(got[h], l + 1)
                    dve.wait_ge(biased[h], l + 1)
                    dve.tensor_tensor(x, psum[:, bank].rearrange("p (b d) -> p b d", b=HB), x, ALU.add).then_inc(done[h], 1)
                    dve.wait_ge(done[h], l + 1)

                def half_step(h, l, o, m):
                    if h is not None:
                        differ(h, l, 0)
                        reduce(h, l, 0)
                    if o is not None:
                        filtered(o, m)
                        residual(o, m, 7, p_in, xb, x1)
                        statistics(o)
                    if h is not None:
                        reduce(h, l, 1)
                        differ(h, l, 1)
                    if o is not None:
                        normalise(o, m, 1)
                    if h is None:
                        residual(o, m, 0, y_in, xb2, x2)
                        return
                    ham = hamilton(dve, h, 0, HALF - POOL_COLS, l * (2 * STEPS) + h * STEPS, hv)
                    quaternions(h, l)
                    ham(0, 1)
                    reduce(h, l, 2)
                    ham(1, 3)
                    differ(h, l, 2)
                    ham(3, 5)
                    dve.wait_ge(cosd[h], l * 3 + 2)
                    ham(5, CUT)
                    if o is not None:
                        residual(o, m, 0, y_in, xb2, x2)
                        statistics(o)
                    ham(CUT, 10)
                    dve.wait_ge(dif[h], l * 3 + 3)
                    dve.wait_ge(cosd[h], l * 3 + 3)
                    if o is not None:
                        normalise(o, m + 1, 0)
                    ham(10, STEPS)

                for h in range(2):
                    statistics(h)
                for h in range(2):
                    normalise(h, 0, 0)
                layers(dve, half_step)
                for h in range(2):
                    t = slice(HB * h, HB * h + HB)
                    m = dve.tensor_tensor(xres[:, t], xres[:, t], xl[:, t], ALU.add)
                m.then_inc(last, 1)

            @block.scalar
            def _(act):
                act.wait_ge(cst, 10)
                act.wait_ge(in_c, 64)
                act.wait_ge(wc_in, 1)
                act.activation(wc[:].rearrange("p l d -> p (l d)"), psum[:, 7], ACT.Copy).then_inc(wc_out, 1)

                def columns(l, dst, done):
                    act.drain()
                    src = cols[:, l, :] if isinstance(l, int) else cols[:, bass.ds(l, 1), :].rearrange("p o k -> p (o k)")
                    act.activation(dst[:], src, ACT.Copy).then_inc(done, 1)
                    act.wait_ge(done, l + 1)

                def take_norm(h, l, i):
                    col, w, b = ((colA, LW1, LB1), (colF, LW2, LB2))[i]
                    act.wait_ge(N[h].turned, l * 2 + (i + 1))
                    act.activation(xnT[:, h], psum[:, 0], ACT.Identity, scale=col[:, w:w + 1], bias=col[:, b:b + 1]
                                   ).then_inc(N[h].xT, 1)

                def take_q(h, l, n):
                    act.wait_ge(q_in[h], l * NQ + (n + 1))
                    act.activation(Q[:, h, 2 * (n % 2), KQV[n // 2]], psum[:, 1 + n % 3], ACT.Identity,
                                   bias=colA[:, LQB + n:LQB + n + 1]).then_inc(q_out[h], 1)

                def turns(h, l, n):
                    x, y = Q[:, h, 0, KQV[n]], Q[:, h, 3, KQV[n]]
                    act.wait_ge(q_out[h], l * NQ + (2 * n + 1))
                    act.activation(y, x, ACT.Identity, scale=float(0.5 / np.pi), bias=rnd[:, 0:1]).then_inc(rr[h], 1)
                    act.wait_ge(rr[h], l * 3 + (n + 1))
                    act.activation(y, y, ACT.Identity, bias=rnd[:, 1:2]).then_inc(kk[h], 1)

                def cosine(h, l, n):
                    y = Q[:, h, 3, KQV[n]]
                    act.wait_ge(red[h], l * 3 + (n + 1))
                    act.activation(y, y, ACT.Abs).then_inc(absd[h], 1)
                    act.wait_ge(absd[h], l * 3 + (n + 1))
                    act.activation(y, y, ACT.Sin, scale=-1.0, bias=halfpi[:]).then_inc(cosd[h], 1)

                def gelu(h, l):
                    for f in range(LFB):
                        act.wait_ge(h_in[h], l * LFB + (f + 1))
                        act.activation(gT[:, h, f], psum[:, 4 + f % 3], ACT.Gelu, bias=colF[:, LFC + f:LFC + f + 1]
                                       ).then_inc(g_out[h], 1)

                def half_step(h, l, o, m):
                    if h == 0:
                        columns(l, colA, col_a)
                    if o == 0:
                        columns(m, colF, col_f)
                    if h is not None:
                        take_norm(h, l, 0)
                        take_q(h, l, 0)
                        turns(h, l, 0)
                        take_q(h, l, 1)
                        cosine(h, l, 0)
                        take_q(h, l, 2)
                        take_q(h, l, 3)
                        turns(h, l, 1)
                        take_q(h, l, 4)
                        turns(h, l, 2)
                        take_q(h, l, 5)
                    if o is not None:
                        take_norm(o, m, 1)
                    if h is not None:
                        cosine(h, l, 1)
                        cosine(h, l, 2)
                    if o is not None:
                        gelu(o, m)

                layers(act, half_step)

            @block.tensor
            def _(pe):
                pe.wait_ge(in_c, 64)
                pe.wait_ge(neg, 1)
                pe.wait_ge(in_p, 16)
                for l in range(LL):
                    m = pe.matmul(psum[:, 7, l * D:(l + 1) * D], hart[:], wp[:, l], start=True, stop=True)
                m.then_inc(wc_in, 1)

                def turn(h, l, i):
                    pe.wait_ge(N[h].hat, l * 2 + (i + 1))
                    for k in range(HB):
                        m = pe.transpose(psum[:, 0, k * P:(k + 1) * P], xhat[:, HB * h + k], ident[:])
                    m.then_inc(N[h].turned, 1)

                def project(h, l, first, end):
                    for k in range(first, end):
                        if k >= 3:
                            pe.wait_ge(q_out[h], l * NQ + (k - 2))
                        pe.matmul(psum[:, 1 + k % 3], wqkv[:, k], xnT[:, h], start=True, stop=True).then_inc(q_in[h], 1)

                def hartley(h, l):
                    pe.wait_ge(hv, l * (2 * STEPS) + STEPS * (h + 1))
                    pe.wait_ge(hp, l * (2 * STEPS) + STEPS * (h + 1))
                    for k in range(4):
                        m = pe.matmul(psum[:, 7], (hneg if k else hart)[:], R[:, h, k], start=(k == 0), stop=(k == 3))
                    m.then_inc(f_in[h], 1)

                def out(h, l):
                    w = wc[:, l] if isinstance(l, int) else wc[:, bass.ds(l, 1), :].rearrange("p o d -> p (o d)")
                    pe.wait_ge(f_out[h], l + 1)
                    for k in range(HB):
                        m = pe.matmul(psum[:, 7, k * P:(k + 1) * P], z[:, h, k * P:(k + 1) * P], w, start=True, stop=True)
                    m.then_inc(p_in[h], 1)

                def fc(h, l):
                    pe.wait_ge(N[h].xT, l * 2 + 2)
                    pe.wait_ge(in_f, l * 16 + 16)
                    for f in range(LFB):
                        if f >= 3:
                            pe.wait_ge(g_out[h], l * LFB + (f - 2))
                        pe.matmul(psum[:, 4 + f % 3], wf[:, f * P:(f + 1) * P], xnT[:, h], start=True, stop=True
                                  ).then_inc(h_in[h], 1)

                def mproj(h, l):
                    pe.wait_ge(g_out[h], l * LFB + LFB)
                    pe.wait_ge(in_m, 16)
                    for k in range(HB):
                        for f in range(LFB):
                            w = wm[:, l * LFB + f] if isinstance(l, int) else wm[:, bass.ds(l * LFB + f, 1), :].rearrange("p o d -> p (o d)")
                            m = pe.matmul(psum[:, 0, k * P:(k + 1) * P], gT[:, h, f, k * P:(k + 1) * P], w,
                                          start=(f == 0), stop=(f == LFB - 1))
                    m.then_inc(y_in[h], 1)

                def keep_warm(bank, n):
                    for k in range(n):
                        pe.matmul(psum[:, bank], ident[:], xnT[:, 0], start=True, stop=True)

                def half_step(h, l, o, m):
                    if h is not None:
                        turn(h, l, 0)
                        pe.wait_ge(in_q, l * 16 + 16)
                        if o is not None:
                            pe.wait_ge(q_out[o], m * NQ + NQ)
                        pe.wait_ge(N[h].xT, l * 2 + 1)
                        project(h, l, 0, 2)
                    if o is not None:
                        hartley(o, m)
                    if h is not None:
                        project(h, l, 2, 3)
                    if o is not None:
                        out(o, m)
                    if h is not None:
                        project(h, l, 3, NQ)
                        if o is not None:
                            keep_warm(0, WARM0)
                    if o is not None:
                        turn(o, m, 1)
                        fc(o, m)
                        mproj(o, m)
                        if h is not None:
                            keep_warm(7, WARM)

                pe.wait_ge(wc_out, 1)
                layers(pe, half_step)


YH, YD = 4, 32


def stage_cross1(nc, S, A):
    psum, ident, xres, xhat, xT = S.psum, S.ident, S.xres, S.xhat, S.xT
    with ExitStack() as c:
        sem = S.sem

        def sb(name, shape, dt=F32):
            return c.enter_context(nc.sbuf_tensor(name, shape, dt))

        w, cols, rows = sb("y_w", [P, 4, D]), sb("y_cols", [P, 2]), sb("y_rows", [P, 2, D])
        maski, keep, fill = sb("y_mask", [P, NB, P], I32), sb("y_keep", [P, NB, P]), sb("y_fill", [P, NB, P])
        qT, kT, vall = sb("y_qT", [P, NB * P]), sb("y_kT", [P, NB * P]), sb("y_v", [P, NB, D])
        qTp, kTp = sb("y_qTp", [P, 2, P]), sb("y_kTp", [P, 2, P])
        wt, e = sb("y_wt", [P, 2, YH, P]), sb("y_e", [P, 2, YH, P])
        mx, nmx, ssum, rs = (sb(f"y_{n}", [P, 2, YH]) for n in ("max", "nmax", "sum", "rsum"))
        vn, oT = sb("y_vn", [P, 2, D]), sb("y_oT", [P, 2, P])
        N = Norm(sem, "y")
        in_y, kps, kTr, vps, vr, qps, qTr, xb, kpr, fl = (sem(n) for n in (
            "y_in", "y_k_psum", "y_kT_made", "y_v_psum", "y_v_made", "y_q_psum", "y_qT_made", "y_x_bo", "y_keep_made",
            "y_fill_made"))
        with nc.Block() as block:
            @block.sync
            def _(sp):
                for k, n in enumerate("kvqo"):
                    load(sp, w[:, "qkvo".index(n)], A["y" + "w" + n], in_y)
                load(sp, cols[:, 0:1], A["ybq"], in_y)
                load(sp, cols[:, 1:2], A["ybk"], in_y)
                load(sp, rows[:, 0], A["ybv"].partition_broadcast(P), in_y)
                load(sp, rows[:, 1], A["ybo"].partition_broadcast(P), in_y)
                load(sp, maski[:], A["maskT"], in_y)

            @block.gpsimd
            def _(pool):
                norm_pool(pool, S, N, EPS_OUTER)
                pool.wait_ge(in_y, 16 * 9)
                pool.wait_ge(N.hat, 2)
                pool.tensor_tensor(xres[:], xres[:], rows[:, 1, None, :].broadcast_to([P, NB, D]), ALU.add).then_inc(xb, 1)

            @block.vector
            def _(dve):
                norm_vector(dve, S, N, xres, xhat)
                dve.wait_ge(in_y, 16 * 9)
                for h in range(2):
                    dve.wait_ge(vps, h + 1)
                    dve.tensor_tensor(vall[:, HB * h:HB * h + HB], psum[:, 2 + h].rearrange("p (b d) -> p b d", b=HB),
                                      rows[:, 0, None, :].broadcast_to([P, HB, D]), ALU.add).then_inc(vr, 1)
                dve.tensor_scalar(keep[:], maski[:], 0.0, None, ALU.not_equal).then_inc(kpr, 1)
                dve.wait_ge(kpr, 1)
                dve.tensor_scalar(fill[:], keep[:], -1.0, 1e9, ALU.add, ALU.mult).then_inc(fl, 1)

            @block.tensor
            def _(pe):
                pe.wait_ge(in_y, 16 * 9)
                for h in range(2):
                    pe.matmul(psum[:, h], w[:, 1], S.ctxT[:, h * HALF:(h + 1) * HALF], start=True, stop=True).then_inc(kps, 1)
                for h in range(2):
                    for i in range(HB):
                        b = HB * h + i
                        m = pe.matmul(psum[:, 2 + h, i * P:(i + 1) * P], S.ctxT[:, b * P:(b + 1) * P], w[:, 2], start=True, stop=True)
                    m.then_inc(vps, 1)
                norm_tensor(pe, S, N, 4)
                for h in range(2):
                    pe.wait_ge(N.xT, h + 1)
                    pe.matmul(psum[:, 6 + h], w[:, 0], xT[:, h * HALF:(h + 1) * HALF], start=True, stop=True).then_inc(qps, 1)

            @block.scalar
            def _(act):
                act.wait_ge(in_y, 16 * 9)
                for h in range(2):
                    act.wait_ge(kps, h + 1)
                    act.activation(kT[:, h * HALF:(h + 1) * HALF], psum[:, h], ACT.Identity, bias=cols[:, 1:2]).then_inc(kTr, 1)
                norm_scalar(act, S, N, 4, xT)
                for h in range(2):
                    act.wait_ge(qps, h + 1)
                    act.activation(qT[:, h * HALF:(h + 1) * HALF], psum[:, 6 + h], ACT.Identity, bias=cols[:, 0:1]).then_inc(qTr, 1)

        kpc, qpc, s_in, s_out, flr, mxr, nmr, ex, rsr, vnr, a_in, a_out, y_in, y_out = (sem(n) for n in (
            "yl_kT", "yl_qT", "yl_s_psum", "yl_kept", "yl_filled", "yl_max", "yl_nmax", "yl_e", "yl_rsum", "yl_vn",
            "yl_a_psum", "yl_oT", "yl_y_psum", "yl_x"))
        with nc.Block() as block:
            @block.gpsimd
            def _(pool):
                with pool.Fori(0, NB // 2) as i:
                    b = i * 2
                    pool.wait_ge(s_in, b + 1)
                    for j in range(2):
                        pool.tensor_copy(kTp[:, j], kT[:, bass.ds((b + j) * P, P)]).then_inc(kpc, 1)
                        pool.tensor_copy(qTp[:, j], qT[:, bass.ds((b + j) * P, P)]).then_inc(qpc, 1)

            @block.scalar
            def _(act):
                with act.Fori(0, NB // 2) as i:
                    b = i * 2
                    for j in range(2):
                        act.wait_ge(nmr, b + (j + 1))
                        for h in range(YH):
                            m = act.activation(e[:, j, h], wt[:, j, h], ACT.Exp, bias=nmx[:, j, h:h + 1], accum_out=ssum[:, j, h:h + 1])
                        m.then_inc(ex, 1)
                    for j in range(2):
                        act.wait_ge(a_in, b + (j + 1))
                        act.activation(oT[:, j], psum[:, 4 + 2 * j, 0:P], ACT.Copy).then_inc(a_out, 1)

            @block.vector
            def _(dve):
                with dve.Fori(0, NB // 2) as i:
                    b = i * 2
                    for j in range(2):
                        dve.wait_ge(s_in, b + (j + 2))
                        mask = [t[:, bass.ds(b + j, 1), :].broadcast_to([P, YH, P]) for t in (keep, fill)]
                        dve.scalar_tensor_tensor(out=wt[:, j], in0=psum[:, 0:YH, 0:P], scalar=float(np.float32(YD) ** np.float32(-0.5)),
                                                 in1=mask[0], op0=ALU.mult, op1=ALU.mult).then_inc(s_out, 1)
                        dve.wait_ge(s_out, b + (j + 2))
                        dve.tensor_tensor(wt[:, j], wt[:, j], mask[1], ALU.add).then_inc(flr, 1)
                        dve.wait_ge(flr, b + (j + 1))
                        dve.tensor_reduce(mx[:, j], wt[:, j], AX.X, ALU.max).then_inc(mxr, 1)
                        dve.wait_ge(mxr, b + (j + 1))
                        dve.tensor_scalar(nmx[:, j], mx[:, j], -1.0, None, ALU.mult).then_inc(nmr, 1)
                    for j in range(2):
                        dve.wait_ge(ex, b + (j + 1))
                        dve.reciprocal(rs[:, j], ssum[:, j]).then_inc(rsr, 1)
                        dve.wait_ge(rsr, b + (j + 1))
                        dve.tensor_tensor(vn[:, j].rearrange("p (h d) -> p h d", h=YH),
                                          vall[:, bass.ds(b + j, 1), :].rearrange("p o (h d) -> p (o h) d", h=YH),
                                          rs[:, j, :, None].broadcast_to([P, YH, YD]), ALU.mult).then_inc(vnr, 1)
                    for j in range(2):
                        xb_ = xres[:, bass.ds(b + j, 1), :].rearrange("p o d -> p (o d)")
                        dve.wait_ge(y_in, b + (j + 1))
                        dve.tensor_tensor(xb_, psum[:, 5 + 2 * j, 0:D], xb_, ALU.add).then_inc(y_out, 1)

            @block.tensor
            def _(pe):
                for sem_ in (s_in, s_out, a_out, y_out):
                    pe.sem_inc(sem_, 1)
                with pe.Fori(0, NB // 2) as i:
                    b = i * 2
                    for j in range(2):
                        pe.wait_ge(kpc, b + (j + 1))
                        pe.wait_ge(qpc, b + (j + 1))
                        pe.wait_ge(s_out, b + (j + 1))
                        for h in range(YH):
                            rows_ = slice(YD * h, YD * h + YD)
                            m = pe.matmul(psum[:, h, 0:P], kTp[rows_, j], qTp[rows_, j], start=True, stop=True)
                        m.then_inc(s_in, 1)
                    for j in range(2):
                        pe.wait_ge(vnr, b + (j + 1))
                        pe.wait_ge(a_out, b + 1)
                        for h in range(YH):
                            m = pe.matmul(psum[YD * h:YD * h + YD, 4 + 2 * j, 0:P], vn[:, j, YD * h:YD * h + YD], e[:, j, h],
                                          start=True, stop=True)
                        m.then_inc(a_in, 1)
                    for j in range(2):
                        pe.wait_ge(a_out, b + (j + 2))
                        pe.wait_ge(y_out, b + 1)
                        pe.matmul(psum[:, 5 + 2 * j, 0:D], oT[:, j], w[:, 3], start=True, stop=True).then_inc(y_in, 1)


RE, CAP = 8, 100


def stage_router(nc, S, A):
    psum, ident, xres, xhat, xT = S.psum, S.ident, S.xres, S.xhat, S.xT
    with ExitStack() as c:
        sem = S.sem

        def sb(name, shape, dt=F32):
            return c.enter_context(nc.sbuf_tensor(name, shape, dt))

        wg, we, be = sb("r_wg", [P, RE]), sb("r_we", [P, D]), sb("r_be", [P, D])
        tri, rank = sb("r_tri", [P, P]), sb("r_rank", [P, RE])
        R = sb("r_r", [P, 6, NB, RE])
        r1 = sb("r_1", [P, 6, NB])
        y = sb("r_y", [P, NB, D])
        N = Norm(sem, "r")
        in_r, lg, v, ae, cm, e_in, yr, xr, done = (sem(n) for n in (
            "r_in", "r_logits", "r_chain", "r_exp", "r_count_psum", "r_e_psum", "r_expert", "r_x", "r_stored"))
        with nc.Block() as block:
            @block.sync
            def _(sp):
                load(sp, wg[:], A["rwg"], in_r)
                load(sp, we[:], A["rwe"], in_r)
                load(sp, be[:], A["rbe"].partition_broadcast(P), in_r)
                load(sp, tri[:], A["upto"], in_r)
                load(sp, rank[:], A["rank"].partition_broadcast(P), in_r)
                for h in range(2):
                    t = slice(HB * h, HB * h + HB)
                    sp.wait_ge(xr, h + 1)
                    sp.dma_start(A["out"][:, t], xres[:, t]).then_inc(done, 16)
                sp.wait_ge(done, 32)

            @block.gpsimd
            def _(pool):
                norm_pool(pool, S, N, EPS_OUTER)

            @block.vector
            def _(dve):
                norm_vector(dve, S, N, xres, xhat)
                count = [0]

                def step(m):
                    count[0] += 1
                    m.then_inc(v, 1)
                    dve.wait_ge(v, count[0])

                def bc(a):
                    return a[:, :, None].broadcast_to([P, NB, RE])

                dve.wait_ge(in_r, 80)
                dve.wait_ge(lg, 1)
                lgt = psum[:, 2, 0:NB * RE].rearrange("p (b e) -> p b e", b=NB)
                step(dve.tensor_reduce(r1[:, 0], lgt, AX.X, ALU.max))
                step(dve.tensor_tensor(R[:, 0], lgt, bc(r1[:, 0]), ALU.subtract))
                dve.wait_ge(ae, 1)
                step(dve.tensor_reduce(r1[:, 1], R[:, 0], AX.X, ALU.add))
                step(dve.reciprocal(r1[:, 2], r1[:, 1]))
                step(dve.tensor_tensor(R[:, 1], R[:, 0], bc(r1[:, 2]), ALU.mult))
                step(dve.tensor_reduce(r1[:, 3], R[:, 1], AX.X, ALU.max))
                step(dve.tensor_tensor(R[:, 2], R[:, 1], bc(r1[:, 3]), ALU.is_equal))
                step(dve.tensor_tensor(R[:, 2], R[:, 2], rank[:, None, :].broadcast_to([P, NB, RE]), ALU.mult))
                step(dve.tensor_reduce(r1[:, 4], R[:, 2], AX.X, ALU.max))
                step(dve.tensor_tensor(R[:, 3], R[:, 2], bc(r1[:, 4]), ALU.is_equal))
                dve.wait_ge(cm, 1)
                cnt = psum[:, 3, 0:NB * RE].rearrange("p (b e) -> p b e", b=NB)
                step(dve.tensor_scalar(R[:, 4], cnt, CAP + 0.5, None, ALU.is_lt))
                step(dve.tensor_tensor(R[:, 5], R[:, 4], R[:, 3], ALU.mult))
                step(dve.tensor_reduce(r1[:, 5], R[:, 5], AX.X, ALU.add))
                step(dve.tensor_tensor(r1[:, 4], r1[:, 5], r1[:, 3], ALU.mult))
                for h in range(2):
                    t = slice(HB * h, HB * h + HB)
                    dve.wait_ge(e_in, h + 1)
                    dve.tensor_tensor(y[:, t], psum[:, 4 + h].rearrange("p (b d) -> p b d", b=HB),
                                      be[:, None, :].broadcast_to([P, HB, D]), ALU.add).then_inc(yr, 1)
                    dve.wait_ge(yr, h + 1)
                    for i in range(HB):
                        b = HB * h + i
                        m = dve.scalar_tensor_tensor(out=xres[:, b], in0=y[:, b], scalar=r1[:, 4, b:b + 1], in1=xres[:, b],
                                                     op0=ALU.mult, op1=ALU.add)
                    m.then_inc(xr, 1)

            @block.scalar
            def _(act):
                norm_scalar(act, S, N, 0, xT)
                act.wait_ge(v, 2)
                act.activation(R[:, 0], R[:, 0], ACT.Exp).then_inc(ae, 1)

            @block.tensor
            def _(pe):
                norm_tensor(pe, S, N, 0)
                pe.wait_ge(in_r, 80)
                pe.wait_ge(N.xT, 2)
                for b in range(NB):
                    m = pe.matmul(psum[:, 2, b * RE:(b + 1) * RE], xT[:, b * P:(b + 1) * P], wg[:], start=True, stop=True)
                m.then_inc(lg, 1)
                for h in range(2):
                    for i in range(HB):
                        b = HB * h + i
                        m = pe.matmul(psum[:, 4 + h, i * P:(i + 1) * P], xT[:, b * P:(b + 1) * P], we[:], start=True, stop=True)
                    m.then_inc(e_in, 1)
                pe.wait_ge(v, 10)
                hot = R[:, 3].rearrange("p b e -> p (b e)")
                pe.matmul(psum[:, 3, 0:NB * RE], tri[:], hot, start=True, stop=False, skip_group_check=True)
                for k in range(1, NB):
                    m = pe.matmul(psum[:, 3, k * RE:NB * RE], S.ones[:], hot[:, 0:(NB - k) * RE], start=False,
                                  stop=(k == NB - 1), skip_group_check=True)
                m.then_inc(cm, 1)


def spectral_tables():
    h, d = np.divmod(np.arange(P), QD)
    turns = np.outer(h, h) / QH + np.outer(d, d) / QD
    hartley = np.cos(2 * np.pi * turns) + np.sin(2 * np.pi * turns)
    fs, fh, fd = np.fft.fftfreq(P), np.fft.fftfreq(QH)[h], np.fft.fftfreq(QD)[d]
    km = np.sqrt(fs[None, :] ** 2 + fh[:, None] ** 2 + fd[:, None] ** 2 + 1e-10)
    real = np.cos(np.arctan(np.log(km + 1e-10)))
    s = np.arange(P)
    lam, t = s / P, s * 0.1
    modulation = np.sin(t + lam) * np.cos(t - 2.0 * lam + 0.5 * lam ** 2)
    return hartley.astype(np.float32), (real * (1.0 + 0.1 * modulation) / P).astype(np.float32)


def program(nc, A):
    S = Shared()
    with ExitStack() as ctx:

        def sem(name):
            return ctx.enter_context(nc.semaphore(name))

        def sb(name, shape, dt=F32):
            return ctx.enter_context(nc.sbuf_tensor(name, shape, dt))

        S.sem = lambda name: nc.alloc_semaphore(name=name)
        S.psum = ctx.enter_context(nc.psum_tensor("psum", [P, 8, 512], F32))
        S.xres = sb("xres", [P, NB, D])
        S.xhat = sb("xhat", [P, NB, D])
        S.xT = sb("xT", [P, NB * P])
        S.ident = sb("ident", [P, P])
        S.ones = sb("ones", [P, P])
        S.nhalf = sb("nhalf", [P, NB])
        S.eps = sb("eps", [P, NB])
        S.stats = sb("stats", [P, 2, HB, 6])
        S.mv = sb("mv", [P, 2, HB, 2])
        S.rstd = sb("rstd", [P, 2, HB])
        S.ctxT = sb("ctxT", [P, NB * P])
        S.x0w, S.x0cols, S.x0rows = sb("x0w", [P, 4, D]), sb("x0cols", [P, 2]), sb("x0rows", [P, 2, D])
        S.headmask = sb("headmask", [P, XH])
        S.in_x0 = sem("in_x0")
        for stage in (stage_performer, stage_cross0, stage_moe, stage_layers, stage_cross1, stage_router):
            with nc.cleanup_on_exit():
                stage(nc, S, A)


def lay_out(i):
    c = np.ascontiguousarray
    wq, wk = i["L0_attn_Wq"], i["L0_attn_Wk"]
    r = {
        "x": c(i["x"].transpose(1, 0, 2)),
        "ident": np.eye(P, dtype=np.float32),
        "pwq": c(wq.reshape(D, -1)), "pwk": c(wk.reshape(D, -1)), "pwv": c(i["L0_attn_Wv"].reshape(D, -1)),
        "pwqT": c(wq.reshape(D, NPAIR, P).transpose(2, 1, 0)), "pwkT": c(wk.reshape(D, NPAIR, P).transpose(2, 1, 0)),
        "projT": c(i["L0_attn_proj"].T),
        "pwo": c(i["L0_attn_Wo"].reshape(NPAIR, P, D).transpose(1, 0, 2)),
        "pw1": i["L0_attn_W1"], "pw2": c(i["L0_attn_W2"].reshape(PFB, P, D).transpose(1, 0, 2)),
        "pb1": c(i["L0_attn_b1"].reshape(PFB, P).T), "pb2": i["L0_attn_b2"],
        "pln1g": i["L0_attn_ln1_g"], "pln1b": i["L0_attn_ln1_b"],
        "pln2g": i["L0_attn_ln2_g"], "pln2b": i["L0_attn_ln2_b"],
        "ctxT": c(i["ctx_1024"].transpose(2, 0, 1).reshape(D, -1)),
        "headmask": c(np.repeat(np.eye(XH, dtype=np.float32), XD, 0)),
        "router": i["L0_ffn_router_kernel_DE"],
        "rank": np.arange(ME, 0, -1, dtype=np.float32),
        "mwg": c(i["L0_ffn_kernel_gating_EDF"].transpose(1, 0, 2)), "mwu": c(i["L0_ffn_kernel_up_EDF"].transpose(1, 0, 2)),
        "mwd": c(i["L0_ffn_kernel_down_EFD"].reshape(ME * MFB, P, D).transpose(1, 0, 2)),
    }
    aw = i["L1_attn_attn_w"].reshape(LL, D, QH, 3, QD).transpose(1, 0, 3, 2, 4)
    ab = i["L1_attn_attn_b"].reshape(LL, QH, 3, QD).transpose(0, 2, 1, 3)
    aw, ab = aw[:, :, list(KQV)], ab[:, list(KQV)]
    r["lwqkv"] = c(np.stack([aw, np.roll(aw, 1, axis=3)], 3).reshape(D, LL, -1))
    ab6 = np.stack([ab, np.roll(ab, 1, axis=2)], 2).reshape(LL, NQ, D)
    r["lwp"] = c(i["L1_attn_aproj_w"].transpose(1, 0, 2))
    r["lwf"] = c(i["L1_attn_fc_w"].transpose(1, 0, 2))
    r["lwm"] = c(i["L1_attn_mproj_w"].reshape(LL, LFB, P, D).transpose(2, 0, 1, 3).reshape(P, LL, -1))
    ln = np.stack([i["L1_attn_" + n] for n in ("ln1_w", "ln1_b", "ln2_w", "ln2_b")], 1)
    r["lcols"] = c(np.concatenate([ln, ab6, i["L1_attn_fc_b"].reshape(LL, LFB, P)], 1).transpose(2, 0, 1))
    r["lrows"] = c(np.stack([i["L1_attn_aproj_b"], i["L1_attn_mproj_b"]], 1).reshape(-1))
    r["hartley"], r["filter"] = spectral_tables()
    r["maskT"] = c(i["mask_Bx1xSxS2_ik1"][:, 0].transpose(2, 0, 1))
    for n in "qkvo":
        r["yw" + n] = c(i["L1_xattn_W" + n].T)
        b = i["L1_xattn_b" + n]
        r["yb" + n] = b.reshape(D, 1) if n in "qk" else b
    r["rwg"], r["rwe"], r["rbe"] = i["L1_ffn_w_gate"], i["L1_ffn_w_expert"], i["L1_ffn_b_expert"]
    r["upto"] = np.triu(np.ones((P, P), np.float32))
    for n in "qkvo":
        r["x0w" + n] = c(i["L0_xattn_W" + n].T)
    for n in "qk":
        r["x0b" + n] = i["L0_xattn_b" + n].reshape(D, 1)
    for n in "vo":
        r["x0b" + n] = i["L0_xattn_b" + n]
    return r


def kernel(**inputs):
    import concourse.bacc as bacc
    from concourse.bass_utils import run_bass_kernel_spmd

    nc = bacc.Bacc("TRN2", target_bir_lowering=False, num_devices=1)
    arrays, A = {}, {}
    for name, a in lay_out({k: np.asarray(v) for k, v in inputs.items()}).items():
        a = np.ascontiguousarray(a)
        arrays[f"in_{name}_dram"] = a
        A[name] = nc.dram_tensor(f"in_{name}_dram", a.shape, mybir.dt.from_np(a.dtype), kind="ExternalInput").ap()
    A["out"] = nc.dram_tensor("out_0_dram", (P, NB, D), F32, kind="ExternalOutput").ap()
    program(nc, A)
    r = run_bass_kernel_spmd(nc, [arrays], core_ids=[0])
    return np.ascontiguousarray(r.results[0]["out_0_dram"].transpose(1, 0, 2))
```

```python
from contextlib import ExitStack

import numpy as np

import concourse.bass as bass
from concourse import mybir

F32 = mybir.dt.float32
I32 = mybir.dt.int32
ACT = mybir.ActivationFunctionType
ALU = mybir.AluOpType
AX = mybir.AxisListType

P = 128
NB = 8
HB = NB // 2
D = 128
HALF = HB * P
EPS_OUTER = 1e-5
CROSS0_FILLERS, MOE_FILLERS, ROUTER_FILLERS = 1, 3, 3

PH, PD, PM = 16, 64, 64
NPAIR = PH // 2
VA = PD + 1
PAIR = 2 * VA
DN = float(PD) ** -0.25
EPS_KERN = 1e-6
PF = 512
PFB = PF // P


def load(eng, dst, src, sem):
    eng.dma_start(dst, src).then_inc(sem, 16)


def one(n):
    return slice(n, n + 1) if isinstance(n, int) else bass.ds(n, 1)


def batches(eng, slot):
    slot(0, 0)
    with eng.Fori(0, NB // 2 - 1) as i:
        slot(i * 2 + 1, 1)
        slot(i * 2 + 2, 0)
    slot(NB - 1, 1)
    slot(NB, 0)


def parts(n):
    return (n < NB - 1, n < NB, n > 0) if isinstance(n, int) else (True, True, True)


def keep_warm(pe, S, bank, n):
    for _ in range(n):
        pe.matmul(S.psum[:, bank], S.ident[:], S.ctxT[:, 0:HALF], start=True, stop=True)


class Shared:
    pass


class Norm:

    def __init__(self, sem, name):
        self.stats, self.mv, self.eps, self.rstd, self.hat, self.turned, self.xT = (
            sem(f"{name}_{n}") for n in ("stats", "mv", "var_eps", "rstd", "xhat", "turned", "xT"))


def norm_vector(dve, S, N, src, dst, n0=0):
    for h in range(2):
        for i in range(HB):
            m = dve.bn_stats(S.stats[:, h, i], src[:, HB * h + i])
        m.then_inc(N.stats, 1)
        dve.wait_ge(N.stats, n0 + h + 1)
        for i in range(HB):
            m = dve.bn_aggr(S.mv[:, h, i], S.stats[:, h, i])
        m.then_inc(N.mv, 1)
    for h in range(2):
        dve.wait_ge(N.mv, n0 + h + 1)
        dve.wait_ge(N.rstd, n0 + h + 1)
        for i in range(HB):
            b = HB * h + i
            m = dve.tensor_scalar(dst[:, b], src[:, b], S.mv[:, h, i, 0:1], S.rstd[:, h, i:i + 1],
                                  ALU.subtract, ALU.mult)
        m.then_inc(N.hat, 1)


def norm_pool(pool, S, N, eps, n0=0):
    for h in range(2):
        pool.wait_ge(N.mv, n0 + h + 1)
        pool.tensor_scalar(S.rstd[:, h], S.mv[:, h, :, 1], eps, 1.0, ALU.add, ALU.mult).then_inc(N.eps, 1)
        pool.wait_ge(N.eps, n0 + h + 1)
        pool.tensor_tensor(S.rstd[:, h], S.rstd[:, h], S.nhalf[:, 0:HB], ALU.pow).then_inc(N.rstd, 1)


def norm_tensor(pe, S, N, bank):
    for h in range(2):
        pe.wait_ge(N.hat, h + 1)
        for i in range(HB):
            m = pe.transpose(S.psum[:, bank + h, i * P:(i + 1) * P], S.xhat[:, HB * h + i], S.ident[:])
        m.then_inc(N.turned, 1)


def norm_scalar(act, S, N, bank, dst):
    for h in range(2):
        act.wait_ge(N.turned, h + 1)
        act.activation(dst[:, h * HALF:(h + 1) * HALF], S.psum[:, bank + h], ACT.Copy).then_inc(N.xT, 1)


def stage_performer(nc, S, A):
    with ExitStack() as ctx:
        def sb(name, shape, dt=F32):
            return ctx.enter_context(nc.sbuf_tensor(name, shape, dt))

        sem = S.sem
        psum = S.psum
        xres, xhat, xT, ident, mv, stats = S.xres, S.xhat, S.xT, S.ident, S.mv, S.stats

        wq, wk, wv = (sb(f"p_w{n}", [P, PH * PD]) for n in "qkv")
        wo = sb("p_wo", [P, NPAIR, D])
        w1, w2 = sb("p_w1", [P, PF]), sb("p_w2", [P, PFB, D])
        b1 = sb("p_b1", [P, PFB])
        rows = sb("p_rows", [P, 5, D])
        proj2 = sb("p_proj2", [P, P])
        wdq, wdk = sb("p_wdq", [P, PH * PM]), sb("p_wdk", [P, PH * PM])
        xTp = sb("p_xTp", [P, 2, P])
        vaug = sb("p_vaug", [P, NB, PH, VA])
        ddk = sb("p_ddk", [P, NB, PH * PM])
        sq = sb("p_sq", [P, 2, PH * PD])
        diag = sb("p_diag", [P, 2, PH])
        kmax = sb("p_kmax", [P, NB])
        kmax1 = sb("p_kmax1", [P, 1])
        kmaxn = sb("p_kmaxn", [1, 1])
        nkmax = sb("p_nkmax", [P, 1])
        epsk = sb("p_epsk", [P, 1])
        ones = S.ones

        in_x, in_id, in_row = sem("in_x"), sem("in_ident"), sem("in_rows")
        in_wk, in_wdk, in_wv, in_wq, in_wo, in_ffn = (sem(n) for n in (
            "in_wk", "in_wdk", "in_wv", "in_wq", "in_wo", "in_ffn"))
        with ExitStack() as c2:
            wqT = c2.enter_context(nc.sbuf_tensor("p_wqT", [P, NPAIR, D], F32))
            wkT = c2.enter_context(nc.sbuf_tensor("p_wkT", [P, NPAIR, D], F32))
            cst, dstat, dmv, rstd, hat, tp, xTr = (sem(n) for n in (
                "a_const", "a_stats", "a_mv", "a_rstd", "a_hat", "a_tp", "a_xT"))
            wdp, wde, xtp, k_in, dk_in, v_in, sq_ok, v_ok, red_ok, dk_ok, pchain = (sem(n) for n in (
                "a_wd_psum", "a_wd", "a_xTp", "a_k_psum", "a_dk_psum", "a_v_psum", "a_sq", "a_v", "a_red",
                "a_dk_used", "a_pool"))
            m1, m2, m3, m4, m5 = (sem(n) for n in ("a_max1", "a_maxT", "a_max2", "a_maxbc", "a_max3"))
            kept = dict(wq=wq, wdq=wdq, wo=wo, xTp=xTp, vaug=vaug, ddk=ddk, sq=sq, diag=diag, nkmax=nkmax, epsk=epsk,
                        in_wo=in_wo, in_ffn=in_ffn, in_row=in_row, v_in=v_in, sq_ok=sq_ok, dk_ok=dk_ok, red_ok=red_ok,
                        consts=pchain, negated=m5)
            queries_pool, queries_act, queries_dve, queries_pe = performer_queries(nc, S, c2, kept)
            block = c2.enter_context(nc.Block())

            @block.sync
            def _(sp):
                load(sp, xres[:], A["x"], in_x)
                load(sp, ident[:], A["ident"], in_id)
                load(sp, wkT[:], A["pwkT"], in_wdk)
                sp.wait_ge(cst, 1)
                load(sp, proj2[0:PD, 0:PM], A["projT"], in_wdk)
                load(sp, proj2[PD:P, PM:P], A["projT"], in_wdk)
                load(sp, wk[:], A["pwk"], in_wk)
                load(sp, wv[:], A["pwv"], in_wv)
                load(sp, wqT[:], A["pwqT"], in_wq)
                load(sp, wq[:], A["pwq"], in_wq)
                load(sp, wo[:], A["pwo"], in_wo)
                load(sp, w1[:], A["pw1"], in_ffn)
                load(sp, w2[:], A["pw2"], in_ffn)
                load(sp, b1[:], A["pb1"], in_ffn)
                load(sp, S.ctxT[:], A["ctxT"], S.in_x0)
                for i, n in enumerate("qkvo"):
                    load(sp, S.x0w[:, i], A["x0w" + n], S.in_x0)
                load(sp, S.headmask[:], A["headmask"], S.in_x0)
                load(sp, S.x0cols[:, 0:1], A["x0bq"], S.in_x0)
                load(sp, S.x0cols[:, 1:2], A["x0bk"], S.in_x0)
                load(sp, S.x0rows[:, 0], A["x0bv"].partition_broadcast(P), S.in_x0)
                load(sp, S.x0rows[:, 1], A["x0bo"].partition_broadcast(P), S.in_x0)
                for i, n in enumerate(("pln1g", "pln1b", "pln2g", "pln2b", "pb2")):
                    load(sp, rows[:, i, :], A[n].partition_broadcast(P), in_row)

            @block.gpsimd
            def _(pool):
                pool.memset(proj2[:], 0.0).then_inc(cst, 1)
                pool.memset(ones[:], 1.0).then_inc(pchain, 1)
                pool.memset(S.nhalf[:], -0.5).then_inc(pchain, 1)
                pool.memset(epsk[:], EPS_KERN).then_inc(pchain, 1)
                pool.memset(vaug[:, :, :, PD:VA], 1.0).then_inc(pchain, 1)
                pool.wait_ge(pchain, 4)
                for h in range(2):
                    pool.wait_ge(dmv, h + 1)
                    pool.tensor_scalar(S.rstd[:, h], mv[:, h, :, 1], EPS_OUTER, None, ALU.add).then_inc(pchain, 1)
                    pool.wait_ge(pchain, 5 + h)
                    pool.tensor_tensor(S.rstd[:, h], S.rstd[:, h], S.nhalf[:, 0:HB], ALU.pow).then_inc(rstd, 1)
                with pool.Fori(0, NB // 2) as i:
                    b = i * 2
                    for j in range(2):
                        pool.wait_ge(xTr, 2)
                        pool.wait_ge(v_in, b + (j + 1))
                        pool.tensor_copy(xTp[:, j], xT[:, bass.ds((b + j) * P, P)]).then_inc(xtp, 1)
                queries_pool(pool)

            @block.vector
            def _(dve):
                dve.wait_ge(in_x, 16)
                for h in range(2):
                    for i in range(HB):
                        dve.bn_stats(stats[:, h, i], xres[:, HB * h + i]).then_inc(dstat, 1)
                    dve.wait_ge(dstat, HB * (h + 1))
                    for i in range(HB):
                        m = dve.bn_aggr(mv[:, h, i], stats[:, h, i])
                    m.then_inc(dmv, 1)
                for h in range(2):
                    dve.wait_ge(dmv, h + 1)
                    dve.wait_ge(rstd, h + 1)
                    for i in range(HB):
                        b = HB * h + i
                        m = dve.tensor_scalar(xhat[:, b], xres[:, b], mv[:, h, i, 0:1], S.rstd[:, h, i:i + 1],
                                              ALU.subtract, ALU.mult)
                    m.then_inc(hat, 1)
                dve.sem_inc(red_ok, 2)
                dve.sem_inc(dk_ok, 1)
                with dve.Fori(0, NB // 2) as i:
                    b = i * 2
                    for j in range(2):
                        dve.wait_ge(sq_ok, b + (j + 2))
                        dve.wait_ge(dk_ok, b + (j + 1))
                        dve.tensor_reduce(diag[:, j], sq[:, j].rearrange("p (h d) -> p h d", h=PH), AX.X, ALU.add
                                          ).then_inc(red_ok, 1)
                        dve.wait_ge(dk_in, b + (j + 1))
                        dve.tensor_reduce(kmax[:, bass.ds(b + j, 1)], psum[:, 2:4, :].rearrange("p a n -> p (a n)"), AX.X, ALU.max)
                        dve.wait_ge(red_ok, b + (j + 3))
                        dve.tensor_tensor(ddk[:, bass.ds(b + j, 1), :].rearrange("p o (h m) -> p (o h) m", h=PH),
                                          psum[:, 2:4, :].rearrange("p a (h m) -> p (a h) m", m=PM),
                                          diag[:, j, :, None].broadcast_to([P, PH, PM]),
                                          ALU.subtract).then_inc(dk_ok, 1)
                dve.wait_ge(dk_ok, NB + 1)
                dve.tensor_reduce(kmax1[:], kmax[:], AX.X, ALU.max).then_inc(m1, 1)
                dve.wait_ge(m2, 1)
                dve.tensor_reduce(kmaxn[:], psum[0:1, 6, 0:P], AX.X, ALU.max).then_inc(m3, 1)
                dve.wait_ge(m4, 1)
                dve.tensor_scalar(nkmax[:], psum[:, 7, 0:1], -1.0, None, ALU.mult).then_inc(m5, 1)
                queries_dve(dve)

            @block.tensor
            def _(pe):
                pe.wait_ge(in_id, 16)
                for h in range(2):
                    pe.wait_ge(hat, h + 1)
                    for i in range(HB):
                        m = pe.transpose(psum[:, 6 + h, i * P:(i + 1) * P], xhat[:, HB * h + i], ident[:])
                    m.then_inc(tp, 1)
                pe.wait_ge(in_wdk, 48)
                for n, w in enumerate((wkT, wqT)):
                    if n:
                        pe.wait_ge(in_wq, 32)
                        pe.wait_ge(wde, 1)
                    for q in range(NPAIR):
                        m = pe.matmul(psum[:, q // 4, (q % 4) * P:(q % 4 + 1) * P], w[:, q], proj2[:], start=True, stop=True)
                    m.then_inc(wdp, 1)
                pe.wait_ge(in_wk, 16)
                pe.wait_ge(in_wv, 16)
                pe.wait_ge(wde, 2)
                pe.sem_inc(v_in, 2)
                pe.sem_inc(sq_ok, 1)
                pe.sem_inc(v_ok, 1)
                with pe.Fori(0, NB // 2) as i:
                    b = i * 2
                    for j in range(2):
                        pe.wait_ge(xtp, b + (j + 1))
                        for (w, bank, done, used) in ((wk, 0, k_in, sq_ok), (wdk, 2, dk_in, dk_ok), (wv, 4, v_in, v_ok)):
                            pe.wait_ge(used, b + (j + 1))
                            for n in range(2):
                                m = pe.matmul(psum[:, bank + n, :], xTp[:, j], w[:, n * 512:(n + 1) * 512], start=True, stop=True)
                            m.then_inc(done, 1)
                queries_pe(pe, 0)
                pe.wait_ge(m1, 1)
                pe.transpose(psum[0:1, 6, 0:P], kmax1[:], ident[:]).then_inc(m2, 1)
                queries_pe(pe, 1)
                pe.wait_ge(m3, 1)
                pe.matmul(psum[:, 7, 0:1], ones[0:1, :], kmaxn[:], start=True, stop=True).then_inc(m4, 1)
                queries_pe(pe, 2)

            @block.scalar
            def _(act):
                for h in range(2):
                    act.wait_ge(tp, h + 1)
                    act.activation(xT[:, h * HALF:(h + 1) * HALF], psum[:, 6 + h], ACT.Copy).then_inc(xTr, 1)
                for n, w in enumerate((wdk, wdq)):
                    act.wait_ge(wdp, n + 1)
                    act.activation(w[:], psum[:, 0:2].rearrange("p a n -> p (a n)"), ACT.Copy, scale=DN).then_inc(wde, 1)
                with act.Fori(0, NB // 2) as i:
                    b = i * 2
                    for j in range(2):
                        act.wait_ge(k_in, b + (j + 1))
                        act.wait_ge(red_ok, b + (j + 1))
                        act.activation(sq[:, j], psum[:, 0:2].rearrange("p a n -> p (a n)"), ACT.Square,
                                       scale=DN / 2 ** 0.5).then_inc(sq_ok, 1)
                        act.wait_ge(v_in, b + (j + 3))
                        act.activation(vaug[:, bass.ds(b + j, 1), :, 0:PD].rearrange("p o h d -> p (o h) d"),
                                       psum[:, 4:6].rearrange("p a (h d) -> p (a h) d", d=PD),
                                       ACT.Copy).then_inc(v_ok, 1)
                queries_act(act)
        performer_ffn(nc, S, kept, w1, w2, b1, rows)


def performer_queries(nc, S, ctx, L):
    sem, psum, xhat, xT, ident = S.sem, S.psum, S.xhat, S.xT, S.ident
    wq, wdq, wo = (L[n] for n in ("wq", "wdq", "wo"))
    xTp, vaug, ddk, sq, diag, nkmax, epsk = (L[n] for n in ("xTp", "vaug", "ddk", "sq", "diag", "nkmax", "epsk"))

    def sb(name, shape, dt=F32):
        return ctx.enter_context(nc.sbuf_tensor(name, shape, dt))

    qe = sb("p_qe", [P, 2, PH * PM])
    qfT = sb("p_qfT", [P, 2, NPAIR, P])
    kf = sb("p_kf", [P, 2, PH * PM])
    kvb = sb("p_kvb", [P, 2, NPAIR, PAIR])
    qmax, qtot, rden = sb("p_qmax", [P, 2, PH]), sb("p_qtot", [P, 2, PH]), sb("p_rden", [P, 2, PH])
    att, attT = sb("p_att", [P, 2, PH * PD]), sb("p_attT", [P, 2, NPAIR, P])

    (kvz, xtp, kfe, kfr, q_in, sqr, red, dq_in, qmx, qto, dqs, qex, qft, qfte, kv_in, kvr, num_in, rdn, nrm, att_in,
     atte, wo_in, xo) = (
        sem(n) for n in (
            "b_zeros", "b_xTp", "b_kf_exp", "b_kf", "b_q_psum", "b_sq", "b_diag", "b_dq_psum", "b_qmax", "b_qtot",
            "b_qe", "b_qf", "b_qfT_psum", "b_qfT", "b_kv_psum", "b_kv", "b_num_psum", "b_rden", "b_att",
            "b_attT_psum", "b_attT", "b_wo_psum", "b_x"))

    DQ0, QF0, AT0, NR0, XO0 = 2, 2, 3, 2, 1

    def queries_pool(pool):
        pool.memset(kvb[:], 0.0).then_inc(kvz, 1)
        pool.wait_ge(L["v_in"], NB + 2)
        pool.sem_inc(dq_in, DQ0)
        with pool.Fori(0, NB // 2) as i:
            for j in range(2):
                n = i * 2 + j
                pool.wait_ge(dq_in, n - 1 + DQ0)
                pool.tensor_copy(xTp[:, j], xT[:, bass.ds(n * P, P)]).then_inc(xtp, 1)
                pool.wait_ge(kfe, n + 1)
                pool.tensor_tensor(kf[:, j], kf[:, j], epsk[:].broadcast_to([P, PH * PM]), ALU.add).then_inc(kfr, 1)

    def queries_act(act):
        def exp_k(n, j):
            act.activation(kf[:, j], ddk[:, one(n), :].rearrange("p o n -> p (o n)"), ACT.Exp,
                           bias=nkmax[:]).then_inc(kfe, 1)

        def square_q(n, j):
            act.wait_ge(q_in, n + 1)
            act.activation(sq[:, j], psum[:, 0:2].rearrange("p a n -> p (a n)"), ACT.Square,
                           scale=DN / 2 ** 0.5).then_inc(sqr, 1)

        def exp_q(n, j):
            act.wait_ge(dqs, n + 1)
            act.activation(qe[:, j], qe[:, j], ACT.Exp).then_inc(qex, 1)

        def take_qfT(n, j):
            act.wait_ge(qft, n + 1)
            act.activation(qfT[:, j].rearrange("p q n -> p (q n)"), psum[:, 0:2].rearrange("p a n -> p (a n)"),
                           ACT.Identity, bias=epsk[:]).then_inc(qfte, 1)

        def take_attT(n, j):
            act.wait_ge(att_in, n + 1)
            act.activation(attT[:, j].rearrange("p q n -> p (q n)"),
                           psum[:, 2:4].rearrange("p a n -> p (a n)"), ACT.Copy).then_inc(atte, 1)

        def slot(n, j):
            first, second, last = parts(n)
            if first:
                exp_k(n + 1, 1 - j)
                square_q(n + 1, 1 - j)
            if second:
                take_qfT(n, j)
            if last:
                take_attT(n - 1, 1 - j)
            if first:
                exp_q(n + 1, 1 - j)

        act.wait_ge(L["consts"], 4)
        act.wait_ge(L["red_ok"], NB + 2)
        square_q(0, 0)
        act.wait_ge(L["negated"], 1)
        exp_k(0, 0)
        exp_q(0, 0)
        batches(act, slot)

    def queries_dve(dve):
        def shift_q(n, j):
            dd = psum[:, 2:4, :].rearrange("p a (h m) -> p (a h) m", m=PM)
            dve.wait_ge(sqr, n + 1)
            dve.tensor_reduce(diag[:, j], sq[:, j].rearrange("p (h d) -> p h d", h=PH), AX.X, ALU.add).then_inc(red, 1)
            dve.wait_ge(dq_in, n + 1 + DQ0)
            dve.tensor_reduce(qmax[:, j], dd, AX.X, ALU.max).then_inc(qmx, 1)
            dve.wait_ge(red, n + 1)
            dve.wait_ge(qmx, n + 1)
            dve.tensor_tensor(qtot[:, j], diag[:, j], qmax[:, j], ALU.add).then_inc(qto, 1)
            dve.wait_ge(qto, n + 1)
            dve.tensor_tensor(qe[:, j].rearrange("p (h m) -> p h m", h=PH), dd,
                              qtot[:, j, :, None].broadcast_to([P, PH, PM]), ALU.subtract).then_inc(dqs, 1)

        def take_kv(n, j):
            dve.wait_ge(kv_in, n + 1)
            for lo, c in ((0, 0), (PD, VA)):
                for q, m_, banks in ((0, 3, 2), (6, 2, 1)):
                    m = dve.tensor_copy(
                        kvb[lo:lo + PD, j, q:q + m_ * banks, c:c + VA],
                        psum[lo:lo + PD, 4 + q // 3:4 + q // 3 + banks, 0:m_ * PAIR].rearrange(
                            "p a (q n) -> p (a q) n" if banks == 1 else "p a (q n) -> p a q n", n=PAIR)[..., c:c + VA])
            m.then_inc(kvr, 1)

        def divide(n, j):
            dve.wait_ge(num_in, n + 1)
            two = psum[:, 4:6, 0:3 * PAIR].rearrange("p a (h n) -> p a h n", n=VA)
            single = psum[:, 6, 0:2 * PAIR].rearrange("p (h n) -> p h n", n=VA)
            dve.reciprocal(rden[:, j, 0:12].rearrange("p (a h) -> p a h", a=2), two[:, :, :, PD])
            dve.reciprocal(rden[:, j, 12:16], single[:, :, PD]).then_inc(rdn, 1)
            dve.wait_ge(rdn, n + 1)
            dve.tensor_tensor(att[:, j, 0:12 * PD].rearrange("p (a h d) -> p a h d", a=2, h=6), two[:, :, :, 0:PD],
                              rden[:, j, 0:12, None].rearrange("p (a h) o -> p a h o", a=2).broadcast_to([P, 2, 6, PD]),
                              ALU.mult)
            dve.tensor_tensor(att[:, j, 12 * PD:].rearrange("p (h d) -> p h d", h=4), single[:, :, 0:PD],
                              rden[:, j, 12:16, None].broadcast_to([P, 4, PD]), ALU.mult).then_inc(nrm, 1)

        def add(n):
            x = xhat[:, one(n), :].rearrange("p o d -> p (o d)")
            dve.wait_ge(wo_in, n + 1)
            dve.tensor_tensor(x, psum[:, 7, 0:D], x, ALU.add).then_inc(xo, 1)

        def slot(n, j):
            first, second, last = parts(n)
            if first:
                shift_q(n + 1, 1 - j)
                take_kv(n + 1, 1 - j)
            if second:
                divide(n, j)
            if last:
                add(n - 1)

        dve.wait_ge(kvz, 1)
        shift_q(0, 0)
        take_kv(0, 0)
        batches(dve, slot)

    def queries_pe(pe, part):
        def project(n, j, which=(0, 1)):
            both = ((wq, 0, q_in, qfte, n - 1 + QF0), (wdq, 2, dq_in, atte, n - 2 + AT0))
            for w, bank, done, used, count in both[which[0]:which[-1] + 1]:
                pe.wait_ge(xtp, n + 1)
                pe.wait_ge(used, count)
                for c in range(2):
                    m = pe.matmul(psum[:, bank + c, :], xTp[:, j], w[:, c * 512:(c + 1) * 512], start=True, stop=True)
                m.then_inc(done, 1)

        def begin(part):
            if part == 0:
                pe.sem_inc(qfte, QF0)
                pe.sem_inc(atte, AT0)
                pe.sem_inc(nrm, NR0)
                pe.sem_inc(xo, XO0)
                pe.wait_ge(L["sq_ok"], NB + 1)
            else:
                pe.wait_ge(L["dk_ok"], NB + 1)
                pe.wait_ge(L["in_wo"], 16)
            project(0, 0, (part,))

        def keys_values(n, j):
            pe.wait_ge(kfr, n + 1)
            pe.wait_ge(nrm, n - 1 + NR0)
            for q in range(NPAIR):
                m = pe.matmul(psum[:, 4 + q // 3, (q % 3) * PAIR:(q % 3 + 1) * PAIR], kf[:, j, q * P:(q + 1) * P],
                              vaug[:, one(n), 2 * q:2 * q + 2, :].rearrange("p o h d -> p (o h d)"),
                              start=True, stop=True)
            m.then_inc(kv_in, 1)

        def turn_q(n, j, squared):
            pe.wait_ge(qex, n + 1)
            pe.wait_ge(sqr, squared)
            for q in range(NPAIR):
                m = pe.transpose(psum[:, q // 4, (q % 4) * P:(q % 4 + 1) * P], qe[:, j, q * P:(q + 1) * P], ident[:])
            m.then_inc(qft, 1)

        def numerators(n, j, taken):
            pe.wait_ge(kvr, taken)
            pe.wait_ge(qfte, n + 1 + QF0)
            for q in range(NPAIR):
                m = pe.matmul(psum[:, 4 + q // 3, (q % 3) * PAIR:(q % 3 + 1) * PAIR], qfT[:, j, q], kvb[:, j, q],
                              start=True, stop=True)
            m.then_inc(num_in, 1)

        def turn_att(n, j, shifted):
            pe.wait_ge(nrm, n + 1 + NR0)
            pe.wait_ge(dqs, shifted)
            for q in range(NPAIR):
                m = pe.transpose(psum[:, 2 + q // 4, (q % 4) * P:(q % 4 + 1) * P], att[:, j, q * P:(q + 1) * P], ident[:])
            m.then_inc(att_in, 1)

        def output(n, j):
            pe.wait_ge(atte, n + 1 + AT0)
            pe.wait_ge(xo, n + XO0)
            for q in range(NPAIR):
                m = pe.matmul(psum[:, 7, 0:D], attT[:, j, q], wo[:, q], start=(q == 0), stop=(q == NPAIR - 1))
            m.then_inc(wo_in, 1)

        def slot(n, j):
            first, second, last = parts(n)
            begun = n + 2 if first else NB
            if first:
                project(n + 1, 1 - j)
                keys_values(n + 1, 1 - j)
            if second:
                turn_q(n, j, begun)
            if last:
                turn_att(n - 1, 1 - j, begun)
            if second:
                numerators(n, j, begun)
            if last:
                output(n - 1, 1 - j)

        if part < 2:
            begin(part)
            return
        keys_values(0, 0)
        pe.wait_ge(sqr, 1)
        pe.wait_ge(dqs, 1)
        pe.wait_ge(kvr, 1)
        batches(pe, slot)

    return queries_pool, queries_act, queries_dve, queries_pe


def performer_ffn(nc, S, L, w1, w2, b1, rows):
    sem, psum, xres, xhat, xT, ident = S.sem, S.psum, S.xres, S.xhat, S.xT, S.ident
    stats, mv, rstd = S.stats, S.mv, S.rstd
    EPS = 1e-6
    with ExitStack() as c:
        def sb(name, shape, dt=F32):
            return c.enter_context(nc.sbuf_tensor(name, shape, dt))

        o1b = sb("f_o1b", [P, NB, D])
        hb, he = (L["ddk"][:, n * HB:(n + 1) * HB, :].rearrange("p b (a n) -> p (b a n)", n=HALF).rearrange(
            "p (h f n) -> p h f n", h=2, n=HALF) for n in range(2))
        flat = L["vaug"][:].rearrange("p b h d -> p (b h d)")
        hm, hT = (flat[:, n * NB * HALF:(n + 1) * NB * HALF].rearrange("p (h f n) -> p h f n", h=2, n=HALF) for n in range(2))
        st, mvr, eps_, rs, half1, o1, o1br, tp, o1T, h_in, hbr, hmr, her, hpr, hTr, y_in, x2, half2, nrm, xr = (
            sem(n) for n in (
                "f_stats", "f_mv", "f_var_eps", "f_rstd", "f_ln_half", "f_out1", "f_out1_b2", "f_tp", "f_out1T",
                "f_h_psum", "f_hb", "f_hm", "f_he", "f_hp", "f_hT", "f_y_psum", "f_x2", "f_ln_half2", "f_ln2", "f_x"))
        with nc.Block() as block:
            @block.gpsimd
            def _(pool):
                def rsqrt(n, h):
                    pool.wait_ge(mvr, n + 1)
                    pool.tensor_scalar(rstd[:, h], mv[:, h, :, 1], EPS, 1.0, ALU.add, ALU.mult).then_inc(eps_, 1)
                    pool.wait_ge(eps_, n + 1)
                    pool.tensor_tensor(rstd[:, h], rstd[:, h], S.nhalf[:, 0:HB], ALU.pow).then_inc(rs, 1)

                rsqrt(0, 0)
                rsqrt(1, 1)
                pool.wait_ge(L["in_row"], 80)
                for h in range(2):
                    pool.wait_ge(o1, h + 1)
                    t = slice(HB * h, HB * h + HB)
                    pool.tensor_tensor(o1b[:, t], xhat[:, t], rows[:, 4, None, :].broadcast_to([P, HB, D]), ALU.add
                                       ).then_inc(o1br, 1)
                rsqrt(2, 0)
                rsqrt(3, 1)

            @block.vector
            def _(dve):
                def statistics(n, h, src):
                    for i in range(HB):
                        dve.bn_stats(stats[:, h, i], src[:, HB * h + i]).then_inc(st, 1)
                    dve.wait_ge(st, HB * (n + 1))
                    for i in range(HB):
                        m = dve.bn_aggr(mv[:, h, i], stats[:, h, i])
                    m.then_inc(mvr, 1)

                def normalise(n, h, x, g, half, done):
                    dve.wait_ge(rs, n + 1)
                    dve.wait_ge(mvr, n + 1)
                    for i in range(HB):
                        b = HB * h + i
                        m = dve.scalar_tensor_tensor(out=x[:, b], in0=x[:, b], scalar=mv[:, h, i, 0:1], in1=rows[:, g],
                                                     op0=ALU.subtract, op1=ALU.mult)
                    m.then_inc(half, 1)
                    dve.wait_ge(half, h + 1)
                    for i in range(HB):
                        b = HB * h + i
                        m = dve.scalar_tensor_tensor(out=x[:, b], in0=x[:, b], scalar=rstd[:, h, i:i + 1],
                                                     in1=rows[:, g + 1], op0=ALU.mult, op1=ALU.add)
                    m.then_inc(done, 1)

                def gather(h, f):
                    n = PFB * h + f
                    dve.wait_ge(her, n + 1)
                    dve.wait_ge(hpr, n + 1)
                    dve.tensor_tensor(hT[:, h, f], hb[:, h, f], he[:, h, f], ALU.add).then_inc(hTr, 1)

                statistics(0, 0, xhat)
                statistics(1, 1, xhat)
                dve.wait_ge(L["in_row"], 80)
                normalise(0, 0, xhat, 0, half1, o1)
                normalise(1, 1, xhat, 0, half1, o1)
                for h in range(2):
                    for f in range(PFB):
                        if f:
                            gather(h, f - 1)
                        n = PFB * h + f
                        dve.wait_ge(hbr, n + 1)
                        dve.tensor_scalar(hm[:, h, f], hb[:, h, f], 0.0, None, ALU.min).then_inc(hmr, 1)
                        dve.tensor_scalar(hb[:, h, f], hb[:, h, f], 0.0, -1.0, ALU.max, ALU.add).then_inc(hpr, 1)
                    gather(h, PFB - 1)
                for h in range(2):
                    t = slice(HB * h, HB * h + HB)
                    dve.wait_ge(y_in, h + 1)
                    dve.wait_ge(o1br, h + 1)
                    dve.tensor_tensor(o1b[:, t], psum[:, 6 + h].rearrange("p (b d) -> p b d", b=HB), o1b[:, t], ALU.add
                                      ).then_inc(x2, 1)
                    dve.wait_ge(x2, h + 1)
                    statistics(2 + h, h, o1b)
                for h in range(2):
                    t = slice(HB * h, HB * h + HB)
                    normalise(2 + h, h, o1b, 2, half2, nrm)
                    dve.wait_ge(nrm, h + 1)
                    dve.tensor_tensor(xres[:, t], xres[:, t], o1b[:, t], ALU.add).then_inc(xr, 1)

            @block.tensor
            def _(pe):
                def turn(h):
                    pe.wait_ge(o1, h + 1)
                    for i in range(HB):
                        m = pe.transpose(psum[:, h, i * P:(i + 1) * P], xhat[:, HB * h + i], ident[:])
                    m.then_inc(tp, 1)

                def hidden(h, f):
                    if h:
                        pe.wait_ge(hbr, f + 1)
                    pe.matmul(psum[:, 2 + f], w1[:, f * P:(f + 1) * P], xT[:, h * HALF:(h + 1) * HALF],
                              start=True, stop=True).then_inc(h_in, 1)

                pe.wait_ge(L["in_ffn"], 48)
                pe.wait_ge(S.in_x0, 16 * 10)
                turn(0)
                pe.wait_ge(o1T, 1)
                hidden(0, 0)
                turn(1)
                for f in range(1, PFB):
                    hidden(0, f)
                pe.wait_ge(o1T, 2)
                for f in range(PFB):
                    hidden(1, f)
                for h in range(2):
                    pe.wait_ge(hTr, PFB * (h + 1))
                    for i in range(HB):
                        for f in range(PFB):
                            m = pe.matmul(psum[:, 6 + h, i * P:(i + 1) * P], hT[:, h, f, i * P:(i + 1) * P], w2[:, f],
                                          start=(f == 0), stop=(f == PFB - 1))
                    m.then_inc(y_in, 1)
                for h in range(2):
                    pe.matmul(psum[:, h], S.x0w[:, 1], S.ctxT[:, h * HALF:(h + 1) * HALF], start=True, stop=True
                              ).then_inc(S.k_psum, 1)

            @block.scalar
            def _(act):
                act.wait_ge(L["in_ffn"], 48)
                act.wait_ge(S.in_x0, 16 * 10)
                def take_out1(h):
                    act.wait_ge(tp, h + 1)
                    act.activation(xT[:, h * HALF:(h + 1) * HALF], psum[:, h], ACT.Copy).then_inc(o1T, 1)

                def take_hidden(h, f):
                    act.wait_ge(h_in, PFB * h + f + 1)
                    act.activation(hb[:, h, f], psum[:, 2 + f], ACT.Identity, bias=b1[:, f:f + 1]).then_inc(hbr, 1)

                def exp(h, f):
                    act.wait_ge(hmr, PFB * h + f + 1)
                    act.activation(he[:, h, f], hm[:, h, f], ACT.Exp).then_inc(her, 1)

                take_out1(0)
                take_hidden(0, 0)
                take_out1(1)
                for f in range(1, PFB):
                    take_hidden(0, f)
                    exp(0, f - 1)
                take_hidden(1, 0)
                exp(0, PFB - 1)
                for f in range(1, PFB):
                    take_hidden(1, f)
                    exp(1, f - 1)
                exp(1, PFB - 1)
                for h in range(2):
                    act.wait_ge(S.k_psum, h + 1)
                    act.activation(S.x0kT[:, h * HALF:(h + 1) * HALF], psum[:, h], ACT.Identity, bias=S.x0cols[:, 1:2]
                                   ).then_inc(S.kT_made, 1)


XH, XD = 16, 8
XC = 4
XHC = XH // XC
DIVIDE, TURN_ATT, TAKE_ATT, OUTPUT, RESIDUAL = 1, 3, 2, 4, 3


def stage_cross0(nc, S, A):
    psum, ident, xres, xhat, xT = S.psum, S.ident, S.xres, S.xhat, S.xT
    with ExitStack() as c:
        sem = S.sem

        def sb(name, shape, dt=F32):
            return c.enter_context(nc.sbuf_tensor(name, shape, dt))

        qT, kT = sb("x_qT", [P, NB * P]), S.x0kT
        vall = sb("x_v", [P, NB, XH, XD + 1])
        km = sb("x_km", [P, 2, XH, P])
        qTp = sb("x_qTp", [P, 2, P])
        mx = sb("x_max", [P, 2, XH])
        e, eT = sb("x_e", [P, 2, XH, P]), sb("x_eT", [P, 2, XH, P])
        rden, att, attT = sb("x_rden", [P, 2, XH]), sb("x_att", [P, 2, D]), sb("x_attT", [P, 2, P])
        N = Norm(sem, "x")
        ones_v, vps, vr, qps, qTr, xb = (sem(n) for n in (
            "x_ones", "x_v_psum", "x_v", "x_q_psum", "x_qT", "x_x_bo"))
        kmr, qpr, s_in, mxr, sub, ex, t_in, t_out, o_in, rd, o_out, at_in, at_out, y_in, y_out = (sem(n) for n in (
            "xl_km", "xl_qT", "xl_s_psum", "xl_max", "xl_e_sub", "xl_e", "xl_eT_psum", "xl_eT", "xl_o_psum", "xl_rden",
            "xl_att", "xl_attT_psum", "xl_attT", "xl_y_psum", "xl_x"))
        S0, E0, T0 = 2 * XC, XC, 2

        with nc.Block() as block:
            @block.sync
            def _(sp):
                load_moe(sp, S, A)

            @block.gpsimd
            def _(pool):
                pool.memset(vall[:, :, :, XD:XD + 1], 1.0).then_inc(ones_v, 1)
                norm_pool(pool, S, N, EPS_OUTER)

                pool.sem_inc(s_in, S0)
                pool.wait_ge(S.kT_made, 2)
                pool.wait_ge(S.in_x0, 16 * 10)
                with pool.Fori(0, NB // 2) as i:
                    for j in range(2):
                        n = i * 2 + j
                        pool.wait_ge(s_in, n * XC + XC)
                        pool.tensor_tensor(
                            km[:, j], kT[:, bass.ds(n * P, P)].rearrange("p (o n) -> p o n", o=1).broadcast_to([P, XH, P]),
                            S.headmask[:, :, None].broadcast_to([P, XH, P]), ALU.mult).then_inc(kmr, 1)
                        pool.wait_ge(qTr, 2)
                        pool.tensor_copy(qTp[:, j], qT[:, bass.ds(n * P, P)]).then_inc(qpr, 1)

            @block.vector
            def _(dve):
                norm_vector(dve, S, N, xres, xhat)
                dve.wait_ge(S.in_x0, 16 * 10)
                for h in range(2):
                    dve.wait_ge(vps, h + 1)
                    dve.tensor_tensor(vall[:, HB * h:HB * h + HB, :, 0:XD],
                                      psum[:, 2 + h].rearrange("p (b h d) -> p b h d", b=HB, h=XH),
                                      S.x0rows[:, 0, :].rearrange("p (o h d) -> p o h d", o=1, h=XH).broadcast_to([P, HB, XH, XD]),
                                      ALU.add).then_inc(vr, 1)

                def shift(n, j, k):
                    s = psum[:, k].rearrange("p (h n) -> p h n", h=XHC)
                    dve.wait_ge(s_in, n * XC + (k + 1 + S0))
                    dve.tensor_reduce(mx[:, j, k * XHC:(k + 1) * XHC], s, AX.X, ALU.max).then_inc(mxr, 1)
                    dve.wait_ge(mxr, n * XC + (k + 1))
                    dve.tensor_tensor(e[:, j, k * XHC:(k + 1) * XHC], s,
                                      mx[:, j, k * XHC:(k + 1) * XHC, None].broadcast_to([P, XHC, P]),
                                      ALU.subtract).then_inc(sub, 1)

                def divide(n, j):
                    o = psum[:, 6, 0:XH * (XD + 1)].rearrange("p (h d) -> p h d", h=XH)
                    dve.wait_ge(o_in, n + 1)
                    dve.reciprocal(rden[:, j], o[:, :, XD]).then_inc(rd, 1)
                    dve.wait_ge(rd, n + 1)
                    dve.tensor_tensor(att[:, j].rearrange("p (h d) -> p h d", h=XH), o[:, :, 0:XD],
                                      rden[:, j, :, None].broadcast_to([P, XH, XD]), ALU.mult).then_inc(o_out, 1)

                def residual(n):
                    x = xres[:, one(n), :].rearrange("p o d -> p (o d)")
                    dve.wait_ge(y_in, n + 1)
                    dve.tensor_tensor(x, psum[:, 7, P:2 * P], x, ALU.add).then_inc(y_out, 1)

                def slot(n, j):
                    first, second, last = parts(n)
                    for k in range(XC):
                        if first:
                            shift(n + 1, 1 - j, k)
                        if last:
                            if k == DIVIDE:
                                divide(n - 1, 1 - j)
                            if k == RESIDUAL:
                                residual(n - 1)

                dve.sem_inc(sub, E0)
                dve.wait_ge(N.hat, 2)
                dve.tensor_tensor(xres[:], xres[:], S.x0rows[:, 1, None, :].broadcast_to([P, NB, D]), ALU.add).then_inc(xb, 1)
                dve.wait_ge(xb, 1)
                for k in range(XC):
                    shift(0, 0, k)
                batches(dve, slot)

            @block.scalar
            def _(act):
                act.wait_ge(S.in_x0, 16 * 10)
                norm_scalar(act, S, N, 4, xT)
                for h in range(2):
                    act.wait_ge(qps, h + 1)
                    act.activation(qT[:, h * HALF:(h + 1) * HALF], psum[:, 6 + h], ACT.Identity, bias=S.x0cols[:, 0:1]).then_inc(qTr, 1)

                def exp(n, j, k):
                    act.wait_ge(sub, n * XC + (k + 1 + E0))
                    ap = e[:, j, k * XHC:(k + 1) * XHC]
                    act.activation(ap, ap, ACT.Exp, scale=float(XD) ** -0.5).then_inc(ex, 1)

                def take(n, j, k):
                    act.wait_ge(t_in, n * XC + (k + 1))
                    act.activation(eT[:, j, k * XHC:(k + 1) * XHC].rearrange("p h n -> p (h n)"), psum[:, 4 + k % 2],
                                   ACT.Copy).then_inc(t_out, 1)

                def take_att(n, j):
                    act.wait_ge(at_in, n + 1)
                    act.activation(attT[:, j], psum[:, 7, 0:P], ACT.Copy).then_inc(at_out, 1)

                def slot(n, j):
                    first, second, last = parts(n)
                    for k in range(XC):
                        if second:
                            take(n, j, k)
                        if first:
                            exp(n + 1, 1 - j, k)
                        if k == TAKE_ATT and last:
                            take_att(n - 1, 1 - j)

                for k in range(XC):
                    exp(0, 0, k)
                batches(act, slot)

            @block.tensor
            def _(pe):
                pe.wait_ge(S.in_x0, 16 * 10)
                for h in range(2):
                    for i in range(HB):
                        b = HB * h + i
                        m = pe.matmul(psum[:, 2 + h, i * P:(i + 1) * P], S.ctxT[:, b * P:(b + 1) * P], S.x0w[:, 2],
                                      start=True, stop=True)
                    m.then_inc(vps, 1)
                keep_warm(pe, S, 7, CROSS0_FILLERS)
                norm_tensor(pe, S, N, 4)
                for h in range(2):
                    pe.wait_ge(N.xT, h + 1)
                    pe.matmul(psum[:, 6 + h], S.x0w[:, 0], xT[:, h * HALF:(h + 1) * HALF], start=True, stop=True).then_inc(qps, 1)

                pe.sem_inc(t_out, T0)
                pe.sem_inc(o_out, 1)
                pe.sem_inc(y_out, 1)

                def scores(n, j, k):
                    if k == 0:
                        pe.wait_ge(kmr, n + 1)
                        pe.wait_ge(qpr, n + 1)
                    pe.wait_ge(sub, n * XC + (k + 1))
                    pe.matmul(psum[:, k], qTp[:, j], km[:, j, k * XHC:(k + 1) * XHC].rearrange("p h n -> p (h n)"),
                              start=True, stop=True).then_inc(s_in, 1)

                def turn(n, j, k):
                    pe.wait_ge(ex, n * XC + (k + 1))
                    pe.wait_ge(t_out, n * XC + (k - 1 + T0))
                    for h in range(XHC):
                        m = pe.transpose(psum[:, 4 + k % 2, h * P:(h + 1) * P], e[:, j, k * XHC + h], ident[:])
                    m.then_inc(t_in, 1)

                def values(n, j, first, end):
                    if first == 0:
                        pe.wait_ge(t_out, n * XC + (XC + T0))
                        pe.wait_ge(o_out, n + 1)
                    for h in range(first, end):
                        m = pe.matmul(psum[:, 6, h * (XD + 1):(h + 1) * (XD + 1)], eT[:, j, h],
                                      vall[:, one(n), h].rearrange("p o d -> p (o d)"), start=True, stop=True)
                    if end == XH:
                        m.then_inc(o_in, 1)

                def turn_att(n, j):
                    pe.wait_ge(o_out, n + 2)
                    pe.wait_ge(y_out, n + 1)
                    pe.transpose(psum[:, 7, 0:P], att[:, j], ident[:]).then_inc(at_in, 1)

                def output(n, j):
                    pe.wait_ge(at_out, n + 1)
                    pe.matmul(psum[:, 7, P:2 * P], attT[:, j], S.x0w[:, 3], start=True, stop=True).then_inc(y_in, 1)

                def slot(n, j):
                    first, second, last = parts(n)
                    for k in range(XC):
                        if last:
                            if k == TURN_ATT:
                                turn_att(n - 1, 1 - j)
                            if k == OUTPUT:
                                output(n - 1, 1 - j)
                        if second:
                            turn(n, j, k)
                        if first:
                            scores(n + 1, 1 - j, k)
                        if k < 2 and last:
                            values(n - 1, 1 - j, k * XH // 2, (k + 1) * XH // 2)
                    if OUTPUT == XC and last:
                        output(n - 1, 1 - j)

                pe.wait_ge(vr, 2)
                pe.wait_ge(ones_v, 1)
                pe.wait_ge(qTr, 2)
                for k in range(XC):
                    scores(0, 0, k)
                batches(pe, slot)


ME, MF = 8, 256
MFB = MF // P
MU = 2 * MFB


def load_expert(sp, S, A, e, j):
    for w, n in ((S.m_wg, "mwg"), (S.m_wu, "mwu")):
        sp.dma_start(w[:, j], A[n][:, one(e), :].rearrange("p o f -> p (o f)")).then_inc(S.in_expert[j], 16)


def load_moe(sp, S, A):
    load(sp, S.m_router[:], A["router"], S.in_router)
    load(sp, S.m_rank[:], A["rank"].partition_broadcast(P), S.in_router)
    for j in range(2):
        load_expert(sp, S, A, j, j)
    load(sp, S.m_wd[:], A["mwd"], S.in_wd)


def stage_moe(nc, S, A):
    psum, xres, xhat, xT = S.psum, S.xres, S.xhat, S.xT
    with ExitStack() as c:
        sem = S.sem

        def sb(name, shape, dt=F32):
            return c.enter_context(nc.sbuf_tensor(name, shape, dt))

        router, rank, wg, wu, wd = S.m_router, S.m_rank, S.m_wg, S.m_wu, S.m_wd
        R = sb("m_r", [P, 8, NB, ME])
        r1 = sb("m_r1", [P, 8, NB])
        sg, fT = sb("m_sg", [P, 2, HALF]), sb("m_fT", [P, 2, MU, HALF])
        N = Norm(sem, "m")
        lg, v, ae = (sem(n) for n in ("m_logits", "m_route", "m_exp"))
        gu, sgr, fr, dn, added = (sem(n) for n in ("m_gu_psum", "m_silu", "m_fused", "m_down_psum", "m_added"))
        F0, ADD0 = 2, 4

        def flat(t):
            return t.rearrange("p b e -> p (b e)")

        with nc.Block() as block:
            @block.sync
            def _(sp):
                load_layers(sp, S, A)
                with sp.Fori(1, ME // 2) as i:
                    for j in range(2):
                        sp.wait_ge(gu, (i * 2 + j - 1) * MU)
                        load_expert(sp, S, A, i * 2 + j, j)

            @block.gpsimd
            def _(pool):
                norm_pool(pool, S, N, EPS_OUTER)

            @block.scalar
            def _(act):
                def silu(e, n):
                    act.wait_ge(gu, e * MU + (n + 1))
                    act.wait_ge(fr, e * MU + (n - 1 + F0))
                    act.activation(sg[:, n % 2], psum[:, n % 2], ACT.Silu).then_inc(sgr, 1)

                norm_scalar(act, S, N, 0, xT)
                act.wait_ge(v, 2)
                act.activation(flat(R[:, 0]), flat(R[:, 0]), ACT.Exp).then_inc(ae, 1)
                for n in range(2):
                    silu(0, n)
                act.wait_ge(v, 17)
                act.activation(r1[:, 5], r1[:, 4], ACT.Exp).then_inc(ae, 1)
                for n in range(2, MU):
                    silu(0, n)

                def slot(e, j):
                    if parts(e)[0]:
                        for n in range(MU):
                            silu(e + 1, n)

                batches(act, slot)

            @block.vector
            def _(dve):
                norm_vector(dve, S, N, xres, xhat)
                count = [0]

                def step(m):
                    count[0] += 1
                    m.then_inc(v, 1)
                    dve.wait_ge(v, count[0])

                def bc(a):
                    return a[:, :, None].broadcast_to([P, NB, ME])

                def fuse(e, j, n):
                    dve.wait_ge(sgr, e * MU + (n + 1))
                    dve.tensor_tensor(fT[:, j, n], sg[:, n % 2], psum[:, 2 + n % 2], ALU.mult).then_inc(fr, 1)

                def add(e, j, h):
                    dve.wait_ge(dn, e * 2 + (h + 1))
                    dve.wait_ge(added, e * 2 + (h - 1 + ADD0))
                    for q in range(HB):
                        b = HB * h + q
                        m = dve.scalar_tensor_tensor(out=xres[:, b], in0=psum[:, 4 + 2 * j + h, q * P:(q + 1) * P],
                                                     scalar=R[:, 7, b, one(e)], in1=xres[:, b], op0=ALU.mult, op1=ALU.add)
                    m.then_inc(added, 1)

                dve.sem_inc(added, ADD0)
                dve.wait_ge(lg, 1)
                dve.wait_ge(S.in_router, 32)
                lgt = psum[:, 7, 0:NB * ME].rearrange("p (b e) -> p b e", b=NB)
                rk = rank[:, None, :].broadcast_to([P, NB, ME])
                step(dve.tensor_reduce(r1[:, 0], lgt, AX.X, ALU.max))
                step(dve.tensor_tensor(R[:, 0], lgt, bc(r1[:, 0]), ALU.subtract))
                dve.wait_ge(ae, 1)
                step(dve.tensor_reduce(r1[:, 1], R[:, 0], AX.X, ALU.add))
                step(dve.reciprocal(r1[:, 2], r1[:, 1]))
                step(dve.tensor_tensor(R[:, 1], R[:, 0], bc(r1[:, 2]), ALU.mult))
                for k in range(2):
                    pr, first = R[:, 1 + 3 * k], R[:, 3 + 3 * k]
                    step(dve.tensor_reduce(r1[:, 3 + 3 * k], pr, AX.X, ALU.max))
                    step(dve.tensor_tensor(R[:, 2 + 3 * k], pr, bc(r1[:, 3 + 3 * k]), ALU.is_equal))
                    step(dve.tensor_tensor(R[:, 2 + 3 * k], R[:, 2 + 3 * k], rk, ALU.mult))
                    step(dve.tensor_reduce(r1[:, 7], R[:, 2 + 3 * k], AX.X, ALU.max))
                    step(dve.tensor_tensor(first, R[:, 2 + 3 * k], bc(r1[:, 7]), ALU.is_equal))
                    if k == 0:
                        step(dve.scalar_tensor_tensor(out=flat(R[:, 4]), in0=flat(first), scalar=-2.0, in1=flat(pr),
                                                      op0=ALU.mult, op1=ALU.add))
                    fuse(0, 0, k)
                step(dve.tensor_tensor(r1[:, 4], r1[:, 6], r1[:, 3], ALU.subtract))
                assert count[0] == 17
                dve.wait_ge(ae, 2)
                step(dve.tensor_scalar(r1[:, 0], r1[:, 5], 1.0, None, ALU.add))
                step(dve.reciprocal(r1[:, 1], r1[:, 0]))
                step(dve.tensor_tensor(r1[:, 2], r1[:, 5], r1[:, 1], ALU.mult))
                for n in range(2, MU):
                    fuse(0, 0, n)
                step(dve.tensor_tensor(R[:, 3], R[:, 3], bc(r1[:, 1]), ALU.mult))
                step(dve.tensor_tensor(R[:, 6], R[:, 6], bc(r1[:, 2]), ALU.mult))
                step(dve.tensor_tensor(R[:, 7], R[:, 3], R[:, 6], ALU.add))

                def slot(e, j):
                    first, second, last = parts(e)
                    for n in range(MU):
                        if first:
                            fuse(e + 1, 1 - j, n)
                        if second and n % 2:
                            add(e, j, n // 2)

                batches(dve, slot)

            @block.tensor
            def _(pe):
                def up(e, j, n):
                    fb, h = n // 2, n % 2
                    if n == 0:
                        pe.wait_ge(S.in_expert[j], (e - j) * 16 + 32)
                    pe.wait_ge(fr, e * MU + (n - 1 + F0))
                    pe.matmul(psum[:, h], wg[:, j, fb * P:(fb + 1) * P], xT[:, h * HALF:(h + 1) * HALF], start=True, stop=True)
                    pe.matmul(psum[:, 2 + h], wu[:, j, fb * P:(fb + 1) * P], xT[:, h * HALF:(h + 1) * HALF],
                              start=True, stop=True).then_inc(gu, 1)

                def down(e, j, h):
                    pe.wait_ge(fr, e * MU + (MU - 1 + h + F0))
                    pe.wait_ge(added, e * 2 + (h - 3 + ADD0))
                    for q in range(HB):
                        for fb in range(MFB):
                            m = pe.matmul(psum[:, 4 + 2 * j + h, q * P:(q + 1) * P], fT[:, j, 2 * fb + h, q * P:(q + 1) * P],
                                          wd[:, one(e * MFB + fb), :].rearrange("p o d -> p (o d)"),
                                          start=(fb == 0), stop=(fb == MFB - 1))
                    m.then_inc(dn, 1)

                keep_warm(pe, S, 7, MOE_FILLERS)
                norm_tensor(pe, S, N, 0)
                pe.sem_inc(fr, F0)
                pe.wait_ge(S.in_router, 32)
                pe.wait_ge(N.xT, 2)
                for b in range(NB):
                    m = pe.matmul(psum[:, 7, b * ME:(b + 1) * ME], xT[:, b * P:(b + 1) * P], router[:], start=True, stop=True)
                m.then_inc(lg, 1)
                for n in range(MU):
                    up(0, 0, n)
                pe.wait_ge(S.in_wd, 16)
                pe.wait_ge(v, 2)

                def slot(e, j):
                    first, second, last = parts(e)
                    for n in range(MU):
                        if first:
                            up(e + 1, 1 - j, n)
                        if second and n % 2:
                            down(e, j, n // 2)

                batches(pe, slot)


LL = 4
QH, QD = 16, 8
LF = 512
LFB = LF // P
NQ = 6
KQV = (1, 0, 2)
EPS_L1 = 1e-5
ROUND = 1.5 * 2.0 ** 23
LW1, LB1, LW2, LB2, LQB, LFC = 0, 1, 2, 3, 4, 4 + NQ
LCOLS = LFC + LFB
STEPS = 11
WARM0, WARM = 2, 5
CUT = 8
POOL_COLS = 144


def load_layers(sp, S, A):
    load(sp, S.l_cols[:], A["lcols"], S.in_l)
    load(sp, S.hart[:], A["hartley"], S.in_l)
    load(sp, S.filt[:], A["filter"], S.in_l)
    load(sp, S.l_rows[:].rearrange("p l k d -> p (l k d)"), A["lrows"].partition_broadcast(P), S.in_l)
    load(sp, S.wqkv[:].rearrange("p a b -> p (a b)"), A["lwqkv"][:, 0], S.in_wqkv)
    load(sp, S.wp[:], A["lwp"], S.in_wp)
    load(sp, S.wf[:], A["lwf"][:, 0], S.in_wf)
    load(sp, S.wm[:].rearrange("p a b -> p (a b)"), A["lwm"].rearrange("p l n -> p (l n)"), S.in_wm)


def stage_layers(nc, S, A):
    psum, ident, xres, xhat = S.psum, S.ident, S.xres, S.xhat
    with ExitStack() as c:
        sem = S.sem

        def sb(name, shape, dt=F32):
            return c.enter_context(nc.sbuf_tensor(name, shape, dt))

        def pair(name):
            return [sem(f"l_{name}{h}") for h in range(2)]

        wqkv, wf, wp, wm, cols, rows, hart, filt = S.wqkv, S.wf, S.wp, S.wm, S.l_cols, S.l_rows, S.hart, S.filt
        in_c, in_q, in_p, in_f, in_m = S.in_l, S.in_wqkv, S.in_wp, S.in_wf, S.in_wm
        wc = sb("l_wc", [P, LL, D])
        colA, colF = sb("l_col_a", [P, LCOLS]), sb("l_col_f", [P, LCOLS])
        hneg = sb("l_hneg", [P, P])
        halfpi, rnd = sb("l_halfpi", [P, 1]), sb("l_round", [P, 2])
        xl = sb("l_x", [P, NB, D])
        xnT = sb("l_xnT", [P, 2, HALF])
        Q = sb("l_q", [P, 2, 4, 3, HALF])
        R, T = sb("l_r", [P, 2, 4, HALF]), sb("l_t", [P, 3, 4, HALF])
        z = sb("l_z", [P, 2, HALF])
        gT = sb("l_g", [P, 2, LFB, HALF])
        N0 = Norm(sem, "l0")
        N = [Norm(sem, f"l{h}") for h in (1, 2)]
        cst, neg, wc_in, wc_out, hv, hp, col_a, col_f, last = (sem(f"l_{n}") for n in (
            "const", "hneg_made", "wc_psum", "wc_made",
            "ham_vector", "ham_pool", "columns_a", "columns_f", "x_out"))
        q_in, q_out, rr, kk, red, absd, cosd, dif = (pair(n) for n in (
            "q_psum", "q_taken", "turns_t", "turns", "reduced", "abs", "cos", "diff"))
        f_in, f_out, p_in, x1, xb, h_in, g_out, y_in, x2, xb2 = (pair(n) for n in (
            "hart_psum", "z_made", "proj_psum", "x1", "x_bias", "h_psum", "gelu", "y_psum", "x2", "x_bias2"))

        def layers(eng, half_step):
            half_step(0, 0, None, None)
            half_step(1, 0, 0, 0)
            with eng.Fori(1, LL) as l:
                half_step(0, l, 1, l - 1)
                half_step(1, l, 0, l)
            half_step(None, None, 1, LL - 1)

        with nc.Block() as block:
            @block.sync
            def _(sp):
                load_cross1(sp, S, A)
                load_router(sp, S, A)
                with sp.Fori(1, LL) as l:
                    sp.wait_ge(q_in[1], l * NQ)
                    sp.dma_start(wqkv[:].rearrange("p a b -> p (a b)"),
                                 A["lwqkv"][:, bass.ds(l, 1), :].rearrange("p o f -> p (o f)")).then_inc(in_q, 16)
                    sp.wait_ge(h_in[1], l * LFB)
                    sp.dma_start(wf[:], A["lwf"][:, bass.ds(l, 1), :].rearrange("p o f -> p (o f)")).then_inc(in_f, 16)

            def hamilton(eng, h, lo, hi, base, done):
                n = hi - lo
                a, b, v = (Q[:, h, :, k, lo:hi] for k in range(3))
                r = R[:, h, :, lo:hi]
                t = [T[:, i, :, lo:hi] for i in range(3)]

                def sq(x):
                    return x.rearrange("p (s c) n -> p s c n", s=2)

                def bc(i, shape):
                    x = a[:, i]
                    return (x[:, None, :] if len(shape) == 3 else x[:, None, None, :]).broadcast_to(shape)

                four, two = [P, 4, n], [P, 2, 2, n]
                steps = (
                    (r, bc(0, four), b, ALU.mult, 0),
                    (sq(t[0]), bc(1, two), sq(b)[:, :, ::-1], ALU.mult, 0),
                    (sq(t[1]), bc(2, two), sq(b)[:, ::-1], ALU.mult, 0),
                    (r[:, 0:4:2], r[:, 0:4:2], t[0][:, 0:4:2], ALU.subtract, 2),
                    (r[:, 1:4:2], r[:, 1:4:2], t[0][:, 1:4:2], ALU.add, 2),
                    (t[2], bc(3, four), b[:, ::-1], ALU.mult, 0),
                    (r[:, 0:4:3], r[:, 0:4:3], t[1][:, 0:4:3], ALU.subtract, 5),
                    (r[:, 1:3], r[:, 1:3], t[1][:, 1:3], ALU.add, 5),
                    (r[:, 0:2], r[:, 0:2], t[2][:, 0:2], ALU.subtract, 8),
                    (r[:, 2:4], r[:, 2:4], t[2][:, 2:4], ALU.add, 8),
                    (r, r, v, ALU.mult, 10))

                def run(first, end):
                    for out, x, y, op, after in steps[first:end]:
                        if after:
                            eng.wait_ge(done, base + after)
                        eng.tensor_tensor(out, x, y, op).then_inc(done, 1)

                return run

            @block.gpsimd
            def _(pool):
                norm_pool(pool, S, N0, EPS_OUTER)
                pool.memset(halfpi[:], float(np.pi / 2)).then_inc(cst, 1)
                pool.memset(rnd[:, 0:1], ROUND).then_inc(cst, 1)
                pool.memset(rnd[:, 1:2], -ROUND).then_inc(cst, 1)
                pool.memset(S.eps[:], EPS_L1).then_inc(cst, 1)
                for h in range(2):
                    for k in range(3):
                        pool.memset(Q[:, h, 1, k].rearrange("p (b n) -> p b n", n=P)[:, :, 0:1], 0.0).then_inc(cst, 1)
                pool.wait_ge(cst, 10)

                def rsqrt(h, l, i):
                    pool.wait_ge(N[h].mv, l * 2 + (i + 1))
                    pool.tensor_tensor(S.rstd[:, h], S.mv[:, h, :, 1], S.eps[:, 0:HB], ALU.add).then_inc(N[h].eps, 1)
                    pool.wait_ge(N[h].eps, l * 2 + (i + 1))
                    pool.tensor_tensor(S.rstd[:, h], S.rstd[:, h], S.nhalf[:, 0:HB], ALU.pow).then_inc(N[h].rstd, 1)

                def add_bias(h, l, i, done):
                    pool.wait_ge(in_c, 64)
                    pool.wait_ge(N[h].hat, l * 2 + (i + 1))
                    x = xl[:, HB * h:HB * h + HB]
                    row = rows[:, l, i, None, :] if isinstance(l, int) else rows[:, bass.ds(l, 1), i, :]
                    pool.tensor_tensor(x, x, row.broadcast_to([P, HB, D]), ALU.add).then_inc(done[h], 1)

                def quaternions(h, l):
                    pool.wait_ge(cosd[h], l * 3 + 1)
                    pool.wait_ge(dif[h], l * 3 + 2)
                    pool.wait_ge(q_out[h], l * NQ + 4)

                def half_step(h, l, o, m):
                    if h is not None:
                        add_bias(h, l, 0, xb)
                    if o is not None:
                        rsqrt(o, m, 1)
                        add_bias(o, m, 1, xb2)
                    if h is None:
                        return
                    ham = hamilton(pool, h, HALF - POOL_COLS, HALF, l * (2 * STEPS) + h * STEPS, hp)
                    quaternions(h, l)
                    ham(0, 5)
                    pool.wait_ge(cosd[h], l * 3 + 2)
                    ham(5, 10)
                    pool.wait_ge(dif[h], l * 3 + 3)
                    pool.wait_ge(cosd[h], l * 3 + 3)
                    ham(10, STEPS)
                    if o is not None:
                        rsqrt(o, m + 1, 0)

                rsqrt(0, 0, 0)
                rsqrt(1, 0, 0)
                layers(pool, half_step)

            @block.vector
            def _(dve):
                norm_vector(dve, S, N0, xres, xl)
                dve.wait_ge(in_c, 64)
                dve.tensor_scalar(hneg[:], hart[:], -1.0, None, ALU.mult).then_inc(neg, 1)
                dve.wait_ge(cst, 10)
                dve.wait_ge(N0.hat, 2)

                def statistics(h):
                    for k in range(HB):
                        m = dve.bn_stats(S.stats[:, h, k], xl[:, HB * h + k])
                    dve.drain()
                    for k in range(HB):
                        m = dve.bn_aggr(S.mv[:, h, k], S.stats[:, h, k])
                    m.then_inc(N[h].mv, 1)

                def normalise(h, l, i):
                    dve.wait_ge(N[h].mv, l * 2 + (i + 1))
                    dve.wait_ge(N[h].rstd, l * 2 + (i + 1))
                    for k in range(HB):
                        b = HB * h + k
                        m = dve.tensor_scalar(xhat[:, b], xl[:, b], S.mv[:, h, k, 0:1], S.rstd[:, h, k:k + 1],
                                              ALU.subtract, ALU.mult)
                    m.then_inc(N[h].hat, 1)

                def reduce(h, l, n):
                    k = KQV[n]
                    dve.wait_ge(kk[h], l * 3 + (n + 1))
                    dve.scalar_tensor_tensor(out=Q[:, h, 3, k], in0=Q[:, h, 3, k], scalar=-2.0 * float(np.pi),
                                             in1=Q[:, h, 0, k], op0=ALU.mult, op1=ALU.add).then_inc(red[h], 1)

                def differ(h, l, n):
                    x, y = (Q[:, h, c_, KQV[n]].rearrange("p (b n) -> p b n", n=P) for c_ in range(2))
                    dve.wait_ge(q_out[h], l * NQ + (2 * n + 1))
                    dve.tensor_tensor(y[:, :, 1:P], x[:, :, 1:P], x[:, :, 0:P - 1], ALU.subtract).then_inc(dif[h], 1)

                def filtered(h, l):
                    dve.wait_ge(f_in[h], l + 1)
                    dve.tensor_tensor(z[:, h].rearrange("p (b n) -> p b n", n=P),
                                      psum[:, 7].rearrange("p (b n) -> p b n", n=P),
                                      filt[:, None, :].broadcast_to([P, HB, P]), ALU.mult).then_inc(f_out[h], 1)

                def residual(h, l, bank, got, biased, done):
                    x = xl[:, HB * h:HB * h + HB]
                    dve.wait_ge(got[h], l + 1)
                    dve.wait_ge(biased[h], l + 1)
                    dve.tensor_tensor(x, psum[:, bank].rearrange("p (b d) -> p b d", b=HB), x, ALU.add).then_inc(done[h], 1)
                    dve.wait_ge(done[h], l + 1)

                def half_step(h, l, o, m):
                    if h is not None:
                        differ(h, l, 0)
                        reduce(h, l, 0)
                    if o is not None:
                        filtered(o, m)
                        residual(o, m, 7, p_in, xb, x1)
                        statistics(o)
                    if h is not None:
                        ham = hamilton(dve, h, 0, HALF - POOL_COLS, l * (2 * STEPS) + h * STEPS, hv)
                        dve.wait_ge(cosd[h], l * 3 + 1)
                        dve.wait_ge(dif[h], l * 3 + 1)
                        dve.wait_ge(q_out[h], l * NQ + 3)
                        ham(0, 1)
                    if o is not None:
                        normalise(o, m, 1)
                    if h is None:
                        residual(o, m, 0, y_in, xb2, x2)
                        return
                    reduce(h, l, 1)
                    differ(h, l, 1)
                    reduce(h, l, 2)
                    dve.wait_ge(dif[h], l * 3 + 2)
                    dve.wait_ge(q_out[h], l * NQ + 4)
                    ham(1, 3)
                    differ(h, l, 2)
                    ham(3, 5)
                    dve.wait_ge(cosd[h], l * 3 + 2)
                    ham(5, CUT)
                    if o is not None:
                        residual(o, m, 0, y_in, xb2, x2)
                        statistics(o)
                    ham(CUT, 10)
                    dve.wait_ge(dif[h], l * 3 + 3)
                    dve.wait_ge(cosd[h], l * 3 + 3)
                    if o is not None:
                        normalise(o, m + 1, 0)
                    ham(10, STEPS)

                for h in range(2):
                    statistics(h)
                for h in range(2):
                    normalise(h, 0, 0)
                layers(dve, half_step)
                for h in range(2):
                    t = slice(HB * h, HB * h + HB)
                    m = dve.tensor_tensor(xres[:, t], xres[:, t], xl[:, t], ALU.add)
                m.then_inc(last, 1)

            @block.scalar
            def _(act):
                act.wait_ge(cst, 10)
                act.wait_ge(in_c, 64)
                act.wait_ge(wc_in, 1)
                act.activation(wc[:].rearrange("p l d -> p (l d)"), psum[:, 7], ACT.Copy).then_inc(wc_out, 1)

                def columns(l, dst, done):
                    act.drain()
                    src = cols[:, l, :] if isinstance(l, int) else cols[:, bass.ds(l, 1), :].rearrange("p o k -> p (o k)")
                    act.activation(dst[:], src, ACT.Copy).then_inc(done, 1)
                    act.wait_ge(done, l + 1)

                def take_norm(h, l, i):
                    col, w, b = ((colA, LW1, LB1), (colF, LW2, LB2))[i]
                    act.wait_ge(N[h].turned, l * 2 + (i + 1))
                    act.activation(xnT[:, h], psum[:, 0], ACT.Identity, scale=col[:, w:w + 1], bias=col[:, b:b + 1]
                                   ).then_inc(N[h].xT, 1)

                def take_q(h, l, n):
                    act.wait_ge(q_in[h], l * NQ + (n + 1))
                    act.activation(Q[:, h, 2 * (n % 2), KQV[n // 2]], psum[:, 1 + n % 3], ACT.Identity,
                                   bias=colA[:, LQB + n:LQB + n + 1]).then_inc(q_out[h], 1)

                def turns(h, l, n):
                    x, y = Q[:, h, 0, KQV[n]], Q[:, h, 3, KQV[n]]
                    act.wait_ge(q_out[h], l * NQ + (2 * n + 1))
                    act.activation(y, x, ACT.Identity, scale=float(0.5 / np.pi), bias=rnd[:, 0:1]).then_inc(rr[h], 1)
                    act.wait_ge(rr[h], l * 3 + (n + 1))
                    act.activation(y, y, ACT.Identity, bias=rnd[:, 1:2]).then_inc(kk[h], 1)

                def cosine(h, l, n):
                    y = Q[:, h, 3, KQV[n]]
                    act.wait_ge(red[h], l * 3 + (n + 1))
                    act.activation(y, y, ACT.Abs).then_inc(absd[h], 1)
                    act.wait_ge(absd[h], l * 3 + (n + 1))
                    act.activation(y, y, ACT.Sin, scale=-1.0, bias=halfpi[:]).then_inc(cosd[h], 1)

                def gelu(h, l):
                    for f in range(LFB):
                        act.wait_ge(h_in[h], l * LFB + (f + 1))
                        act.activation(gT[:, h, f], psum[:, 4 + f % 3], ACT.Gelu, bias=colF[:, LFC + f:LFC + f + 1]
                                       ).then_inc(g_out[h], 1)

                def half_step(h, l, o, m):
                    if h == 0:
                        columns(l, colA, col_a)
                    if o == 0:
                        columns(m, colF, col_f)
                    if h is not None:
                        take_norm(h, l, 0)
                        take_q(h, l, 0)
                        turns(h, l, 0)
                        take_q(h, l, 1)
                        cosine(h, l, 0)
                        take_q(h, l, 2)
                        take_q(h, l, 3)
                        turns(h, l, 1)
                        take_q(h, l, 4)
                        turns(h, l, 2)
                        take_q(h, l, 5)
                    if o is not None:
                        take_norm(o, m, 1)
                    if h is not None:
                        cosine(h, l, 1)
                    if o is not None:
                        gelu(o, m)
                    if h is not None:
                        cosine(h, l, 2)

                layers(act, half_step)

            @block.tensor
            def _(pe):
                pe.wait_ge(in_c, 64)
                pe.wait_ge(neg, 1)
                pe.wait_ge(in_p, 16)
                for l in range(LL):
                    m = pe.matmul(psum[:, 7, l * D:(l + 1) * D], hart[:], wp[:, l], start=True, stop=True)
                m.then_inc(wc_in, 1)

                def turn(h, l, i):
                    pe.wait_ge(N[h].hat, l * 2 + (i + 1))
                    for k in range(HB):
                        m = pe.transpose(psum[:, 0, k * P:(k + 1) * P], xhat[:, HB * h + k], ident[:])
                    m.then_inc(N[h].turned, 1)

                def project(h, l, first, end):
                    for k in range(first, end):
                        if k >= 3:
                            pe.wait_ge(q_out[h], l * NQ + (k - 2))
                        pe.matmul(psum[:, 1 + k % 3], wqkv[:, k], xnT[:, h], start=True, stop=True).then_inc(q_in[h], 1)

                def hartley(h, l):
                    pe.wait_ge(hv, l * (2 * STEPS) + STEPS * (h + 1))
                    pe.wait_ge(hp, l * (2 * STEPS) + STEPS * (h + 1))
                    for k in range(4):
                        m = pe.matmul(psum[:, 7], (hneg if k else hart)[:], R[:, h, k], start=(k == 0), stop=(k == 3))
                    m.then_inc(f_in[h], 1)

                def out(h, l):
                    w = wc[:, l] if isinstance(l, int) else wc[:, bass.ds(l, 1), :].rearrange("p o d -> p (o d)")
                    pe.wait_ge(f_out[h], l + 1)
                    for k in range(HB):
                        m = pe.matmul(psum[:, 7, k * P:(k + 1) * P], z[:, h, k * P:(k + 1) * P], w, start=True, stop=True)
                    m.then_inc(p_in[h], 1)

                def fc(h, l):
                    pe.wait_ge(N[h].xT, l * 2 + 2)
                    pe.wait_ge(in_f, l * 16 + 16)
                    for f in range(LFB):
                        if f >= 3:
                            pe.wait_ge(g_out[h], l * LFB + (f - 2))
                        pe.matmul(psum[:, 4 + f % 3], wf[:, f * P:(f + 1) * P], xnT[:, h], start=True, stop=True
                                  ).then_inc(h_in[h], 1)

                def mproj(h, l):
                    pe.wait_ge(g_out[h], l * LFB + LFB)
                    pe.wait_ge(in_m, 16)
                    for k in range(HB):
                        for f in range(LFB):
                            w = wm[:, l * LFB + f] if isinstance(l, int) else wm[:, bass.ds(l * LFB + f, 1), :].rearrange("p o d -> p (o d)")
                            m = pe.matmul(psum[:, 0, k * P:(k + 1) * P], gT[:, h, f, k * P:(k + 1) * P], w,
                                          start=(f == 0), stop=(f == LFB - 1))
                    m.then_inc(y_in[h], 1)

                def half_step(h, l, o, m):
                    if h is not None:
                        turn(h, l, 0)
                        if o is not None:
                            keep_warm(pe, S, 7, 1)
                        pe.wait_ge(in_q, l * 16 + 16)
                        if o is not None:
                            pe.wait_ge(q_out[o], m * NQ + NQ)
                        pe.wait_ge(N[h].xT, l * 2 + 1)
                        project(h, l, 0, 2)
                    if o is not None:
                        hartley(o, m)
                    if h is not None:
                        project(h, l, 2, 3)
                    if o is not None:
                        out(o, m)
                    if h is not None:
                        project(h, l, 3, NQ)
                        if o is not None:
                            keep_warm(pe, S, 0, WARM0)
                    if o is not None:
                        turn(o, m, 1)
                        keep_warm(pe, S, 7, 1)
                        fc(o, m)
                        mproj(o, m)
                        if h is not None:
                            keep_warm(pe, S, 7, WARM)

                pe.wait_ge(wc_out, 1)
                layers(pe, half_step)


YH, YD = 4, 32


def load_cross1(sp, S, A):
    for n in "kvqo":
        load(sp, S.y_w[:, "qkvo".index(n)], A["yw" + n], S.in_y)
    load(sp, S.y_cols[:, 0:1], A["ybq"], S.in_y)
    load(sp, S.y_cols[:, 1:2], A["ybk"], S.in_y)
    load(sp, S.y_rows[:, 0], A["ybv"].partition_broadcast(P), S.in_y)
    load(sp, S.y_rows[:, 1], A["ybo"].partition_broadcast(P), S.in_y)
    load(sp, S.y_mask[:], A["maskT"], S.in_y)


def stage_cross1(nc, S, A):
    psum, xres, xhat, xT = S.psum, S.xres, S.xhat, S.xT
    with ExitStack() as c:
        sem = S.sem

        def sb(name, shape, dt=F32):
            return c.enter_context(nc.sbuf_tensor(name, shape, dt))

        w, cols, rows, maski, in_y = S.y_w, S.y_cols, S.y_rows, S.y_mask, S.in_y
        keep, fill = sb("y_keep", [P, NB, P]), sb("y_fill", [P, NB, P])
        qT, kT, vall = sb("y_qT", [P, NB * P]), sb("y_kT", [P, NB * P]), sb("y_v", [P, NB, D])
        qTp, kTp = sb("y_qTp", [P, 2, P]), sb("y_kTp", [P, 2, P])
        wt, e = sb("y_wt", [P, 2, YH, P]), sb("y_e", [P, 2, YH, P])
        mx, nmx, ssum, rs = (sb(f"y_{n}", [P, 2, YH]) for n in ("max", "nmax", "sum", "rsum"))
        vn, oT = sb("y_vn", [P, 2, D]), sb("y_oT", [P, 2, P])
        N = Norm(sem, "y")
        kps, kTr, vps, vr, qps, qTr, xb, kpr, fl = (sem(n) for n in (
            "y_k_psum", "y_kT_made", "y_v_psum", "y_v_made", "y_q_psum", "y_qT_made", "y_x_bo", "y_keep_made",
            "y_fill_made"))
        kpc, qpc, s_in, s_out, flr, mxr, nmr, ex, rsr, vnr, a_in, a_out, y_in, y_out = (sem(n) for n in (
            "yl_kT", "yl_qT", "yl_s_psum", "yl_kept", "yl_filled", "yl_max", "yl_nmax", "yl_e", "yl_rsum", "yl_vn",
            "yl_a_psum", "yl_oT", "yl_y_psum", "yl_x"))
        SI0, SO0, YO0 = 2, 1, 2
        with nc.Block() as block:
            @block.gpsimd
            def _(pool):
                norm_pool(pool, S, N, EPS_OUTER)

                pool.sem_inc(s_in, SI0)
                with pool.Fori(0, NB // 2) as i:
                    for j in range(2):
                        n = i * 2 + j
                        pool.wait_ge(kTr, 2)
                        pool.wait_ge(s_in, n - 1 + SI0)
                        pool.tensor_copy(kTp[:, j], kT[:, bass.ds(n * P, P)]).then_inc(kpc, 1)
                        pool.wait_ge(qTr, 2)
                        pool.tensor_copy(qTp[:, j], qT[:, bass.ds(n * P, P)]).then_inc(qpc, 1)

            @block.vector
            def _(dve):
                norm_vector(dve, S, N, xres, xhat)
                dve.wait_ge(in_y, 16 * 9)
                for h in range(2):
                    dve.wait_ge(vps, h + 1)
                    dve.tensor_tensor(vall[:, HB * h:HB * h + HB], psum[:, 2 + h].rearrange("p (b d) -> p b d", b=HB),
                                      rows[:, 0, None, :].broadcast_to([P, HB, D]), ALU.add).then_inc(vr, 1)
                dve.tensor_scalar(keep[:], maski[:], 0.0, None, ALU.not_equal).then_inc(kpr, 1)
                dve.wait_ge(kpr, 1)
                dve.tensor_scalar(fill[:], keep[:], -1.0, 1e9, ALU.add, ALU.mult).then_inc(fl, 1)

                def weigh(n, j):
                    dve.wait_ge(s_in, n + 1 + SI0)
                    keep_, fill_ = (t[:, one(n), :].broadcast_to([P, YH, P]) for t in (keep, fill))
                    dve.scalar_tensor_tensor(out=wt[:, j], in0=psum[:, 0:YH, 0:P], scalar=float(np.float32(YD) ** np.float32(-0.5)),
                                             in1=keep_, op0=ALU.mult, op1=ALU.mult).then_inc(s_out, 1)
                    dve.wait_ge(s_out, n + 1 + SO0)
                    dve.tensor_tensor(wt[:, j], wt[:, j], fill_, ALU.add).then_inc(flr, 1)
                    dve.wait_ge(flr, n + 1)
                    dve.tensor_reduce(mx[:, j], wt[:, j], AX.X, ALU.max).then_inc(mxr, 1)
                    dve.wait_ge(mxr, n + 1)
                    dve.tensor_scalar(nmx[:, j], mx[:, j], -1.0, None, ALU.mult).then_inc(nmr, 1)

                def scale_values(n, j):
                    dve.wait_ge(ex, n + 1)
                    dve.reciprocal(rs[:, j], ssum[:, j]).then_inc(rsr, 1)
                    dve.wait_ge(rsr, n + 1)
                    dve.tensor_tensor(vn[:, j].rearrange("p (h d) -> p h d", h=YH),
                                      vall[:, one(n), :].rearrange("p o (h d) -> p (o h) d", h=YH),
                                      rs[:, j, :, None].broadcast_to([P, YH, YD]), ALU.mult).then_inc(vnr, 1)

                def residual(n, j):
                    x = xres[:, one(n), :].rearrange("p o d -> p (o d)")
                    dve.wait_ge(y_in, n + 1)
                    dve.tensor_tensor(x, psum[:, 5 + 2 * j, 0:D], x, ALU.add).then_inc(y_out, 1)

                def slot(n, j):
                    first, second, last = parts(n)
                    if first:
                        weigh(n + 1, 1 - j)
                    if second:
                        residual(n, j)
                    if first:
                        scale_values(n + 1, 1 - j)

                dve.wait_ge(fl, 1)
                dve.wait_ge(vr, 2)
                dve.wait_ge(N.hat, 2)
                dve.tensor_tensor(xres[:], xres[:], rows[:, 1, None, :].broadcast_to([P, NB, D]), ALU.add).then_inc(xb, 1)
                dve.wait_ge(xb, 1)
                weigh(0, 0)
                scale_values(0, 0)
                batches(dve, slot)

            @block.tensor
            def _(pe):
                pe.wait_ge(in_y, 16 * 9)
                for h in range(2):
                    pe.matmul(psum[:, h], w[:, 1], S.ctxT[:, h * HALF:(h + 1) * HALF], start=True, stop=True).then_inc(kps, 1)
                for h in range(2):
                    for i in range(HB):
                        b = HB * h + i
                        m = pe.matmul(psum[:, 2 + h, i * P:(i + 1) * P], S.ctxT[:, b * P:(b + 1) * P], w[:, 2], start=True, stop=True)
                    m.then_inc(vps, 1)
                norm_tensor(pe, S, N, 4)
                for h in range(2):
                    pe.wait_ge(N.xT, h + 1)
                    pe.matmul(psum[:, 6 + h], w[:, 0], xT[:, h * HALF:(h + 1) * HALF], start=True, stop=True).then_inc(qps, 1)

                pe.sem_inc(s_out, SO0)
                pe.sem_inc(y_out, YO0)
                pe.wait_ge(vr, 2)
                pe.wait_ge(kTr, 2)
                pe.wait_ge(qTr, 2)

                def scores(n, j):
                    pe.wait_ge(kpc, n + 1)
                    pe.wait_ge(qpc, n + 1)
                    pe.wait_ge(s_out, n + SO0)
                    for h in range(YH):
                        rows_ = slice(YD * h, YD * h + YD)
                        m = pe.matmul(psum[:, h, 0:P], kTp[rows_, j], qTp[rows_, j], start=True, stop=True)
                    m.then_inc(s_in, 1)

                def attend(n, j):
                    pe.wait_ge(vnr, n + 1)
                    for h in range(YH):
                        m = pe.matmul(psum[YD * h:YD * h + YD, 4 + 2 * j, 0:P], vn[:, j, YD * h:YD * h + YD], e[:, j, h],
                                      start=True, stop=True)
                    m.then_inc(a_in, 1)

                def output(n, j):
                    pe.wait_ge(a_out, n + 1)
                    pe.wait_ge(y_out, n - 1 + YO0)
                    pe.matmul(psum[:, 5 + 2 * j, 0:D], oT[:, j], w[:, 3], start=True, stop=True).then_inc(y_in, 1)

                def slot(n, j):
                    first, second, last = parts(n)
                    if first:
                        scores(n + 1, 1 - j)
                    if second:
                        attend(n, j)
                        output(n, j)

                scores(0, 0)
                batches(pe, slot)

            @block.scalar
            def _(act):
                act.wait_ge(in_y, 16 * 9)
                for h in range(2):
                    act.wait_ge(kps, h + 1)
                    act.activation(kT[:, h * HALF:(h + 1) * HALF], psum[:, h], ACT.Identity, bias=cols[:, 1:2]).then_inc(kTr, 1)
                norm_scalar(act, S, N, 4, xT)
                for h in range(2):
                    act.wait_ge(qps, h + 1)
                    act.activation(qT[:, h * HALF:(h + 1) * HALF], psum[:, 6 + h], ACT.Identity, bias=cols[:, 0:1]).then_inc(qTr, 1)

                def exp(n, j):
                    act.wait_ge(nmr, n + 1)
                    for h in range(YH):
                        m = act.activation(e[:, j, h], wt[:, j, h], ACT.Exp, bias=nmx[:, j, h:h + 1], accum_out=ssum[:, j, h:h + 1])
                    m.then_inc(ex, 1)

                def take(n, j):
                    act.wait_ge(a_in, n + 1)
                    act.activation(oT[:, j], psum[:, 4 + 2 * j, 0:P], ACT.Copy).then_inc(a_out, 1)

                def slot(n, j):
                    first, second, last = parts(n)
                    if second:
                        take(n, j)
                    if first:
                        exp(n + 1, 1 - j)

                exp(0, 0)
                batches(act, slot)


RE, CAP = 8, 100


def load_router(sp, S, A):
    load(sp, S.r_wg[:], A["rwg"], S.in_r)
    load(sp, S.r_we[:], A["rwe"], S.in_r)
    load(sp, S.r_be[:], A["rbe"].partition_broadcast(P), S.in_r)
    load(sp, S.r_tri[:], A["upto"], S.in_r)
    load(sp, S.r_rank[:], A["rank"].partition_broadcast(P), S.in_r)


def stage_router(nc, S, A):
    psum, xres, xhat, xT = S.psum, S.xres, S.xhat, S.xT
    with ExitStack() as c:
        sem = S.sem

        def sb(name, shape, dt=F32):
            return c.enter_context(nc.sbuf_tensor(name, shape, dt))

        wg, we, be, tri, rank, in_r = S.r_wg, S.r_we, S.r_be, S.r_tri, S.r_rank, S.in_r
        R = sb("r_r", [P, 6, NB, RE])
        r1 = sb("r_1", [P, 6, NB])
        y = sb("r_y", [P, NB, D])
        N = Norm(sem, "r")
        lg, v, ae, cm, e_in, yr, xr, done = (sem(n) for n in (
            "r_logits", "r_chain", "r_exp", "r_count_psum", "r_e_psum", "r_expert", "r_x", "r_stored"))
        with nc.Block() as block:
            @block.sync
            def _(sp):
                for h in range(2):
                    t = slice(HB * h, HB * h + HB)
                    sp.wait_ge(xr, h + 1)
                    sp.dma_start(A["out"][:, t], xres[:, t]).then_inc(done, 16)
                sp.wait_ge(done, 32)

            @block.gpsimd
            def _(pool):
                norm_pool(pool, S, N, EPS_OUTER)

            @block.vector
            def _(dve):
                norm_vector(dve, S, N, xres, xhat)
                count = [0]

                def step(m):
                    count[0] += 1
                    m.then_inc(v, 1)
                    dve.wait_ge(v, count[0])

                def bc(a):
                    return a[:, :, None].broadcast_to([P, NB, RE])

                dve.wait_ge(in_r, 80)
                dve.wait_ge(lg, 1)
                lgt = psum[:, 2, 0:NB * RE].rearrange("p (b e) -> p b e", b=NB)
                step(dve.tensor_reduce(r1[:, 0], lgt, AX.X, ALU.max))
                step(dve.tensor_tensor(R[:, 0], lgt, bc(r1[:, 0]), ALU.subtract))
                dve.wait_ge(ae, 1)
                step(dve.tensor_reduce(r1[:, 1], R[:, 0], AX.X, ALU.add))
                step(dve.reciprocal(r1[:, 2], r1[:, 1]))
                step(dve.tensor_tensor(R[:, 1], R[:, 0], bc(r1[:, 2]), ALU.mult))
                step(dve.tensor_reduce(r1[:, 3], R[:, 1], AX.X, ALU.max))
                step(dve.tensor_tensor(R[:, 2], R[:, 1], bc(r1[:, 3]), ALU.is_equal))
                step(dve.tensor_tensor(R[:, 2], R[:, 2], rank[:, None, :].broadcast_to([P, NB, RE]), ALU.mult))
                step(dve.tensor_reduce(r1[:, 4], R[:, 2], AX.X, ALU.max))
                step(dve.tensor_tensor(R[:, 3], R[:, 2], bc(r1[:, 4]), ALU.is_equal))
                for h in range(2):
                    t = slice(HB * h, HB * h + HB)
                    dve.wait_ge(e_in, h + 1)
                    dve.tensor_tensor(y[:, t], psum[:, 4 + h].rearrange("p (b d) -> p b d", b=HB),
                                      be[:, None, :].broadcast_to([P, HB, D]), ALU.add).then_inc(yr, 1)
                dve.wait_ge(cm, 1)
                cnt = psum[:, 3, 0:NB * RE].rearrange("p (b e) -> p b e", b=NB)
                step(dve.tensor_scalar(R[:, 4], cnt, CAP + 0.5, None, ALU.is_lt))
                step(dve.tensor_tensor(R[:, 5], R[:, 4], R[:, 3], ALU.mult))
                step(dve.tensor_reduce(r1[:, 5], R[:, 5], AX.X, ALU.add))
                step(dve.tensor_tensor(r1[:, 4], r1[:, 5], r1[:, 3], ALU.mult))
                for h in range(2):
                    dve.wait_ge(yr, h + 1)
                    for i in range(HB):
                        b = HB * h + i
                        m = dve.scalar_tensor_tensor(out=xres[:, b], in0=y[:, b], scalar=r1[:, 4, b:b + 1], in1=xres[:, b],
                                                     op0=ALU.mult, op1=ALU.add)
                    m.then_inc(xr, 1)

            @block.scalar
            def _(act):
                norm_scalar(act, S, N, 0, xT)
                act.wait_ge(v, 2)
                act.activation(R[:, 0], R[:, 0], ACT.Exp).then_inc(ae, 1)

            @block.tensor
            def _(pe):
                keep_warm(pe, S, 7, ROUTER_FILLERS)
                norm_tensor(pe, S, N, 0)
                pe.wait_ge(in_r, 80)
                pe.wait_ge(N.xT, 2)
                for b in range(NB):
                    m = pe.matmul(psum[:, 2, b * RE:(b + 1) * RE], xT[:, b * P:(b + 1) * P], wg[:], start=True, stop=True)
                m.then_inc(lg, 1)
                for h in range(2):
                    for i in range(HB):
                        b = HB * h + i
                        m = pe.matmul(psum[:, 4 + h, i * P:(i + 1) * P], xT[:, b * P:(b + 1) * P], we[:], start=True, stop=True)
                    m.then_inc(e_in, 1)
                pe.wait_ge(v, 10)
                hot = R[:, 3].rearrange("p b e -> p (b e)")
                pe.matmul(psum[:, 3, 0:NB * RE], tri[:], hot, start=True, stop=False, skip_group_check=True)
                for k in range(1, NB):
                    m = pe.matmul(psum[:, 3, k * RE:NB * RE], S.ones[:], hot[:, 0:(NB - k) * RE], start=False,
                                  stop=(k == NB - 1), skip_group_check=True)
                m.then_inc(cm, 1)


def spectral_tables():
    h, d = np.divmod(np.arange(P), QD)
    turns = np.outer(h, h) / QH + np.outer(d, d) / QD
    hartley = np.cos(2 * np.pi * turns) + np.sin(2 * np.pi * turns)
    fs, fh, fd = np.fft.fftfreq(P), np.fft.fftfreq(QH)[h], np.fft.fftfreq(QD)[d]
    km = np.sqrt(fs[None, :] ** 2 + fh[:, None] ** 2 + fd[:, None] ** 2 + 1e-10)
    real = np.cos(np.arctan(np.log(km + 1e-10)))
    s = np.arange(P)
    lam, t = s / P, s * 0.1
    modulation = np.sin(t + lam) * np.cos(t - 2.0 * lam + 0.5 * lam ** 2)
    return hartley.astype(np.float32), (real * (1.0 + 0.1 * modulation) / P).astype(np.float32)


def program(nc, A):
    S = Shared()
    with ExitStack() as ctx:
        def sem(name):
            return ctx.enter_context(nc.semaphore(name))

        def sb(name, shape, dt=F32):
            return ctx.enter_context(nc.sbuf_tensor(name, shape, dt))

        S.sem = lambda name: nc.alloc_semaphore(name=name)
        S.psum = ctx.enter_context(nc.psum_tensor("psum", [P, 8, 512], F32))
        S.xres = sb("xres", [P, NB, D])
        S.xhat = sb("xhat", [P, NB, D])
        S.xT = sb("xT", [P, NB * P])
        S.ident = sb("ident", [P, P])
        S.ones = sb("ones", [P, P])
        S.nhalf = sb("nhalf", [P, NB])
        S.eps = sb("eps", [P, NB])
        S.stats = sb("stats", [P, 2, HB, 6])
        S.mv = sb("mv", [P, 2, HB, 2])
        S.rstd = sb("rstd", [P, 2, HB])
        S.ctxT = sb("ctxT", [P, NB * P])
        S.x0w, S.x0cols, S.x0rows = sb("x0w", [P, 4, D]), sb("x0cols", [P, 2]), sb("x0rows", [P, 2, D])
        S.x0kT = sb("x0kT", [P, NB * P])
        S.headmask = sb("headmask", [P, XH])
        S.in_x0, S.in_router, S.in_wd, S.in_l, S.in_wqkv, S.in_wp, S.in_wf, S.in_wm, S.in_y, S.in_r = (sem(f"in_{n}") for n in (
            "x0", "router", "wd", "layers", "wqkv", "wp", "wf", "wm", "y", "r"))
        S.k_psum, S.kT_made = sem("k_psum"), sem("kT_made")
        S.in_expert = [sem(f"in_expert{j}") for j in range(2)]
        with nc.cleanup_on_exit():
            stage_performer(nc, S, A)
        S.m_router, S.m_wd = sb("m_router", [P, ME]), sb("m_wd", [P, ME * MFB, D])
        S.m_rank = sb("m_rank", [P, ME])
        S.m_wg, S.m_wu = sb("m_wg", [P, 2, MF]), sb("m_wu", [P, 2, MF])
        S.wqkv, S.wf = sb("l_wqkv", [P, NQ, P]), sb("l_wf", [P, LF])
        S.wp, S.wm = sb("l_wp", [P, LL, D]), sb("l_wm", [P, LL * LFB, D])
        S.l_cols, S.l_rows = sb("l_cols", [P, LL, LCOLS]), sb("l_rows", [P, LL, 2, D])
        S.hart, S.filt = sb("l_hart", [P, P]), sb("l_filt", [P, P])
        S.y_w, S.y_cols, S.y_rows = sb("y_w", [P, 4, D]), sb("y_cols", [P, 2]), sb("y_rows", [P, 2, D])
        S.y_mask = sb("y_mask", [P, NB, P], I32)
        S.r_wg, S.r_we, S.r_be = sb("r_wg", [P, RE]), sb("r_we", [P, D]), sb("r_be", [P, D])
        S.r_tri, S.r_rank = sb("r_tri", [P, P]), sb("r_rank", [P, RE])
        for stage in (stage_cross0, stage_moe, stage_layers, stage_cross1, stage_router):
            with nc.cleanup_on_exit():
                stage(nc, S, A)


def lay_out(i):
    c = np.ascontiguousarray
    wq, wk = i["L0_attn_Wq"], i["L0_attn_Wk"]
    r = {
        "x": c(i["x"].transpose(1, 0, 2)),
        "ident": np.eye(P, dtype=np.float32),
        "pwq": c(wq.reshape(D, -1)), "pwk": c(wk.reshape(D, -1)), "pwv": c(i["L0_attn_Wv"].reshape(D, -1)),
        "pwqT": c(wq.reshape(D, NPAIR, P).transpose(2, 1, 0)), "pwkT": c(wk.reshape(D, NPAIR, P).transpose(2, 1, 0)),
        "projT": c(i["L0_attn_proj"].T),
        "pwo": c(i["L0_attn_Wo"].reshape(NPAIR, P, D).transpose(1, 0, 2)),
        "pw1": i["L0_attn_W1"], "pw2": c(i["L0_attn_W2"].reshape(PFB, P, D).transpose(1, 0, 2)),
        "pb1": c(i["L0_attn_b1"].reshape(PFB, P).T), "pb2": i["L0_attn_b2"],
        "pln1g": i["L0_attn_ln1_g"], "pln1b": i["L0_attn_ln1_b"],
        "pln2g": i["L0_attn_ln2_g"], "pln2b": i["L0_attn_ln2_b"],
        "ctxT": c(i["ctx_1024"].transpose(2, 0, 1).reshape(D, -1)),
        "headmask": c(np.repeat(np.eye(XH, dtype=np.float32), XD, 0)),
        "router": i["L0_ffn_router_kernel_DE"],
        "rank": np.arange(ME, 0, -1, dtype=np.float32),
        "mwg": c(i["L0_ffn_kernel_gating_EDF"].transpose(1, 0, 2)), "mwu": c(i["L0_ffn_kernel_up_EDF"].transpose(1, 0, 2)),
        "mwd": c(i["L0_ffn_kernel_down_EFD"].reshape(ME * MFB, P, D).transpose(1, 0, 2)),
    }
    aw = i["L1_attn_attn_w"].reshape(LL, D, QH, 3, QD).transpose(1, 0, 3, 2, 4)
    ab = i["L1_attn_attn_b"].reshape(LL, QH, 3, QD).transpose(0, 2, 1, 3)
    aw, ab = aw[:, :, list(KQV)], ab[:, list(KQV)]
    r["lwqkv"] = c(np.stack([aw, np.roll(aw, 1, axis=3)], 3).reshape(D, LL, -1))
    ab6 = np.stack([ab, np.roll(ab, 1, axis=2)], 2).reshape(LL, NQ, D)
    r["lwp"] = c(i["L1_attn_aproj_w"].transpose(1, 0, 2))
    r["lwf"] = c(i["L1_attn_fc_w"].transpose(1, 0, 2))
    r["lwm"] = c(i["L1_attn_mproj_w"].reshape(LL, LFB, P, D).transpose(2, 0, 1, 3).reshape(P, LL, -1))
    ln = np.stack([i["L1_attn_" + n] for n in ("ln1_w", "ln1_b", "ln2_w", "ln2_b")], 1)
    r["lcols"] = c(np.concatenate([ln, ab6, i["L1_attn_fc_b"].reshape(LL, LFB, P)], 1).transpose(2, 0, 1))
    r["lrows"] = c(np.stack([i["L1_attn_aproj_b"], i["L1_attn_mproj_b"]], 1).reshape(-1))
    r["hartley"], r["filter"] = spectral_tables()
    r["maskT"] = c(i["mask_Bx1xSxS2_ik1"][:, 0].transpose(2, 0, 1))
    for n in "qkvo":
        r["yw" + n] = c(i["L1_xattn_W" + n].T)
        b = i["L1_xattn_b" + n]
        r["yb" + n] = b.reshape(D, 1) if n in "qk" else b
    r["rwg"], r["rwe"], r["rbe"] = i["L1_ffn_w_gate"], i["L1_ffn_w_expert"], i["L1_ffn_b_expert"]
    r["upto"] = np.triu(np.ones((P, P), np.float32))
    for n in "qkvo":
        r["x0w" + n] = c(i["L0_xattn_W" + n].T)
    for n in "qk":
        r["x0b" + n] = i["L0_xattn_b" + n].reshape(D, 1)
    for n in "vo":
        r["x0b" + n] = i["L0_xattn_b" + n]
    return r


def kernel(**inputs):
    import concourse.bacc as bacc
    from concourse.bass_utils import run_bass_kernel_spmd

    nc = bacc.Bacc("TRN2", target_bir_lowering=False, num_devices=1)
    arrays, A = {}, {}
    for name, a in lay_out({k: np.asarray(v) for k, v in inputs.items()}).items():
        a = np.ascontiguousarray(a)
        arrays[f"in_{name}_dram"] = a
        A[name] = nc.dram_tensor(f"in_{name}_dram", a.shape, mybir.dt.from_np(a.dtype), kind="ExternalInput").ap()
    A["out"] = nc.dram_tensor("out_0_dram", (P, NB, D), F32, kind="ExternalOutput").ap()
    program(nc, A)
    r = run_bass_kernel_spmd(nc, [arrays], core_ids=[0])
    return np.ascontiguousarray(r.results[0]["out_0_dram"].transpose(1, 0, 2))
```
